# Optimizing a Trainium2 kernel written in Bass

```python
import numpy as np
import jax
import jax.numpy as jnp

def _softmax(x, axis=-1):
    return jax.nn.softmax(x, axis=axis)

def _gelu(x):
    return jax.nn.gelu(x, approximate=True)

def _silu(x):
    return jax.nn.silu(x)

def _sigmoid(x):
    return jax.nn.sigmoid(x)

def _layernorm(x, axis=-1, eps=1e-05):
    m = jnp.mean(x, axis=axis, keepdims=True)
    v = jnp.var(x, axis=axis, keepdims=True)
    return (x - m) / jnp.sqrt(v + eps)

def _scatter_add(tgt, idx, src, axis=0):
    return tgt.at[idx].add(src)

def _segment_sum(src, seg, n):
    return jax.ops.segment_sum(src, seg, n)
kernel_name = 'mk_gnn_preln_d4_gnn_r8_60ff62'

def setup_inputs(seed: int=0):
    np.random.seed(seed)
    _w = jnp.asarray

    def _rec_inputs():
        import jax
        import jax.numpy as jnp
        _gk = jax.random.key(seed)
        x = -0.0005121 + 1.001 * jax.random.normal(jax.random.fold_in(_gk, 1), (6250, 160), jnp.float32)
        src = jax.random.randint(jax.random.fold_in(_gk, 2), (100000,), 0, 6250, jnp.int32)
        dst = jnp.minimum((6250 * jax.random.uniform(jax.random.fold_in(_gk, 3), (100000,)) ** 2.0).astype(jnp.int32), 49999)
        _o = jnp.argsort(dst, stable=True)
        src = src[_o]
        dst = dst[_o]
        edge_attr_10 = jax.random.uniform(jax.random.fold_in(_gk, 12), (100000, 10), jnp.float32, 0.0, 1)
        edge_attr_16 = -0.000191324 + 0.999809 * jax.random.normal(jax.random.fold_in(_gk, 13), (100000, 16), jnp.float32)
        edge_attr_3 = 0.00047201 + 1.00023 * jax.random.normal(jax.random.fold_in(_gk, 14), (100000, 3), jnp.float32)
        edge_attr_4 = 0.000126197 + 0.999763 * jax.random.normal(jax.random.fold_in(_gk, 15), (100000, 4), jnp.float32)
        edge_attr_64 = 0.000279952 + 1.00013 * jax.random.normal(jax.random.fold_in(_gk, 16), (100000, 64), jnp.float32)
        edge_attr_8 = 0.000735704 + 1.0001 * jax.random.normal(jax.random.fold_in(_gk, 17), (100000, 8), jnp.float32)
        node_vec1 = jax.random.uniform(jax.random.fold_in(_gk, 19), (6250, 1), jnp.float32, 0.0, 1)
        node_vec1_n2 = jax.random.uniform(jax.random.fold_in(_gk, 20), (6250, 1), jnp.float32, 0.0, 1)
        node_vec1_n3 = jax.random.uniform(jax.random.fold_in(_gk, 21), (6250, 1), jnp.float32, 0.0, 1)
        return (x, src, dst, edge_attr_10, edge_attr_16, edge_attr_3, edge_attr_4, edge_attr_64, edge_attr_8, node_vec1, node_vec1_n2, node_vec1_n3)
    x, src, dst, edge_attr_10, edge_attr_16, edge_attr_3, edge_attr_4, edge_attr_64, edge_attr_8, node_vec1, node_vec1_n2, node_vec1_n3 = _rec_inputs()

    def _L0_gnn_setup():
        import jax, jax.numpy as jnp
        import numpy as np
        N = 2500
        E = 40000
        MUL0 = 64
        MUL1 = 32
        FC_IN = 16
        FC_H = 64
        WNUM = 192
        key = jax.random.key(seed)
        ks = jax.random.split(key, 16)
        return {'x': jax.random.normal(ks[0], (N, MUL0 + 3 * MUL1), jnp.float32), 'node_attr': jnp.ones((N, 1), jnp.float32), 'edge_scalars': jax.random.normal(ks[1], (E, FC_IN), jnp.float32), 'edge_attr_sh': jax.random.normal(ks[2], (E, 4), jnp.float32), 'edge_src': jax.random.randint(ks[3], (E,), 0, N), 'edge_dst': jax.random.randint(ks[4], (E,), 0, N), 'Wfc1': jax.random.normal(ks[5], (FC_IN, FC_H), jnp.float32), 'Wfc2': jax.random.normal(ks[6], (FC_H, WNUM), jnp.float32), 'Wsc0': jax.random.normal(ks[7], (MUL0, MUL0), jnp.float32), 'Wsc1': jax.random.normal(ks[8], (MUL1, MUL1), jnp.float32), 'Wl1_0': jax.random.normal(ks[9], (MUL0, MUL0), jnp.float32), 'Wl1_1': jax.random.normal(ks[10], (MUL1, MUL1), jnp.float32), 'Wl2_s': jax.random.normal(ks[11], (MUL0 + MUL1, MUL0), jnp.float32), 'Wl2_v': jax.random.normal(ks[12], (MUL0 + MUL1, MUL1), jnp.float32), 'Wa': 0.1 * jax.random.normal(ks[13], (MUL0 + MUL1, 1), jnp.float32)}
    _L0_gnn_all = _L0_gnn_setup()
    _L0_gnn_in = {k: v for k, v in _L0_gnn_all.items() if k in ('Wfc1', 'Wfc2', 'Wsc0', 'Wsc1', 'Wl1_0', 'Wl1_1', 'Wl2_s', 'Wl2_v', 'Wa')}
    del _L0_gnn_all

    def _L1_gnn_setup():
        import jax, jax.numpy as jnp
        import numpy as np
        N = 3125
        E = 50000
        S = 64
        V = 32
        NB = 10
        H = 100
        WN = 192
        MID = 96
        NUM_NEIGHBORS = 16.0
        C_S = float(np.sin(np.pi / 8.0))
        C_X = float(np.cos(np.pi / 8.0))
        SQRT3 = float(np.sqrt(3.0))

        def fctp_scalar_attr(xs, xv, attr, Ws, Wv):
            s = xs * attr @ Ws
            v = jnp.einsum('nuc,uo->noc', xv * attr[:, :, None], Wv)
            return (s, v)
        key = jax.random.key(seed)
        k = jax.random.split(key, 24)

        def w(i, shape):
            return jax.random.normal(k[i], shape, jnp.float32) / np.sqrt(float(shape[0]))
        return {'node_input': jax.random.normal(k[0], (N, S + 3 * V), jnp.float32), 'node_attr': jax.random.normal(k[1], (N, 1), jnp.float32), 'node_crystal_attr': jax.random.normal(k[2], (N, 1), jnp.float32), 'sym_mask': jax.random.normal(k[3], (N, 1), jnp.float32), 'edge_attr': jax.random.normal(k[4], (E, 4), jnp.float32), 'edge_length_embedded': jax.random.uniform(k[5], (E, NB), dtype=jnp.float32), 'edge_src': jax.random.randint(k[6], (E,), 0, N), 'edge_dst': jax.random.randint(k[7], (E,), 0, N), 'Ws_sc_a': w(8, (S, S)), 'Wv_sc_a': w(9, (V, V)), 'Ws_sc_c': w(10, (S, S)), 'Wv_sc_c': w(11, (V, V)), 'Ws_l1_a': w(12, (S, S)), 'Wv_l1_a': w(13, (V, V)), 'Ws_l1_c': w(14, (S, S)), 'Wv_l1_c': w(15, (V, V)), 'W_fc1': w(16, (NB, H)), 'W_fc2': w(17, (H, WN)), 'Ws_l2_a': w(18, (MID, MID)), 'Wv_l2_a': w(19, (MID, MID)), 'Ws_l2_c': w(20, (MID, MID)), 'Wv_l2_c': w(21, (MID, MID)), 'Ws_l3': w(22, (MID, S)), 'Wv_l3': w(23, (MID, V))}
    _L1_gnn_all = _L1_gnn_setup()
    _L1_gnn_in = {k: v for k, v in _L1_gnn_all.items() if k in ('Ws_sc_a', 'Wv_sc_a', 'Ws_sc_c', 'Wv_sc_c', 'Ws_l1_a', 'Wv_l1_a', 'Ws_l1_c', 'Wv_l1_c', 'W_fc1', 'W_fc2', 'Ws_l2_a', 'Wv_l2_a', 'Ws_l2_c', 'Wv_l2_c', 'Ws_l3', 'Wv_l3')}
    del _L1_gnn_all

    def _L2_gnn_setup():
        import jax, jax.numpy as jnp
        import numpy as np
        N_NODES = 1250
        N_EDGES = 40000
        MUL0, MUL1 = (64, 32)
        EDGE_DIM = 64
        W_NUMEL = 224
        DENOM = 32.0
        SQRT3 = 3.0 ** 0.5
        INV_SQRT3 = 1.0 / SQRT3
        INV_SQRT2 = 2.0 ** (-0.5)

        def _forward(node_feature, edge_attr, edge_feature, W_skip0, W_skip1, W_nl0, W_nl1, W_fc1, W_fc2, W_out_s, W_out_v, edge_index):
            N = node_feature.shape[0]
            E = edge_attr.shape[0]
            s = node_feature[:, :MUL0]
            v = node_feature[:, MUL0:].reshape(N, MUL1, 3)
            skip_s = s @ W_skip0
            skip_v = jnp.einsum('nmi,mk->nki', v, W_skip1)
            s = s @ W_nl0
            v = jnp.einsum('nmi,mk->nki', v, W_nl1)
            rhat = edge_attr / jnp.linalg.norm(edge_attr, axis=-1, keepdims=True)
            sh1 = SQRT3 * rhat
            w = jax.nn.relu(edge_feature @ W_fc1) @ W_fc2
            w0, w1, w2, w3, w4 = jnp.split(w, [64, 128, 160, 192], axis=-1)
            src, dst = (edge_index[0], edge_index[1])
            xs = s[dst]
            xv = v[dst]
            out0a = w0 * xs
            out0b = w3 * (jnp.einsum('emi,ei->em', xv, sh1) * INV_SQRT3)
            out1a = (w1 * xs)[:, :, None] * sh1[:, None, :]
            out1b = w2[:, :, None] * xv
            out1c = w4[:, :, None] * (jnp.cross(xv, sh1[:, None, :]) * INV_SQRT2)
            tp = jnp.concatenate([out0a, out0b, out1a.reshape(E, -1), out1b.reshape(E, -1), out1c.reshape(E, -1)], axis=-1)
            agg = jax.ops.segment_sum(tp, src, num_segments=N) / DENOM
            agg_s = agg[:, :96]
            agg_v = agg[:, 96:].reshape(N, 128, 3)
            out_s = agg_s @ W_out_s + skip_s
            out_v = jnp.einsum('nmi,mk->nki', agg_v, W_out_v) + skip_v
            fs = jax.nn.silu(out_s[:, :MUL0])
            gate = jax.nn.sigmoid(out_s[:, MUL0:MUL0 + 32])
            gv = gate[:, :, None] * out_v
            return jnp.concatenate([fs, gv.reshape(N, -1)], axis=-1)
        key = jax.random.key(seed)
        ks = jax.random.split(key, 12)

        def lin(k, fi, fo):
            return jax.random.normal(k, (fi, fo), jnp.float32) / np.float32(np.sqrt(fi))
        return {'node_feature': jax.random.normal(ks[0], (N_NODES, MUL0 + 3 * MUL1), jnp.float32), 'edge_attr': jax.random.normal(ks[1], (N_EDGES, 3), jnp.float32), 'edge_feature': jax.random.normal(ks[2], (N_EDGES, EDGE_DIM), jnp.float32), 'W_skip0': lin(ks[3], MUL0, 96), 'W_skip1': lin(ks[4], MUL1, 32), 'W_nl0': lin(ks[5], MUL0, MUL0), 'W_nl1': lin(ks[6], MUL1, MUL1), 'W_fc1': lin(ks[7], EDGE_DIM, 64), 'W_fc2': lin(ks[8], 64, W_NUMEL), 'W_out_s': lin(ks[9], 96, 96), 'W_out_v': lin(ks[10], 128, 32), 'edge_index': jax.random.randint(ks[11], (2, N_EDGES), 0, N_NODES)}
    _L2_gnn_all = _L2_gnn_setup()
    _L2_gnn_in = {k: v for k, v in _L2_gnn_all.items() if k in ('W_skip0', 'W_skip1', 'W_nl0', 'W_nl1', 'W_fc1', 'W_fc2', 'W_out_s', 'W_out_v')}
    del _L2_gnn_all

    def _L3_gnn_setup():
        import jax, jax.numpy as jnp
        import numpy as np
        N_NODES = 1250
        N_EDGES = 40000
        NUM_NEIGHBORS = 32.0
        INV_SQRT3 = 1.0 / np.sqrt(3.0)

        def _fctp_scalar_attr(xs, xv, Ws, Wv, a):
            out_s = xs @ Ws * (a / np.sqrt(xs.shape[1]))[:, None]
            out_v = jnp.einsum('nuc,uw->nwc', xv, Wv) * (a / np.sqrt(xv.shape[1]))[:, None, None]
            return (out_s, out_v)
        key = jax.random.key(seed)
        ks = jax.random.split(key, 16)
        f32 = jnp.float32
        return {'node_input': jax.random.normal(ks[0], (N_NODES, 160), f32), 'node_attr': jnp.ones((N_NODES, 1), f32), 'edge_attr': jax.random.normal(ks[1], (N_EDGES, 4), f32), 'edge_scalar_attr': jax.random.normal(ks[2], (N_EDGES, 8), f32), 'Wsc0': jax.random.normal(ks[3], (64, 64), f32), 'Wsc1': jax.random.normal(ks[4], (32, 32), f32), 'Wl1_0': jax.random.normal(ks[5], (64, 64), f32), 'Wl1_1': jax.random.normal(ks[6], (32, 32), f32), 'Wfc1': jax.random.normal(ks[7], (8, 64), f32), 'Wfc2': jax.random.normal(ks[8], (64, 64), f32), 'Wfc3': jax.random.normal(ks[9], (64, 192), f32), 'Wl2_s': jax.random.normal(ks[10], (96, 64), f32), 'Wl2_v': jax.random.normal(ks[11], (96, 32), f32), 'Wa': jax.random.normal(ks[12], (96, 1), f32), 'edge_src': jax.random.randint(ks[13], (N_EDGES,), 0, N_NODES), 'edge_dst': jax.random.randint(ks[14], (N_EDGES,), 0, N_NODES)}
    _L3_gnn_all = _L3_gnn_setup()
    _L3_gnn_in = {k: v for k, v in _L3_gnn_all.items() if k in ('Wsc0', 'Wsc1', 'Wl1_0', 'Wl1_1', 'Wfc1', 'Wfc2', 'Wfc3', 'Wl2_s', 'Wl2_v', 'Wa')}
    del _L3_gnn_all
    return {'x': x, 'src': src, 'dst': dst, 'edge_attr_10': edge_attr_10, 'edge_attr_16': edge_attr_16, 'edge_attr_3': edge_attr_3, 'edge_attr_4': edge_attr_4, 'edge_attr_64': edge_attr_64, 'edge_attr_8': edge_attr_8, 'node_vec1': node_vec1, 'node_vec1_n2': node_vec1_n2, 'node_vec1_n3': node_vec1_n3, 'L0_gnn_Wfc1': _L0_gnn_in['Wfc1'], 'L0_gnn_Wfc2': _L0_gnn_in['Wfc2'], 'L0_gnn_Wsc0': _L0_gnn_in['Wsc0'], 'L0_gnn_Wsc1': _L0_gnn_in['Wsc1'], 'L0_gnn_Wl1_0': _L0_gnn_in['Wl1_0'], 'L0_gnn_Wl1_1': _L0_gnn_in['Wl1_1'], 'L0_gnn_Wl2_s': _L0_gnn_in['Wl2_s'], 'L0_gnn_Wl2_v': _L0_gnn_in['Wl2_v'], 'L0_gnn_Wa': _L0_gnn_in['Wa'], 'L1_gnn_Ws_sc_a': _L1_gnn_in['Ws_sc_a'], 'L1_gnn_Wv_sc_a': _L1_gnn_in['Wv_sc_a'], 'L1_gnn_Ws_sc_c': _L1_gnn_in['Ws_sc_c'], 'L1_gnn_Wv_sc_c': _L1_gnn_in['Wv_sc_c'], 'L1_gnn_Ws_l1_a': _L1_gnn_in['Ws_l1_a'], 'L1_gnn_Wv_l1_a': _L1_gnn_in['Wv_l1_a'], 'L1_gnn_Ws_l1_c': _L1_gnn_in['Ws_l1_c'], 'L1_gnn_Wv_l1_c': _L1_gnn_in['Wv_l1_c'], 'L1_gnn_W_fc1': _L1_gnn_in['W_fc1'], 'L1_gnn_W_fc2': _L1_gnn_in['W_fc2'], 'L1_gnn_Ws_l2_a': _L1_gnn_in['Ws_l2_a'], 'L1_gnn_Wv_l2_a': _L1_gnn_in['Wv_l2_a'], 'L1_gnn_Ws_l2_c': _L1_gnn_in['Ws_l2_c'], 'L1_gnn_Wv_l2_c': _L1_gnn_in['Wv_l2_c'], 'L1_gnn_Ws_l3': _L1_gnn_in['Ws_l3'], 'L1_gnn_Wv_l3': _L1_gnn_in['Wv_l3'], 'L2_gnn_W_skip0': _L2_gnn_in['W_skip0'], 'L2_gnn_W_skip1': _L2_gnn_in['W_skip1'], 'L2_gnn_W_nl0': _L2_gnn_in['W_nl0'], 'L2_gnn_W_nl1': _L2_gnn_in['W_nl1'], 'L2_gnn_W_fc1': _L2_gnn_in['W_fc1'], 'L2_gnn_W_fc2': _L2_gnn_in['W_fc2'], 'L2_gnn_W_out_s': _L2_gnn_in['W_out_s'], 'L2_gnn_W_out_v': _L2_gnn_in['W_out_v'], 'L3_gnn_Wsc0': _L3_gnn_in['Wsc0'], 'L3_gnn_Wsc1': _L3_gnn_in['Wsc1'], 'L3_gnn_Wl1_0': _L3_gnn_in['Wl1_0'], 'L3_gnn_Wl1_1': _L3_gnn_in['Wl1_1'], 'L3_gnn_Wfc1': _L3_gnn_in['Wfc1'], 'L3_gnn_Wfc2': _L3_gnn_in['Wfc2'], 'L3_gnn_Wfc3': _L3_gnn_in['Wfc3'], 'L3_gnn_Wl2_s': _L3_gnn_in['Wl2_s'], 'L3_gnn_Wl2_v': _L3_gnn_in['Wl2_v'], 'L3_gnn_Wa': _L3_gnn_in['Wa']}

def reference(x, src, dst, edge_attr_10, edge_attr_16, edge_attr_3, edge_attr_4, edge_attr_64, edge_attr_8, node_vec1, node_vec1_n2, node_vec1_n3, L0_gnn_Wfc1, L0_gnn_Wfc2, L0_gnn_Wsc0, L0_gnn_Wsc1, L0_gnn_Wl1_0, L0_gnn_Wl1_1, L0_gnn_Wl2_s, L0_gnn_Wl2_v, L0_gnn_Wa, L1_gnn_Ws_sc_a, L1_gnn_Wv_sc_a, L1_gnn_Ws_sc_c, L1_gnn_Wv_sc_c, L1_gnn_Ws_l1_a, L1_gnn_Wv_l1_a, L1_gnn_Ws_l1_c, L1_gnn_Wv_l1_c, L1_gnn_W_fc1, L1_gnn_W_fc2, L1_gnn_Ws_l2_a, L1_gnn_Wv_l2_a, L1_gnn_Ws_l2_c, L1_gnn_Wv_l2_c, L1_gnn_Ws_l3, L1_gnn_Wv_l3, L2_gnn_W_skip0, L2_gnn_W_skip1, L2_gnn_W_nl0, L2_gnn_W_nl1, L2_gnn_W_fc1, L2_gnn_W_fc2, L2_gnn_W_out_s, L2_gnn_W_out_v, L3_gnn_Wsc0, L3_gnn_Wsc1, L3_gnn_Wl1_0, L3_gnn_Wl1_1, L3_gnn_Wfc1, L3_gnn_Wfc2, L3_gnn_Wfc3, L3_gnn_Wl2_s, L3_gnn_Wl2_v, L3_gnn_Wa):
    import jax
    import jax.numpy as jnp

    def _L0_gnn_ref(x, node_attr, edge_scalars, edge_attr_sh, edge_src, edge_dst, Wfc1, Wfc2, Wsc0, Wsc1, Wl1_0, Wl1_1, Wl2_s, Wl2_v, Wa):
        import jax, jax.numpy as jnp
        import numpy as np
        N = 2500
        E = 40000
        MUL0 = 64
        MUL1 = 32
        FC_IN = 16
        FC_H = 64
        WNUM = 192
        n = x.shape[0]
        x0 = x[:, :MUL0]
        x1 = x[:, MUL0:].reshape(n, MUL1, 3)
        a = node_attr
        h = jax.nn.silu(edge_scalars @ (Wfc1 / jnp.sqrt(jnp.float32(FC_IN))))
        w = h @ (Wfc2 / jnp.sqrt(jnp.float32(FC_H)))
        w0 = w[:, :64]
        w1 = w[:, 64:128]
        w2 = w[:, 128:160]
        w3 = w[:, 160:192]
        inv8 = 1.0 / jnp.sqrt(jnp.float32(MUL0))
        inv32 = 1.0 / jnp.sqrt(jnp.float32(MUL1))
        sc = jnp.concatenate([x0 @ Wsc0 * a * inv8, (jnp.einsum('num,uv->nvm', x1, Wsc1) * a[..., None] * inv32).reshape(n, 3 * MUL1)], axis=1)
        f0 = x0 @ Wl1_0 * a * inv8
        f1 = jnp.einsum('num,uv->nvm', x1, Wl1_1) * a[..., None] * inv32
        e0 = f0[edge_src]
        e1 = f1[edge_src]
        sh0 = edge_attr_sh[:, :1]
        sh1 = edge_attr_sh[:, 1:4]
        mid0 = w0 * e0 * sh0
        mid1 = w3 * jnp.einsum('eum,em->eu', e1, sh1) / jnp.sqrt(3.0)
        mid2 = w1[:, :, None] * e0[:, :, None] * sh1[:, None, :]
        mid3 = w2[:, :, None] * e1 * sh0[:, :, None]
        cnt = jnp.clip(jax.ops.segment_sum(jnp.ones(edge_dst.shape, x.dtype), edge_dst, num_segments=n), 1.0)

        def smean(v):
            s = jax.ops.segment_sum(v, edge_dst, num_segments=n)
            return s / cnt.reshape((n,) + (1,) * (v.ndim - 1))
        n0, n1 = (smean(mid0), smean(mid1))
        n2, n3 = (smean(mid2), smean(mid3))
        scal = jnp.concatenate([n0, n1], axis=1)
        vec = jnp.concatenate([n2, n3], axis=1)
        inv96 = 1.0 / jnp.sqrt(jnp.float32(MUL0 + MUL1))
        alpha = scal @ Wa * a * inv96
        out_s = scal @ Wl2_s * a * inv96
        out_v = jnp.einsum('num,uv->nvm', vec, Wl2_v) * a[..., None] * inv96
        conv = jnp.concatenate([out_s, out_v.reshape(n, 3 * MUL1)], axis=1)
        return sc + alpha * conv

    def _L1_gnn_ref(node_input, node_attr, node_crystal_attr, sym_mask, edge_attr, edge_length_embedded, edge_src, edge_dst, Ws_sc_a, Wv_sc_a, Ws_sc_c, Wv_sc_c, Ws_l1_a, Wv_l1_a, Ws_l1_c, Wv_l1_c, W_fc1, W_fc2, Ws_l2_a, Wv_l2_a, Ws_l2_c, Wv_l2_c, Ws_l3, Wv_l3):
        import jax, jax.numpy as jnp
        import numpy as np
        N = 3125
        E = 50000
        S = 64
        V = 32
        NB = 10
        H = 100
        WN = 192
        MID = 96
        NUM_NEIGHBORS = 16.0
        C_S = float(np.sin(np.pi / 8.0))
        C_X = float(np.cos(np.pi / 8.0))
        SQRT3 = float(np.sqrt(3.0))

        def fctp_scalar_attr(xs, xv, attr, Ws, Wv):
            s = xs * attr @ Ws
            v = jnp.einsum('nuc,uo->noc', xv * attr[:, :, None], Wv)
            return (s, v)
        n = node_input.shape[0]
        xs = node_input[:, :S]
        xv = node_input[:, S:].reshape(n, V, 3)
        ssa, sva = fctp_scalar_attr(xs, xv, node_attr, Ws_sc_a, Wv_sc_a)
        ssc, svc = fctp_scalar_attr(xs, xv, node_crystal_attr, Ws_sc_c, Wv_sc_c)
        s_s, s_v = (ssa + ssc, sva + svc)
        l1a_s, l1a_v = fctp_scalar_attr(xs, xv, node_attr, Ws_l1_a, Wv_l1_a)
        l1c_s, l1c_v = fctp_scalar_attr(xs, xv, node_crystal_attr, Ws_l1_c, Wv_l1_c)
        x1s, x1v = (l1a_s + l1c_s, l1a_v + l1c_v)
        weight = jax.nn.silu(edge_length_embedded @ W_fc1) @ W_fc2
        w0 = weight[:, :S]
        w1 = weight[:, S:2 * S]
        w2 = weight[:, 2 * S:2 * S + V]
        w3 = weight[:, 2 * S + V:]
        gs = x1s[edge_src]
        gv = x1v[edge_src]
        e_s = edge_attr[:, :1]
        e_v = edge_attr[:, 1:]
        mid0a = w0 * gs * e_s
        mid0b = w3 * (jnp.einsum('euc,ec->eu', gv, e_v) / SQRT3)
        mid1a = w1[:, :, None] * gs[:, :, None] * e_v[:, None, :]
        mid1b = w2[:, :, None] * gv * e_s[:, :, None]
        edge_feat = jnp.concatenate([mid0a, mid0b, mid1a.reshape(-1, 3 * S), mid1b.reshape(-1, 3 * V)], axis=-1)
        agg = jax.ops.segment_sum(edge_feat, edge_dst, num_segments=n) / np.sqrt(NUM_NEIGHBORS)
        m_s = agg[:, :MID]
        m_v = agg[:, MID:].reshape(n, MID, 3)
        l2a_s, l2a_v = fctp_scalar_attr(m_s, m_v, node_attr, Ws_l2_a, Wv_l2_a)
        l2c_s, l2c_v = fctp_scalar_attr(m_s, m_v, node_crystal_attr, Ws_l2_c, Wv_l2_c)
        m_s, m_v = (l2a_s + l2c_s, l2a_v + l2c_v)
        o_s, o_v = fctp_scalar_attr(m_s, m_v, sym_mask, Ws_l3, Wv_l3)
        out_s = C_S * s_s + C_X * o_s
        out_v = C_S * s_v + C_X * o_v
        return jnp.concatenate([out_s, out_v.reshape(n, 3 * V)], axis=-1)

    def _L2_gnn_ref(node_feature, edge_attr, edge_feature, W_skip0, W_skip1, W_nl0, W_nl1, W_fc1, W_fc2, W_out_s, W_out_v, edge_index):
        import jax, jax.numpy as jnp
        import numpy as np
        N_NODES = 1250
        N_EDGES = 40000
        MUL0, MUL1 = (64, 32)
        EDGE_DIM = 64
        W_NUMEL = 224
        DENOM = 32.0
        SQRT3 = 3.0 ** 0.5
        INV_SQRT3 = 1.0 / SQRT3
        INV_SQRT2 = 2.0 ** (-0.5)

        def _forward(node_feature, edge_attr, edge_feature, W_skip0, W_skip1, W_nl0, W_nl1, W_fc1, W_fc2, W_out_s, W_out_v, edge_index):
            N = node_feature.shape[0]
            E = edge_attr.shape[0]
            s = node_feature[:, :MUL0]
            v = node_feature[:, MUL0:].reshape(N, MUL1, 3)
            skip_s = s @ W_skip0
            skip_v = jnp.einsum('nmi,mk->nki', v, W_skip1)
            s = s @ W_nl0
            v = jnp.einsum('nmi,mk->nki', v, W_nl1)
            rhat = edge_attr / jnp.linalg.norm(edge_attr, axis=-1, keepdims=True)
            sh1 = SQRT3 * rhat
            w = jax.nn.relu(edge_feature @ W_fc1) @ W_fc2
            w0, w1, w2, w3, w4 = jnp.split(w, [64, 128, 160, 192], axis=-1)
            src, dst = (edge_index[0], edge_index[1])
            xs = s[dst]
            xv = v[dst]
            out0a = w0 * xs
            out0b = w3 * (jnp.einsum('emi,ei->em', xv, sh1) * INV_SQRT3)
            out1a = (w1 * xs)[:, :, None] * sh1[:, None, :]
            out1b = w2[:, :, None] * xv
            out1c = w4[:, :, None] * (jnp.cross(xv, sh1[:, None, :]) * INV_SQRT2)
            tp = jnp.concatenate([out0a, out0b, out1a.reshape(E, -1), out1b.reshape(E, -1), out1c.reshape(E, -1)], axis=-1)
            agg = jax.ops.segment_sum(tp, src, num_segments=N) / DENOM
            agg_s = agg[:, :96]
            agg_v = agg[:, 96:].reshape(N, 128, 3)
            out_s = agg_s @ W_out_s + skip_s
            out_v = jnp.einsum('nmi,mk->nki', agg_v, W_out_v) + skip_v
            fs = jax.nn.silu(out_s[:, :MUL0])
            gate = jax.nn.sigmoid(out_s[:, MUL0:MUL0 + 32])
            gv = gate[:, :, None] * out_v
            return jnp.concatenate([fs, gv.reshape(N, -1)], axis=-1)
        return _forward(node_feature, edge_attr, edge_feature, W_skip0, W_skip1, W_nl0, W_nl1, W_fc1, W_fc2, W_out_s, W_out_v, edge_index)

    def _L3_gnn_ref(node_input, node_attr, edge_attr, edge_scalar_attr, Wsc0, Wsc1, Wl1_0, Wl1_1, Wfc1, Wfc2, Wfc3, Wl2_s, Wl2_v, Wa, edge_src, edge_dst):
        import jax, jax.numpy as jnp
        import numpy as np
        N_NODES = 1250
        N_EDGES = 40000
        NUM_NEIGHBORS = 32.0
        INV_SQRT3 = 1.0 / np.sqrt(3.0)

        def _fctp_scalar_attr(xs, xv, Ws, Wv, a):
            out_s = xs @ Ws * (a / np.sqrt(xs.shape[1]))[:, None]
            out_v = jnp.einsum('nuc,uw->nwc', xv, Wv) * (a / np.sqrt(xv.shape[1]))[:, None, None]
            return (out_s, out_v)
        N = node_input.shape[0]
        a = node_attr[:, 0]
        xs = node_input[:, :64]
        xv = node_input[:, 64:].reshape(N, 32, 3)
        sc_s, sc_v = _fctp_scalar_attr(xs, xv, Wsc0, Wsc1, a)
        f_s, f_v = _fctp_scalar_attr(xs, xv, Wl1_0, Wl1_1, a)
        h = jax.nn.gelu(edge_scalar_attr @ Wfc1 / np.sqrt(8.0))
        h = jax.nn.gelu(h @ Wfc2 / np.sqrt(64.0))
        w = h @ Wfc3 / np.sqrt(64.0)
        w0, w1, w2, w3 = (w[:, :64], w[:, 64:128], w[:, 128:160], w[:, 160:192])
        gs = f_s[edge_src]
        gv = f_v[edge_src]
        y0 = edge_attr[:, 0]
        y1 = edge_attr[:, 1:4]
        mid0 = w0 * gs * y0[:, None]
        mid1 = w3 * jnp.einsum('euc,ec->eu', gv, y1) * INV_SQRT3
        mid2 = (w1 * gs)[:, :, None] * y1[:, None, :]
        mid3 = w2[:, :, None] * gv * y0[:, None, None]
        inv = 1.0 / np.sqrt(NUM_NEIGHBORS)
        seg = lambda x: jax.ops.segment_sum(x, edge_dst, num_segments=N) * inv
        ns0, ns1, nv2, nv3 = (seg(mid0), seg(mid1), seg(mid2), seg(mid3))
        mid_s = jnp.concatenate([ns0, ns1], axis=1)
        mid_v = jnp.concatenate([nv2, nv3], axis=1)
        out_s = mid_s @ Wl2_s * (a / np.sqrt(96.0))[:, None]
        out_v = jnp.einsum('nuc,uw->nwc', mid_v, Wl2_v) * (a / np.sqrt(96.0))[:, None, None]
        alpha = mid_s @ Wa * (a / np.sqrt(96.0))[:, None]
        res_s = sc_s + alpha * out_s
        res_v = sc_v + alpha[:, :, None] * out_v
        return jnp.concatenate([res_s, res_v.reshape(N, 96)], axis=1)
    edge_index = jnp.stack([src, dst])
    h = jnp.maximum(_layernorm(x, axis=-1), 0.0)
    x = x + _L0_gnn_ref(h, node_vec1, edge_attr_16, edge_attr_4, src, dst, L0_gnn_Wfc1, L0_gnn_Wfc2, L0_gnn_Wsc0, L0_gnn_Wsc1, L0_gnn_Wl1_0, L0_gnn_Wl1_1, L0_gnn_Wl2_s, L0_gnn_Wl2_v, L0_gnn_Wa)
    h = jnp.maximum(_layernorm(x, axis=-1), 0.0)
    x = x + _L1_gnn_ref(h, node_vec1, node_vec1_n2, node_vec1_n3, edge_attr_4, edge_attr_10, src, dst, L1_gnn_Ws_sc_a, L1_gnn_Wv_sc_a, L1_gnn_Ws_sc_c, L1_gnn_Wv_sc_c, L1_gnn_Ws_l1_a, L1_gnn_Wv_l1_a, L1_gnn_Ws_l1_c, L1_gnn_Wv_l1_c, L1_gnn_W_fc1, L1_gnn_W_fc2, L1_gnn_Ws_l2_a, L1_gnn_Wv_l2_a, L1_gnn_Ws_l2_c, L1_gnn_Wv_l2_c, L1_gnn_Ws_l3, L1_gnn_Wv_l3)
    h = jnp.maximum(_layernorm(x, axis=-1), 0.0)
    x = x + _L2_gnn_ref(h, edge_attr_3, edge_attr_64, L2_gnn_W_skip0, L2_gnn_W_skip1, L2_gnn_W_nl0, L2_gnn_W_nl1, L2_gnn_W_fc1, L2_gnn_W_fc2, L2_gnn_W_out_s, L2_gnn_W_out_v, edge_index)
    h = jnp.maximum(_layernorm(x, axis=-1), 0.0)
    x = x + _L3_gnn_ref(h, node_vec1, edge_attr_4, edge_attr_8, L3_gnn_Wsc0, L3_gnn_Wsc1, L3_gnn_Wl1_0, L3_gnn_Wl1_1, L3_gnn_Wfc1, L3_gnn_Wfc2, L3_gnn_Wfc3, L3_gnn_Wl2_s, L3_gnn_Wl2_v, L3_gnn_Wa, src, dst)
    return x

_drawn_inputs = setup_inputs


def setup_inputs(seed=0):
    import zlib

    import numpy as np

    out = dict(_drawn_inputs(seed))
    spreads = {}
    factors = {}
    for name, (base, spread) in spreads.items():
        noise = np.random.default_rng([zlib.crc32(name.encode()), seed]).standard_normal(out[name].shape)
        drawn = base * np.exp(spread * noise) if base else spread * noise
        out[name] = jnp.asarray(drawn.astype(out[name].dtype))
    for name, factor in factors.items():
        out[name] = (out[name] * factor).astype(out[name].dtype)
    return out
```

```python
from contextlib import ExitStack

import concourse.bass as bass
from concourse import mybir

ALU = mybir.AluOpType
ACT = mybir.ActivationFunctionType
F32 = mybir.dt.float32
I32 = mybir.dt.int32
I16 = mybir.dt.int16
AX_X = mybir.AxisListType.X

N, E, D = 6250, 100000, 160
S, V = 64, 32
P = 128
NT = -(-N // P)
NREST = N - (NT - 1) * P
EP = 125
EC = E // EP
PAIRS = -(-((E + NT * 255) // 256) // 8) * 8
QUADS = PAIRS // 2
ITERS = PAIRS // 8
SLOTS = (QUADS + 2) * 512
CC = 25
CHUNKS = EC // CC
BIG = 640

ROW_D = dict(w=40, a16=0, a10=16, a8=26, sh=34, dl=38, idx=39)
ROW_S = dict(w=69, a64=0, sh=64, dl=67, idx=68)
LAYERS = [
    dict(aw=449, xw=448, mw=96, kin=16, col=ROW_D["a16"], hid=64, wn=192, rows=ROW_D, nout=161, ncat=320),
    dict(aw=448, xw=448, mw=96, kin=10, col=ROW_D["a10"], hid=100, wn=192, rows=ROW_D, nout=320, ncat=640),
    dict(aw=640, xw=640, mw=160, kin=64, col=ROW_S["a64"], hid=64, wn=224, rows=ROW_S, nout=192, ncat=352),
    dict(aw=448, xw=448, mw=96, kin=8, col=ROW_D["a8"], hid=64, wn=192, rows=ROW_D, nout=161, ncat=320),
]
PAIR_STEP = ROW_D["w"]
PAIR_ROWS = PAIR_STEP + ROW_D["sh"]
NC_IDENT, NC_TRI, NC_IOTA, NC_ONES, NC_BUCKET, NC_STEP = 0, 128, 256, 384, 512, 512 + NT
STEPC = -(-PAIRS // P)
NCONST = NC_STEP + STEPC


def shape_constants():
    import numpy as np

    c = np.zeros((P, NCONST), np.float32)
    c[:, NC_IDENT:NC_IDENT + P] = np.eye(P)
    c[:, NC_TRI:NC_TRI + P] = np.triu(np.ones((P, P)), 1)
    c[:, NC_IOTA:NC_IOTA + P] = np.arange(1, P + 1)
    c[:, NC_ONES:NC_ONES + P] = 1.0
    c[:, NC_BUCKET:NC_BUCKET + NT] = np.arange(NT)
    c[:, NC_STEP:] = np.arange(STEPC)[None, :] * P + np.arange(P)[:, None]
    return c


def gnn_kernel(nc, A, out):
    with ExitStack() as ctx:
        sem = lambda name: ctx.enter_context(nc.semaphore(name))

        rows_d = nc.dram_tensor("rows_by_dst", (SLOTS, ROW_D["w"]), F32).ap()
        rows_s = nc.dram_tensor("rows_by_src", (SLOTS, ROW_S["w"]), F32).ap()
        table = nc.dram_tensor("node_table", (NT * P, D), F32).ap()
        skip_dram = nc.dram_tensor("node_skip", (NT * P, 192), F32).ap()
        bucket_dram = nc.dram_tensor("bucket_of_pair", (2, STEPC * P), I16).ap()

        TOTAL = 51900
        arena = ctx.enter_context(nc.sbuf_tensor("arena", [P, TOTAL], F32))
        top = [0]

        def cut(*shape):
            n = 1
            for s in shape:
                n *= s
            off = top[0]
            top[0] += n
            assert top[0] <= TOTAL, (top[0], TOTAL)
            v = arena[:, off:off + n]
            if len(shape) == 2:
                v = v.rearrange("p (a b) -> p a b", b=shape[1])
            elif len(shape) == 3:
                v = v.rearrange("p (a b c) -> p a b c", b=shape[1], c=shape[2])
            elif len(shape) == 4:
                v = v.rearrange("p (a b c d) -> p a b c d", b=shape[1], c=shape[2], d=shape[3])
            return v

        const = cut(NCONST)
        ident = const[:, NC_IDENT:NC_IDENT + P]
        tri = const[:, NC_TRI:NC_TRI + P]
        iota = const[:, NC_IOTA:NC_IOTA + P]
        ones = const[:, NC_ONES:NC_ONES + P]
        X0 = top[0]
        x = cut(NT, D)
        nv = cut(3, NT)
        recip_count = cut(NT)
        attr_sq = cut(NT)
        attr_mask = cut(2, NT)
        ln_sum, ln_mean, ln_sq, ln_rstd, ln_bias = (cut(NT) for _ in range(5))
        eps = cut(1)
        bucket_rows = [cut(STEPC * P // 2).bitcast(I16) for _ in range(2)]
        layer_base = top[0]

        idx_d, idx_s = cut(EC).bitcast(I32), cut(EC).bitcast(I32)
        slot_d, slot_s = cut(EC), cut(EC)
        addr_d, addr_s = cut(EC).bitcast(I32), cut(EC).bitcast(I32)
        low_d, low_s = cut(EC), cut(EC)
        bucket = cut(EC)
        itmp = [cut(EC).bitcast(I32) for _ in range(3)]
        onehot_b, scan_b, ones_e = cut(EC), cut(EC), cut(EC)
        totals, offs, cnt_f, tend, basef = (cut(NT) for _ in range(5))
        cnt_i = cut(NT).bitcast(I32)
        step_cmp, step_f = cut(NT), cut(STEPC)
        step_i = cut(STEPC).bitcast(I16)[:, 0:STEPC]
        zrow = cut(P * 16)
        st64 = [cut(CC, 64) for _ in range(2)]
        st16, st10, st8, st4, st3, sq3 = ([cut(CC, w) for _ in range(2)] for w in (16, 10, 8, 4, 3, 3))
        norm = [cut(3, CC) for _ in range(2)]
        pay_d = [cut(CC, ROW_D["w"]) for _ in range(2)]
        pay_s = [cut(CC, ROW_S["w"]) for _ in range(2)]
        adr = [cut(CC).bitcast(I32) for _ in range(2)]

        B = []
        for L, c in enumerate(LAYERS):
            top[0] = layer_base
            b = {}
            b["agg_off"] = top[0]
            b["agg"] = cut(NT, c["aw"])
            b["w1"] = {0: lambda: cut(128), 1: lambda: cut(2, 100), 2: lambda: cut(64), 3: lambda: cut(128)}[L]()
            b["w2"] = cut(c["wn"] if L == 1 else 2 * c["wn"])
            if L == 3:
                b["wmid"] = cut(128)
            b["ps"] = cut(256 if L == 1 else 160)
            b["pv"] = cut(384 if L == 1 else 192)
            b["oa"] = cut(c["nout"])
            b["ob"] = cut(c["nout"])
            b["om"] = cut(3, c["nout"])
            if L == 2:
                b["oc"] = cut(3, c["nout"])
            rings = top[0]
            b["rows"] = [cut(4, c["rows"]["w"]) for _ in range(4)]
            b["gath"] = [cut(2, D) for _ in range(4)]
            b["X"] = [cut(2, c["xw"]) for _ in range(2)]
            b["S"] = [cut(2, 4 if L == 2 else 5, P) for _ in range(2)]
            b["tT"] = [cut(4 if L == 2 else 2, P) for _ in range(2)]
            b["hT"] = [cut(4 if L == 1 else 2, P) for _ in range(2)]
            if L == 3:
                b["h1T"] = [cut(2, P) for _ in range(2)]
            top[0] = rings
            b["h"] = [cut(D) for _ in range(2)]
            b["hTs"] = [cut(P) for _ in range(2)]
            b["hTv"] = [cut(P) for _ in range(2)]
            b["u"] = [cut(352) for _ in range(2)]
            b["utmp"] = [cut(320) for _ in range(2)]
            b["sk"] = [cut(192) for _ in range(2)]
            b["scal"] = [cut(8) for _ in range(2)]
            top[0] = rings
            b["_pad"] = cut(2 * D + 4 * P + 2 * 352 + 2 * 320 + 2 * 192 + 16)
            b["aggS"] = [cut(c["aw"]) for _ in range(2)]
            nA = 4 if L == 2 else 1
            b["aTA"] = [cut(nA, P) for _ in range(2)]
            b["aTB"] = [cut(4, P) for _ in range(2)]
            if L in (0, 1, 3):
                top[0] = max(top[0], rings + 8000)
            b["ws"] = cut(2, 640) if L != 2 else None
            B.append(b)
        B[2]["ws"] = arena[:, B[2]["agg_off"] + 20000:B[2]["agg_off"] + 21280].rearrange("p (a b) -> p a b", b=640)

        bank = ctx.enter_context(nc.psum_tensor("bank", [P, 8, 512], F32))

        stage_end = sem("stage_end")
        const_in = sem("const_in")
        idx_in, ones_set, zero_set = sem("idx_in"), sem("ones_set"), sem("zero_set")
        x_in = sem("x_in")
        weights_in = sem("weights_in")
        prefilled = sem("prefilled")
        dve_step, act_step = sem("dve_step"), sem("act_step")
        totals_done, offsets_done = sem("totals_done"), sem("offsets_done")
        step_out, step_in = sem("step_out"), sem("step_in")
        table_done = sem("table_done")
        stage_in = [sem(f"stage_in{i}") for i in range(2)]
        payload_ready, norm_ss, norm_root = sem("payload_ready"), sem("norm_ss"), sem("norm_root")
        scattered = [sem(f"scattered{i}") for i in range(2)]
        counts_ready = sem("counts_ready")
        pool_steps = sem("pool_steps")
        rows_in = [sem(f"rows_in{i}") for i in range(4)]
        gath_in = [sem(f"gath_in{i}") for i in range(4)]
        prod_free = sem("prod_free")
        turned, turned_sb, hidden1, hidden1_sb, hidden2, hidden_sb = (
            sem(n) for n in ("turned", "turned_sb", "hidden1", "hidden1_sb", "hidden2", "hidden_sb"))
        onehot_ready = sem("onehot_ready")
        w_ready, first_products, copies_done, x_ready = sem("w_ready"), sem("first_products"), sem("copies_done"), sem("x_ready")
        sums_ready, summed = sem("sums_ready"), sem("summed")
        ln_a, ln_b = sem("ln_a"), sem("ln_b")
        h_ready, hT_ready, hT_sb, f_ready, f_tmp, u_ready, node_x = (
            sem(n) for n in ("h_ready", "hT_ready", "hT_sb", "f_ready", "f_tmp", "u_ready", "node_x"))
        table_out = [sem(f"table_out{i}") for i in range(2)]
        agg_zero = sem("agg_zero")
        agg_st, agg_T, aggA_sb, aggB_sb, o_ready, o_tmp, o_gate, o_y = (
            sem(n) for n in ("agg_st", "agg_T", "aggA_sb", "aggB_sb", "o_ready", "o_tmp", "o_gate", "o_y"))
        skip_in = [sem(f"skip_in{i}") for i in range(2)]
        out_done = sem("out_done")

        block = ctx.enter_context(nc.Block())
        ENGINES = 5

        def stage(e, n):
            e.drain().then_inc(stage_end, 1)
            e.wait_ge(stage_end, ENGINES * n)

        class Count:

            def __init__(self, s):
                self.s, self.n = s, 0

            def up(self, ins):
                ins.then_inc(self.s, 1)
                self.n += 1

        def weight_loads(L):
            b, c = B[L], LAYERS[L]
            lo, hi = b["ws"][:, 0, :], b["ws"][:, 1, :]
            r = []

            def spread(dst, w):
                for m in range(3):
                    r.append((dst[m:96:3, 32 * m:32 * m + 32], w))

            if L in (0, 3):
                p = f"L{L}_gnn_"
                r.append((lo[0:64, 0:64], A[p + "Wl1_0"]))
                r.append((lo[0:64, 64:128], A[p + "Wsc0"]))
                spread(hi[:, 0:96], A[p + "Wl1_1"])
                spread(hi[:, 96:192], A[p + "Wsc1"])
                r.append((lo[0:96, 128:192], A[p + "Wl2_s"]))
                r.append((lo[0:96, 192:193], A[p + "Wa"]))
                r.append((lo[0:64, 193:225], A[p + "Wl2_v"][0:64, :]))
                for m in range(3):
                    r.append((lo[32 * m:32 * m + 32, 225:257], A[p + "Wl2_v"][64:96, :]))
            if L == 1:
                p = "L1_gnn_"
                r.append((lo[0:64, 0:64], A[p + "Ws_l1_a"]))
                r.append((lo[0:64, 64:128], A[p + "Ws_sc_a"]))
                r.append((lo[0:64, 128:192], A[p + "Ws_l1_c"]))
                r.append((lo[0:64, 192:256], A[p + "Ws_sc_c"]))
                spread(hi[:, 0:96], A[p + "Wv_l1_a"])
                spread(hi[:, 96:192], A[p + "Wv_sc_a"])
                spread(hi[:, 192:288], A[p + "Wv_l1_c"])
                spread(hi[:, 288:384], A[p + "Wv_sc_c"])
                for i, n in enumerate(("Ws_l2_a", "Ws_l2_c", "Wv_l2_a", "Wv_l2_c")):
                    r.append((lo[0:96, 256 + 96 * i:352 + 96 * i], A[p + n]))
                r.append((hi[0:96, 384:448], A[p + "Ws_l3"]))
                r.append((hi[0:96, 448:480], A[p + "Wv_l3"]))
            if L == 2:
                p = "L2_gnn_"
                r.append((lo[0:64, 0:64], A[p + "W_nl0"]))
                r.append((lo[0:64, 64:160], A[p + "W_skip0"]))
                spread(hi[:, 0:96], A[p + "W_nl1"])
                spread(hi[:, 96:192], A[p + "W_skip1"])
                r.append((lo[0:96, 160:256], A[p + "W_out_s"]))
                r.append((lo[0:64, 256:288], A[p + "W_out_v"][0:64, :]))
                for m in range(3):
                    r.append((lo[32 * m:32 * m + 32, 288:320], A[p + "W_out_v"][64:96, :]))
                for q in range(2):
                    r.append((lo[32 * q:32 * q + 32, 320:352], A[p + "W_out_v"][96:128, :]))
                r.append((lo[64:96, 352:384], A[p + "W_out_v"][64:96, :]))
            if L == 0:
                for g in range(2):
                    at = PAIR_STEP * g + c["col"]
                    r.append((b["w1"][at:at + 16, 64 * g:64 * g + 64], A["L0_gnn_Wfc1"]))
                    r.append((hi[64 * g:64 * g + 64, 192:384], A["L0_gnn_Wfc2"]))
            if L == 1:
                for g in range(2):
                    at = PAIR_STEP * g + c["col"]
                    r.append((b["w1"][at:at + 10, g, :], A["L1_gnn_W_fc1"]))
                r.append((b["w2"][0:100, :], A["L1_gnn_W_fc2"]))
            if L == 2:
                r.append((b["w1"][0:64, :], A["L2_gnn_W_fc1"]))
                for g in range(2):
                    r.append((b["w2"][64 * g:64 * g + 64, 224 * g:224 * g + 224], A["L2_gnn_W_fc2"]))
            if L == 3:
                for g in range(2):
                    at = PAIR_STEP * g + c["col"]
                    r.append((b["w1"][at:at + 8, 64 * g:64 * g + 64], A["L3_gnn_Wfc1"]))
                    r.append((b["wmid"][64 * g:64 * g + 64, 64 * g:64 * g + 64], A["L3_gnn_Wfc2"]))
                    r.append((hi[64 * g:64 * g + 64, 192:384], A["L3_gnn_Wfc3"]))
            return r

        n_loads = [len(weight_loads(L)) for L in range(4)]
        loads_to = [16 * sum(n_loads[:L + 1]) for L in range(4)]

        def stage_of(L, k):
            return 4 + 5 * L + k

        tile_at = lambda t: bass.ds(X0 + t * D, D)
        x_tile = lambda t: arena[:, tile_at(t)]

        def agg_tile(L, t):
            return arena[:, bass.ds(B[L]["agg_off"] + t * LAYERS[L]["aw"], LAYERS[L]["aw"])]

        def out_count(upto, s):
            tiles = NT - NT // 2 if s == 0 else NT // 2
            return sum(16 * tiles * (2 if L == 2 else 1) for L in range(upto))

        def rows_base(L, q):
            return L * (ITERS + (1 if q < 2 else 0))

        def gath_base(L, s):
            return L * (2 * ITERS + (1 if s == 0 else 0))

        nv_off = X0 + NT * D
        recip_off = nv_off + 3 * NT
        sq_off = recip_off + NT
        mask_off = sq_off + NT
        ln_rstd_off = mask_off + 2 * NT + 3 * NT
        ln_bias_off = ln_rstd_off + NT

        def arena_col(off, t):
            return arena[:, off + t:off + t + 1] if isinstance(t, int) else arena[:, bass.ds(t + off, 1)]

        @block.sync
        def _(sp):
            sp.dma_start(const, A["consts"]).then_inc(const_in, 16)
            sp.dma_start(idx_d[0:EP, :], A["dst"].rearrange("(p c) -> p c", c=EC)).then_inc(idx_in, 16)
            sp.dma_start(idx_s[0:EP, :], A["src"].rearrange("(p c) -> p c", c=EC)).then_inc(idx_in, 16)
            sp.wait_ge(zero_set, 3)
            full = (NT - 1) * P
            sp.dma_start(x[:, 0:NT - 1, :], A["x"][0:full, :].rearrange("(t p) d -> p t d", p=P)).then_inc(x_in, 16)
            sp.dma_start(x[0:NREST, NT - 1, :], A["x"][full:N, :]).then_inc(x_in, 16)
            for rows, w in ((rows_d, ROW_D["w"]), (rows_s, ROW_S["w"])):
                per = SLOTS * w // P
                whole = per // 2048
                flat = rows.rearrange("(p r) w -> p (r w)", p=P)
                for k in range(0, whole):
                    sp.dma_start(flat[:, 2048 * k:2048 * k + 2048], zrow).then_inc(prefilled, 16)
                if per % 2048:
                    sp.dma_start(flat[:, 2048 * whole:per], zrow[:, 0:per % 2048]).then_inc(prefilled, 16)
            for i, name in enumerate(("node_vec1", "node_vec1_n2", "node_vec1_n3")):
                with nc.allow_non_contiguous_dma(reason="node scalars, one per partition"):
                    sp.dma_start(nv[:, i, 0:NT - 1], A[name][0:full, :].rearrange("(t p) o -> p (t o)", p=P)).then_inc(x_in, 16)
                    sp.dma_start(nv[0:NREST, i, NT - 1:NT], A[name][full:N, :]).then_inc(x_in, 16)
            for o in range(2):
                sp.wait_ge(table_done, o + 1)
                with nc.allow_non_contiguous_dma(reason="a short table"):
                    sp.dma_start(bucket_dram[o, :].rearrange("(c p) -> p c", p=P), step_i).then_inc(step_out, 16)
                sp.wait_ge(step_out, 16 * (o + 1))
                sp.dma_start(bucket_rows[o][0:1, :], bucket_dram[o:o + 1, :]).then_inc(step_in, 16)
                sp.wait_ge(step_in, 16 * (o + 1))
            sp.wait_ge(x_in, 16 * 8)
            n_fill = sum(-(-(SLOTS * w // P) // 2048) for w in (ROW_D["w"], ROW_S["w"]))
            sp.wait_ge(prefilled, 16 * n_fill)
            stage(sp, 1)

            def chunk(name, k):
                return A[name].rearrange("(p c) w -> p (c w)", c=EC)[:, bass.ds(k * (CC * A[name].shape[1]), CC * A[name].shape[1])]

            for o, loads in enumerate(((("edge_attr_16", st16), ("edge_attr_10", st10), ("edge_attr_8", st8), ("edge_attr_4", st4)),
                                       (("edge_attr_64", st64), ("edge_attr_3", st3)))):
                with sp.Fori(0, CHUNKS // 2) as i:
                    for s in range(2):
                        sp.wait_ge(payload_ready, i * 2 + (s + 1 + o * CHUNKS))
                        for name, st in loads:
                            sp.dma_start(st[s][0:EP, :, :].rearrange("p c w -> p (c w)"), chunk(name, i * 2 + s)).then_inc(stage_in[s], 16)
                stage(sp, 2 + o)

            for L, c in enumerate(LAYERS):
                b = B[L]
                sp.wait_ge(agg_zero, 2 * L + 1)
                with nc.allow_non_contiguous_dma(reason="weights"):
                    for dst, srcw in weight_loads(L):
                        sp.dma_start(dst, srcw).then_inc(weights_in, 16)
                sp.wait_ge(weights_in, loads_to[L])
                stage(sp, stage_of(L, 0))
                stage(sp, stage_of(L, 1))

                def store(t, s, k):
                    sp.wait_ge(u_ready, k + 2)
                    sp.dma_start(table[bass.ds(t * P, P), :], b["u"][s][:, 0:D]).then_inc(table_out[s], 16)
                    if L == 2:
                        sp.dma_start(skip_dram[bass.ds(t * P, P), :], b["u"][s][:, 160:352]).then_inc(table_out[s], 16)

                with sp.Fori(0, NT // 2) as i:
                    for s in range(2):
                        store(i * 2 + s, s, i * 2 + (NT * L + s + 1))
                store(NT - 1, 0, NT * L + NT)
                for s in range(2):
                    sp.wait_ge(table_out[s], out_count(L + 1, s))
                stage(sp, stage_of(L, 2))

                R = rows_s if L == 2 else rows_d
                w = c["rows"]["w"]
                per_quad = R.rearrange("(q p u) w -> p q (u w)", p=P, u=4)

                def load(q, s, k):
                    sp.wait_ge(x_ready, k)
                    sp.wait_ge(copies_done, k)
                    sp.dma_start(b["rows"][s].rearrange("p a b -> p (a b)"), per_quad[:, q, :] if isinstance(q, int) else
                                 per_quad[:, bass.ds(q, 1), :].rearrange("p a b -> p (a b)")).then_inc(rows_in[s], 16)

                with sp.Fori(0, ITERS) as i:
                    for s in range(4):
                        load(i * 4 + s, s, i * 8 + ((PAIRS + 1) * L + 2 * s + 2))
                for s in range(2):
                    load(QUADS + s, s, (PAIRS + 1) * L + 2 * (QUADS + s) + 2 - s * 0)
                stage(sp, stage_of(L, 3))

                if L == 2:
                    def fetch(t, s, k):
                        if k is not None:
                            sp.wait_ge(o_y, k)
                        sp.dma_start(b["sk"][s], skip_dram[bass.ds(t * P, P), :]).then_inc(skip_in[s], 16)

                    fetch(0, 0, None)
                    fetch(1, 1, None)
                    with sp.Fori(0, NT // 2 - 1) as i:
                        for s in range(2):
                            fetch(i * 2 + (s + 2), s, i * 2 + (s + 1))
                    fetch(NT - 1, 0, NT - 2)
                    sp.wait_ge(o_y, NT)
                stage(sp, stage_of(L, 4))
            sp.dma_start(out[0:full, :].rearrange("(t p) d -> p t d", p=P), x[:, 0:NT - 1, :]).then_inc(out_done, 16)
            sp.dma_start(out[full:N, :], x[0:NREST, NT - 1, :]).then_inc(out_done, 16)
            sp.wait_ge(out_done, 32)

        @block.gpsimd
        def _(pool):
            pool.memset(x[:, NT - 1, :], 0.0).then_inc(zero_set, 1)
            pool.memset(nv, 0.0).then_inc(zero_set, 1)
            pool.memset(zrow, 0.0).then_inc(zero_set, 1)
            stage(pool, 1)
            for o, (pay, w, rows) in enumerate(((pay_d, ROW_D["w"], rows_d), (pay_s, ROW_S["w"], rows_s))):
                with pool.Fori(0, CHUNKS // 2) as i:
                    for s in range(2):
                        pool.wait_ge(payload_ready, i * 2 + (CHUNKS * o + s + 3))
                        pool.sem_inc(pool_steps, 1)
                        for j in range(CC):
                            pool.indirect_dma_start(
                                out=rows, out_offset=bass.IndirectOffsetOnAxis(ap=adr[s][0:EP, j:j + 1], axis=0),
                                in_=pay[s][0:EP, j, :], in_offset=None).then_inc(scattered[s], 16)
                for s in range(2):
                    pool.wait_ge(scattered[s], 16 * CC * (CHUNKS // 2) * (o + 1))
                stage(pool, 2 + o)
            for L, c in enumerate(LAYERS):
                b = B[L]
                hi_end = b["agg_off"] + NT * c["aw"]
                first = [b["w1"], b["w2"]] + ([b["wmid"]] if L == 3 else []) + [b["ws"], b["pv"], b["oa"], b["ob"], b["om"]] + ([b["oc"]] if L == 2 else [])
                for k, v in enumerate(first):
                    ins = pool.memset(v, 0.0)
                    if k == len(first) - 1:
                        ins.then_inc(agg_zero, 1)
                stage(pool, stage_of(L, 0))
                stage(pool, stage_of(L, 1))
                pool.memset(b["agg"], 0.0).then_inc(agg_zero, 1)
                stage(pool, stage_of(L, 2))

                def gather(rs, q, s, k_rows, k_free):
                    pool.wait_ge(rows_in[q], k_rows)
                    pool.sem_inc(pool_steps, 1)
                    pool.wait_ge(prod_free, k_free)
                    pool.sem_inc(pool_steps, 1)
                    for g in range(2):
                        u = 2 * (rs % 2) + g
                        col = c["rows"]["idx"]
                        pool.indirect_dma_start(
                            out=b["gath"][s][:, g, :], out_offset=None, in_=table,
                            in_offset=bass.IndirectOffsetOnAxis(ap=b["rows"][q].bitcast(I32)[:, u, col:col + 1], axis=0),
                        ).then_inc(gath_in[s], 16)

                with pool.Fori(0, ITERS) as i:
                    for r in range(8):
                        gather(r, r // 2, r % 4, i * 16 + 16 * (rows_base(L, r // 2) + 1), i * 8 + ((PAIRS + 1) * L + r + 1))
                gather(0, 0, 0, 16 * (rows_base(L, 0) + ITERS + 1), (PAIRS + 1) * L + PAIRS + 1)
                stage(pool, stage_of(L, 3))
                stage(pool, stage_of(L, 4))

        @block.scalar
        def _(act):
            act.wait_ge(const_in, 16)
            stage(act, 1)
            stage(act, 2)
            with act.Fori(0, CHUNKS // 2) as i:
                for s in range(2):
                    act.wait_ge(norm_ss, i * 2 + (s + 1))
                    act.activation(norm[s][0:EP, 1, :], norm[s][0:EP, 0, :], ACT.Sqrt).then_inc(norm_root, 1)
            stage(act, 3)
            for L, c in enumerate(LAYERS):
                b = B[L]
                stage(act, stage_of(L, 0))
                sq = arena[:, b["agg_off"]:b["agg_off"] + NT * D]
                act.wait_ge(ln_a, 2 * L + 1)
                act.activation(sq, sq, ACT.Square).then_inc(ln_b, 1)
                act.wait_ge(ln_a, 2 * L + 2)
                act.activation(ln_rstd, ln_sq, ACT.Sqrt, bias=eps, scale=1.0 / D).then_inc(ln_b, 1)
                stage(act, stage_of(L, 1))

                def normed(t, s, k):
                    act.wait_ge(hT_ready, k)
                    act.activation(b["h"][s], x_tile(t), ACT.Relu, bias=arena_col(ln_bias_off, t),
                                   scale=arena_col(ln_rstd_off, t)).then_inc(h_ready, 1)

                def second(t, s, k):
                    act.wait_ge(f_ready, k)
                    act.activation(b["utmp"][s], bank[:, 4 + 2 * s + 1, 0:320], ACT.Copy, scale=arena_col(nv_off + NT, t)).then_inc(f_tmp, 1)

                NB = NT * L
                normed(0, 0, NB + 1)
                normed(1, 1, NB + 2)
                with act.Fori(0, NT // 2 - 1) as i:
                    for s in range(2):
                        normed(i * 2 + (s + 2), s, i * 2 + (NB + s + 3))
                        if L == 1:
                            second(i * 2 + s, s, i * 2 + (NB + s + 1))
                normed(NT - 1, 0, NB + NT)
                if L == 1:
                    for t in range(NT - 3, NT):
                        second(t, t % 2, NB + t + 1)
                stage(act, stage_of(L, 2))

                def act_turn(par, kt):
                    act.wait_ge(turned, kt)
                    rowsn, cols = (ROW_S["w"], 512) if L == 2 else (PAIR_ROWS, 256)
                    act.activation(b["tT"][par][0:rowsn, :, :], bank[0:rowsn, 0, 0:cols].rearrange("p (a b) -> p a b", b=P),
                                   ACT.Copy).then_inc(turned_sb, 1)

                def act_hidden(par, kh):
                    act.wait_ge(hidden1, kh)
                    if L == 0:
                        act.activation(b["hT"][par], bank[:, 1, 0:256].rearrange("p (a b) -> p a b", b=P), ACT.Silu, scale=0.25).then_inc(hidden_sb, 1)
                    elif L == 1:
                        act.activation(b["hT"][par][0:100, :, :], bank[0:100, 1, :].rearrange("p (a b) -> p a b", b=P), ACT.Silu).then_inc(hidden_sb, 1)
                    elif L == 2:
                        act.activation(b["hT"][par], bank[:, 1, 0:256].rearrange("p (a b) -> p a b", b=P), ACT.Relu).then_inc(hidden_sb, 1)
                    else:
                        act.activation(b["h1T"][par], bank[:, 1, 0:256].rearrange("p (a b) -> p a b", b=P), ACT.Gelu_apprx_tanh,
                                       scale=8.0 ** -0.5).then_inc(hidden1_sb, 1)

                def act_hidden2(par, kh):
                    act.wait_ge(hidden2, kh)
                    act.activation(b["hT"][par], bank[:, 1, 256:512].rearrange("p (a b) -> p a b", b=P), ACT.Gelu_apprx_tanh,
                                   scale=0.125).then_inc(hidden_sb, 1)

                def act_pair(q, rp, s, kp):
                    act.wait_ge(onehot_ready, kp)
                    rows, Sx, rw = b["rows"][q], b["S"][s], c["rows"]
                    plain = 0 if L == 2 else 4
                    for k in (2, 3):
                        sh = rw["sh"] + (k - 1 if L == 2 else k)
                        for g in range(2):
                            act.activation(Sx[:, g, k, :], Sx[:, g, plain, :], ACT.Copy, scale=rows[:, 2 * rp + g, sh:sh + 1])
                    act.wait_ge(first_products, kp)
                    X, mw = b["X"][s], c["mw"]
                    Xm = X[:, :, 160:160 + 3 * mw].rearrange("p g (m w) -> p g m w", m=3)
                    act.activation(Xm[:, :, 1:3, 0:64], Xm[:, :, 0:1, 0:64].to_broadcast([P, 2, 2, 64]), ACT.Copy).then_inc(copies_done, 1)

                QB, PB = (QUADS + 2) * L, (PAIRS + 1) * L
                act_turn(0, QB + 1)
                act_turn(1, QB + 2)
                act_hidden(0, QB + 1)
                if L == 3:
                    act_hidden2(0, 1)
                act_hidden(1, QB + 2)
                act_pair(0, 0, 0, PB + 1)
                with act.Fori(0, ITERS) as i:
                    for q in range(4):
                        act_turn(q % 2, i * 4 + (QB + q + 3))
                        if L == 3:
                            act_hidden2((q + 1) % 2, i * 4 + (q + 2))
                        act_pair(q, 1, 1, i * 8 + (PB + 2 * q + 2))
                        act_hidden(q % 2, i * 4 + (QB + q + 3))
                        act_pair((q + 1) % 4, 0, 0, i * 8 + (PB + 2 * q + 3))
                stage(act, stage_of(L, 3))

                def take(t, s, k):
                    act.wait_ge(agg_T, k)
                    act.activation(b["aggS"][s], agg_tile(L, t), ACT.Identity if L == 2 else ACT.Copy, scale=arena_col(recip_off, t) if L == 0 else 1.0).then_inc(agg_st, 1)

                def chunkA(s, k):
                    act.wait_ge(agg_T, k)
                    nA = 4 if L == 2 else 1
                    act.activation(b["aTA"][s][0:64, :, :], bank[0:64, 2 * s, 0:nA * P].rearrange("p (a b) -> p a b", b=P),
                                   ACT.Identity if L == 2 else ACT.Copy).then_inc(aggA_sb, 1)

                def after(t, s, k):
                    if L == 1:
                        act.wait_ge(o_ready, k)
                        act.activation(b["utmp"][s][:, 0:160], bank[:, 4 + s, 160:320], ACT.Copy, scale=arena_col(mask_off + NT, t)).then_inc(o_tmp, 1)
                    if L == 2:
                        act.wait_ge(o_y, k - 2 * NT)
                        act.activation(b["utmp"][s][:, 0:96], b["u"][s][:, 0:96], ACT.Sigmoid).then_inc(o_gate, 1)

                if L == 0:
                    act.wait_ge(counts_ready, 1)
                take(0, 0, NB + 1)
                take(1, 1, NB + 2)
                with act.Fori(0, NT // 2 - 1) as i:
                    for s in range(2):
                        chunkA(s, i * 2 + (NB + s + 3))
                        take(i * 2 + (s + 2), s, i * 2 + (NB + s + 3))
                        after(i * 2 + s, s, i * 2 + (NB + s + 1))
                for t in range(NT - 3, NT):
                    chunkA(t % 2, NB + t + 3)
                    if t == NT - 3:
                        take(NT - 1, 0, NB + NT)
                    after(t, t % 2, NB + t + 1)
                stage(act, stage_of(L, 4))

        @block.tensor
        def _(pe):
            pe.sem_inc(hT_ready, 2)
            pe.sem_inc(agg_T, 2)
            pe.wait_ge(const_in, 16)
            for o in range(2):
                pe.wait_ge(totals_done, o + 1)
                pe.matmul(bank[0:EP, 0, 0:NT], tri[0:EP, 0:EP], totals[0:EP, :], start=True, stop=True)
                pe.matmul(bank[:, 1, 0:NT], ones[0:EP, :], totals[0:EP, :], start=True, stop=True).then_inc(offsets_done, 1)
            stage(pe, 1)
            stage(pe, 2)
            stage(pe, 3)
            for L, c in enumerate(LAYERS):
                b = B[L]
                if L == 1:
                    lo, hi = b["ws"][:, 0, :], b["ws"][:, 1, :]
                    pe.wait_ge(weights_in, loads_to[L])
                    for k in range(4):
                        ins = pe.transpose(bank[0:96, 0, 96 * k:96 * k + 96], lo[0:96, 256 + 96 * k:352 + 96 * k], ident[0:96, 0:96])
                    ins.then_inc(offsets_done, 1)
                    pe.wait_ge(totals_done, 3)
                    for k, (cols, wid) in enumerate(((384, 64), (384, 64), (448, 32), (448, 32))):
                        ins = pe.matmul(bank[0:96, 1, 64 * k:64 * k + wid], lo[0:96, 256 + 96 * k:352 + 96 * k], hi[0:96, cols:cols + wid], start=True, stop=True)
                    for k in range(2):
                        for m in range(3):
                            ins = pe.matmul(bank[32 * m:32 * m + 32, 2, 32 * k:32 * k + 32],
                                            lo[0:96, 256 + 96 * (2 + k) + 64:256 + 96 * (2 + k) + 96], hi[0:96, 448:480], start=True, stop=True,
                                            tile_position=(0, 32 * m))
                    ins.then_inc(offsets_done, 1)
                stage(pe, stage_of(L, 0))
                stage(pe, stage_of(L, 1))

                def turn_h(s, k):
                    pe.wait_ge(h_ready, k)
                    pe.transpose(bank[0:96, s, P:2 * P], b["h"][s][:, 64:160], ident)
                    pe.transpose(bank[0:64, s, 0:P], b["h"][s][:, 0:64], ident).then_inc(hT_ready, 1)

                def mix(s, k, kfree):
                    pe.wait_ge(hT_sb, k)
                    pe.wait_ge(u_ready, kfree)
                    f0, f1 = 4 + 2 * s, 5 + 2 * s
                    hs, hv = b["hTs"][s][0:64, :], b["hTv"][s][0:96, :]
                    if L == 2:
                        parts = [(f0, 64, 96, hv, b["pv"][0:96, 0:96]), (f0, 256, 96, hv, b["pv"][0:96, 96:192]),
                                 (f0, 0, 64, hs, b["ps"][0:64, 0:64]), (f0, 160, 96, hs, b["ps"][0:64, 64:160])]
                    else:
                        parts = []
                        for a in range(2 if L == 1 else 1):
                            for z in range(2):
                                parts.append(((f0, f1)[a], 160 * z + 64, 96, hv, b["pv"][0:96, 192 * a + 96 * z:192 * a + 96 * z + 96]))
                                parts.append(((f0, f1)[a], 160 * z, 64, hs, b["ps"][0:64, 128 * a + 64 * z:128 * a + 64 * z + 64]))
                    for bk, o, n, l, r in parts:
                        ins = pe.matmul(bank[:, bk, o:o + n], l, r, start=True, stop=True)
                    ins.then_inc(f_ready, 1)

                NB = NT * L
                turn_h(0, NB + 1)
                with pe.Fori(0, NT // 2) as i:
                    for s in range(2):
                        turn_h(1 - s, i * 2 + (NB + s + 2))
                        mix(s, i * 2 + (NB + s + 1), i * 2 + (NB + s + 1))
                mix(0, NB + NT, NB + NT)
                stage(pe, stage_of(L, 2))

                kin, wn, xw, mw = c["kin"], c["wn"], c["xw"], c["mw"]
                QB, PB = (QUADS + 2) * L, (PAIRS + 1) * L

                def turn(q, par, k_rows, k_bank):
                    pe.wait_ge(rows_in[q], k_rows)
                    if k_bank is not None:
                        pe.wait_ge(turned_sb, k_bank)
                    rows = b["rows"][q]
                    if L == 2:
                        for u in range(4):
                            ins = pe.transpose(bank[0:ROW_S["w"], 0, P * u:P * u + P], rows[:, u, :], ident)
                    else:
                        flat = rows.rearrange("p a b -> p (a b)")
                        for v in range(2):
                            ins = pe.transpose(bank[0:PAIR_ROWS, 0, P * v:P * v + P],
                                               flat[:, 2 * PAIR_STEP * v:2 * PAIR_STEP * v + PAIR_ROWS], ident)
                    ins.then_inc(turned, 1)

                def first_layer(par, k_turned, k_bank):
                    pe.wait_ge(turned_sb, k_turned)
                    if k_bank is not None:
                        pe.wait_ge(hidden_sb, k_bank)
                    tT = b["tT"][par]
                    if L == 2:
                        for g in range(2):
                            ins = pe.matmul(bank[64 * g:64 * g + 64, 1, 0:256], b["w1"][0:ROW_S["w"], :],
                                            tT[0:ROW_S["w"], g:4:2, :], start=True, stop=True, tile_position=(0, 64 * g))
                    elif L == 1:
                        for u in range(4):
                            ins = pe.matmul(bank[0:100, 1, P * u:P * u + P], b["w1"][0:PAIR_ROWS, u % 2, :],
                                            tT[0:PAIR_ROWS, u // 2, :], start=True, stop=True)
                    else:
                        ins = pe.matmul(bank[:, 1, 0:256], b["w1"][0:PAIR_ROWS, :], tT[0:PAIR_ROWS, :, :], start=True, stop=True)
                    ins.then_inc(hidden1, 1)

                def second_layer(par, k):
                    pe.wait_ge(hidden1_sb, k)
                    for v in range(2):
                        ins = pe.matmul(bank[:, 1, 256 + P * v:256 + P * v + P], b["wmid"], b["h1T"][par][:, v, :], start=True, stop=True)
                    ins.then_inc(hidden2, 1)

                def edge_weights(rp, par, s, k_hidden, k_free):
                    pe.wait_ge(hidden_sb, k_hidden)
                    pe.wait_ge(prod_free, k_free)
                    if L == 1:
                        for g in range(2):
                            ins = pe.matmul(bank[:, 2 + s, wn * g:wn * g + wn], b["hT"][par][0:100, 2 * rp + g, :], b["w2"][0:100, :],
                                            start=True, stop=True)
                    else:
                        ins = pe.matmul(bank[:, 2 + s, 0:2 * wn], b["hT"][par][:, rp, :], b["w2"], start=True, stop=True)
                    ins.then_inc(w_ready, 1)

                def sums(s, k_x, k_free):
                    pe.wait_ge(x_ready, k_x + 8)
                    pe.wait_ge(copies_done, k_x + 8)
                    pe.wait_ge(summed, k_free)
                    X, Sx = b["X"][s], b["S"][s]
                    for g in range(2):
                        last = g == 1
                        for k in range(4):
                            first = g == 0 and (k == 0 or (L == 2 and k == 2))
                            if L == 2:
                                o = bank[:, 4 + 2 * s + k // 2, 160 * (k % 2):160 * (k % 2) + 160]
                            elif k == 0:
                                o = bank[:, 4 + 2 * s, 0:160]
                            else:
                                o = bank[:, 4 + 2 * s, 160 + mw * (k - 1):160 + mw * k]
                            r = X[:, g, 0:160] if k == 0 else X[:, g, 160 + mw * (k - 1):160 + mw * k]
                            ins = pe.matmul(o, Sx[:, g, k, :], r, start=first, stop=last, skip_group_check=True)
                        if L == 0:
                            ins = pe.matmul(bank[:, 4 + 2 * s, 448:449], Sx[:, g, 4, :], ones[:, 0:1], start=False, stop=last, skip_group_check=True)
                    ins.then_inc(sums_ready, 1)

                turn(0, 0, 16 * (rows_base(L, 0) + 1), QB if L else None)
                turn(1, 1, 16 * (rows_base(L, 1) + 1), QB + 1)
                first_layer(0, QB + 1, QB if L else None)
                if L == 3:
                    second_layer(0, 1)
                first_layer(1, QB + 2, QB + 1)
                edge_weights(0, 0, 0, QB + 1, PB + 3)
                with pe.Fori(0, ITERS) as i:
                    for q in range(4):
                        nq = (q + 2) % 4
                        turn(nq, q % 2, i * 16 + 16 * (rows_base(L, nq) + (1 if q < 2 else 2)), i * 4 + (QB + q + 2))
                        if L == 3:
                            second_layer((q + 1) % 2, i * 4 + (q + 2))
                        edge_weights(1, q % 2, 1, i * 4 + (QB + q + 1), i * 8 + (PB + 2 * q + 4))
                        sums(0, i * 8 + (PB + 2 * q + 1), i * 8 + (PAIRS * L + 2 * q + 1))
                        first_layer(q % 2, i * 4 + (QB + q + 3), i * 4 + (QB + q + 2))
                        edge_weights(0, (q + 1) % 2, 0, i * 4 + (QB + q + 2), i * 8 + (PB + 2 * q + 5))
                        sums(1, i * 8 + (PB + 2 * q + 2), i * 8 + (PAIRS * L + 2 * q + 2))
                stage(pe, stage_of(L, 3))

                def turn_sums(s, k):
                    pe.wait_ge(agg_st, k)
                    a = b["aggS"][s]
                    pe.transpose(bank[0:96, 2 * s + 1, 0:P], a[:, 64:160], ident)
                    pe.transpose(bank[0:64, 2 * s, 0:P], a[:, 0:64], ident)
                    if L == 2:
                        for m in range(3):
                            pe.transpose(bank[0:64, 2 * s, P * (m + 1):P * (m + 2)], a[:, 256 + 160 * m:320 + 160 * m], ident)
                    for m in range(3):
                        ins = pe.transpose(bank[0:96, 2 * s + 1, P * (m + 1):P * (m + 2)], a[:, 160 + mw * m:256 + mw * m], ident)
                    ins.then_inc(agg_T, 1)

                def outputs(s, k, kfree):
                    pe.wait_ge(aggA_sb, k)
                    pe.wait_ge(aggB_sb, k)
                    pe.wait_ge(node_x, kfree)
                    o = bank[:, 4 + s, 0:c["nout"]]
                    A, Bt = b["aTA"][s], b["aTB"][s]
                    for m in range(3):
                        pe.matmul(o, Bt[0:96, 1 + m, :], b["om"][0:96, m, :], start=m == 0, stop=False, skip_group_check=True)
                    sv = [(0, 64), (160, 224)] if L == 1 else [(0, 96)] if L == 2 else [(0, 65)]
                    for o0, o1 in sv:
                        pe.matmul(o[:, o0:o1], A[0:64, 0, :], b["oa"][0:64, o0:o1], start=False, stop=True, skip_group_check=True)
                    vv = [(64, 160), (224, 320)] if L == 1 else [(96, 192)] if L == 2 else [(65, 161)]
                    if L == 2:
                        for m in range(3):
                            pe.matmul(o[:, 96:192], A[0:64, 1 + m, :], b["oc"][0:64, m, 96:192], start=False, stop=False, skip_group_check=True)
                    for o0, o1 in vv:
                        ins = pe.matmul(o[:, o0:o1], Bt[0:96, 0, :], b["ob"][0:96, o0:o1], start=False, stop=True, skip_group_check=True)
                    ins.then_inc(o_ready, 1)

                turn_sums(0, NB + 1)
                with pe.Fori(0, NT // 2) as i:
                    for s in range(2):
                        turn_sums(1 - s, i * 2 + (NB + s + 2))
                        outputs(s, i * 2 + (NB + s + 1), i * 2 + (NB + s + 1))
                outputs(0, NB + NT, NB + NT)
                stage(pe, stage_of(L, 4))

        @block.vector
        def _(dve):
            step = Count(dve_step)

            def then(ins):
                step.up(ins)
                dve.wait_ge(dve_step, step.n)

            dve.sem_inc(x_ready, 8)
            dve.sem_inc(copies_done, 8)
            dve.sem_inc(prod_free, 4)
            dve.sem_inc(summed, 2)
            dve.sem_inc(u_ready, 2)
            dve.sem_inc(node_x, 2)
            dve.sem_inc(payload_ready, 2)
            dve.memset(eps, 1e-5)
            dve.memset(ones_e[0:EP, :], 1.0)
            dve.memset(slot_d[0:EP, :], 0.0)
            then(dve.memset(slot_s[0:EP, :], 0.0))
            dve.wait_ge(const_in, 16)
            dve.wait_ge(idx_in, 32)
            bval = lambda k: const[0:EP, bass.ds(NC_BUCKET + k, 1)]
            for o, (idx, slot, addr, low) in enumerate(((idx_d, slot_d, addr_d, low_d), (idx_s, slot_s, addr_s, low_s))):
                dve.tensor_scalar(itmp[0][0:EP, :], idx[0:EP, :], 7, None, ALU.arith_shift_right)
                then(dve.tensor_scalar(itmp[1][0:EP, :], idx[0:EP, :], 127, None, ALU.bitwise_and))
                dve.tensor_copy(bucket[0:EP, :], itmp[0][0:EP, :])
                then(dve.tensor_scalar(low[0:EP, :], itmp[1][0:EP, :], 1.0, None, ALU.add))
                n0 = step.n
                with dve.Fori(0, NT) as k:
                    dve.wait_ge(dve_step, k + n0)
                    dve.tensor_scalar(onehot_b[0:EP, :], bucket[0:EP, :], bval(k), 0.0, ALU.is_equal, ALU.add,
                                      accum_out=totals[0:EP, bass.ds(k, 1)]).then_inc(dve_step, 1)
                step.n += NT
                dve.wait_ge(dve_step, step.n)
                dve.drain().then_inc(totals_done, 1)
                dve.wait_ge(offsets_done, o + 1)
                then(dve.tensor_scalar(cnt_i, bank[:, 1, 0:NT], 255.0, None, ALU.add))
                then(dve.tensor_scalar(cnt_i, cnt_i, 8, None, ALU.arith_shift_right))
                then(dve.tensor_copy(cnt_f, cnt_i))
                then(dve.tensor_tensor_scan(tend, ones[:, 0:NT], cnt_f, 0.0, ALU.mult, ALU.add))
                then(dve.tensor_tensor(basef, tend, cnt_f, ALU.subtract))
                then(dve.tensor_scalar(basef, basef, 256.0, -1.0, ALU.mult, ALU.add))
                then(dve.tensor_tensor(offs[0:EP, :], bank[0:EP, 0, 0:NT], basef[0:EP, :], ALU.add))
                for j in range(STEPC):
                    then(dve.tensor_scalar(step_cmp, tend, const[:, NC_STEP + j:NC_STEP + j + 1], 0.0, ALU.is_le, ALU.add,
                                           accum_out=step_f[:, j:j + 1]))
                if o == 1:
                    dve.wait_ge(step_out, 16)
                then(dve.tensor_scalar(step_i, step_f, float(NT - 1), None, ALU.min))
                dve.drain().then_inc(table_done, 1)
                n0 = step.n
                with dve.Fori(0, NT) as k:
                    dve.wait_ge(dve_step, k * 4 + n0)
                    dve.tensor_scalar(onehot_b[0:EP, :], bucket[0:EP, :], bval(k), None, ALU.is_equal).then_inc(dve_step, 1)
                    dve.wait_ge(dve_step, k * 4 + (n0 + 1))
                    dve.tensor_tensor_scan(scan_b[0:EP, :], ones_e[0:EP, :], onehot_b[0:EP, :], offs[0:EP, bass.ds(k, 1)],
                                           ALU.mult, ALU.add).then_inc(dve_step, 1)
                    dve.wait_ge(dve_step, k * 4 + (n0 + 2))
                    dve.tensor_tensor(scan_b[0:EP, :], scan_b[0:EP, :], onehot_b[0:EP, :], ALU.mult).then_inc(dve_step, 1)
                    dve.wait_ge(dve_step, k * 4 + (n0 + 3))
                    dve.tensor_tensor(slot[0:EP, :], slot[0:EP, :], scan_b[0:EP, :], ALU.add).then_inc(dve_step, 1)
                step.n += 4 * NT
                dve.wait_ge(dve_step, step.n)
                s_i, hi_i, mid_i = (t[0:EP, :] for t in itmp)
                then(dve.tensor_copy(s_i, slot[0:EP, :]))
                dve.tensor_scalar(hi_i, s_i, -512, None, ALU.bitwise_and)
                dve.tensor_scalar(mid_i, s_i, 127, 2, ALU.bitwise_and, ALU.logical_shift_left)
                then(dve.tensor_scalar(addr[0:EP, :], s_i, 7, 3, ALU.arith_shift_right, ALU.bitwise_and))
                then(dve.tensor_tensor(hi_i, hi_i, mid_i, ALU.add))
                then(dve.tensor_tensor(addr[0:EP, :], addr[0:EP, :], hi_i, ALU.add))
            stage(dve, 1)

            for o in range(2):
                idx, addr, low = ((idx_s, addr_d, low_d), (idx_d, addr_s, low_s))[o]
                r = (ROW_D, ROW_S)[o]
                pay = (pay_d, pay_s)[o]
                def fill(i, s):
                    k = i * 2 + s
                    cols = slice(k * CC, k * CC + CC) if isinstance(k, int) else bass.ds(k * CC, CC)
                    dve.wait_ge(stage_in[s], i * (64, 32)[o] + (64 * (CHUNKS // 2) * o + (64, 32)[o]))
                    pay_ = pay[s][0:EP, :, :]
                    if o == 1:
                        dve.tensor_tensor(sq3[s][0:EP, :, :], st3[s][0:EP, :, :], st3[s][0:EP, :, :], ALU.mult).then_inc(dve_step, 1)
                        dve.wait_ge(dve_step, i * 4 + (step.n + 2 * s + 1))
                        dve.tensor_reduce(norm[s][0:EP, 0, :], sq3[s][0:EP, :, :], AX_X, ALU.add).then_inc(norm_ss, 1)
                    if o or not isinstance(i, int):
                        dve.wait_ge(scattered[s], i * (16 * CC) + 16 * CC * (CHUNKS // 2) * o)
                    dve.tensor_copy(adr[s][0:EP, :], addr[0:EP, cols])
                    dve.tensor_copy(pay_[:, :, r["idx"]:r["idx"] + 1].bitcast(I32), idx[0:EP, cols].rearrange("p (c o) -> p c o", o=1))
                    dve.tensor_copy(pay_[:, :, r["dl"]:r["dl"] + 1], low[0:EP, cols].rearrange("p (c o) -> p c o", o=1))
                    if o == 0:
                        dve.tensor_copy(pay_[:, :, r["a16"]:r["a16"] + 16], st16[s][0:EP, :, :])
                        dve.tensor_copy(pay_[:, :, r["a10"]:r["a10"] + 10], st10[s][0:EP, :, :])
                        dve.tensor_copy(pay_[:, :, r["a8"]:r["a8"] + 8], st8[s][0:EP, :, :])
                        dve.tensor_copy(pay_[:, :, r["sh"]:r["sh"] + 4], st4[s][0:EP, :, :]).then_inc(payload_ready, 1)
                    else:
                        dve.tensor_copy(pay_[:, :, 0:64], st64[s][0:EP, :, :])
                        dve.wait_ge(norm_root, i * 2 + (s + 1))
                        dve.reciprocal(norm[s][0:EP, 2, :], norm[s][0:EP, 1, :]).then_inc(dve_step, 1)
                        dve.wait_ge(dve_step, i * 4 + (step.n + 2 * s + 2))
                        dve.tensor_tensor(pay_[:, :, 64:67], st3[s][0:EP, :, :],
                                          norm[s][0:EP, 2, :].rearrange("p (c o) -> p c o", o=1).to_broadcast([EP, CC, 3]), ALU.mult).then_inc(payload_ready, 1)
                for s in range(2):
                    fill(0, s)
                with dve.Fori(0, CHUNKS // 2 - 1) as i:
                    for s in range(2):
                        fill(i + 1, s)
                step.n += 2 * CHUNKS * o
                stage(dve, 2 + o)

            for L, c in enumerate(LAYERS):
                b = B[L]
                mw, xw, wn = c["mw"], c["xw"], c["wn"]
                if L == 0:
                    dve.tensor_tensor(attr_sq, nv[:, 0, :], nv[:, 0, :], ALU.mult)
                    dve.tensor_tensor(attr_mask[:, 0, :], nv[:, 0, :], nv[:, 2, :], ALU.mult)
                    dve.tensor_tensor(attr_mask[:, 1, :], nv[:, 1, :], nv[:, 2, :], ALU.mult)
                dve.wait_ge(weights_in, loads_to[L])
                lo, hi = b["ws"][:, 0, :], b["ws"][:, 1, :]

                def scaled(dst, src, f):
                    dve.tensor_scalar(dst, src, float(f), None, ALU.mult)

                def comps(dst, src, f, m=None):
                    d = dst.rearrange("p (v m) -> p m v", m=3)
                    if m is None:
                        dve.tensor_scalar(d, src.rearrange("p (m v) -> p m v", m=3), float(f), None, ALU.mult)
                    else:
                        dve.tensor_scalar(d[:, m, :], src, float(f), None, ALU.mult)

                r3 = 3.0 ** -0.5
                if L in (0, 3):
                    i0, i1, i9 = 64.0 ** -0.5, 32.0 ** -0.5, 96.0 ** -0.5
                    g9 = i9 * (1.0 if L == 0 else 32.0 ** -0.5)
                    scaled(b["ps"][0:64, 0:128], lo[0:64, 0:128], i0)
                    scaled(b["pv"][0:96, 0:96], hi[0:96, 0:96], i1)
                    comps(b["pv"][0:96, 96:192], hi[0:96, 96:192], i1)
                    for g in range(2):
                        scaled(b["w2"][64 * g:64 * g + 64, 192 * g:192 * g + 192], hi[64 * g:64 * g + 64, 192:384], 0.125)
                    scaled(b["oa"][0:64, 1:65], lo[0:64, 128:192], g9)
                    scaled(b["oa"][0:64, 0:1], lo[0:64, 192:193], g9)
                    for m in range(3):
                        comps(b["ob"][32 * m:32 * m + 32, 65:161], lo[32 * m:32 * m + 32, 225:257], g9, m)
                        comps(b["om"][0:64, m, 65:161], lo[0:64, 193:225], g9, m)
                        scaled(b["om"][64:96, m, 1:65], lo[64:96, 128:192], g9 * r3)
                        scaled(b["om"][64:96, m, 0:1], lo[64:96, 192:193], g9 * r3)
                if L == 1:
                    import math
                    cs, cx = math.sin(math.pi / 8), math.cos(math.pi / 8)
                    for a in range(2):
                        scaled(b["ps"][0:64, 128 * a:128 * a + 64], lo[0:64, 128 * a:128 * a + 64], 1.0)
                        scaled(b["ps"][0:64, 128 * a + 64:128 * a + 128], lo[0:64, 128 * a + 64:128 * a + 128], cs)
                        scaled(b["pv"][0:96, 192 * a:192 * a + 96], hi[0:96, 192 * a:192 * a + 96], 1.0)
                        comps(b["pv"][0:96, 192 * a + 96:192 * a + 192], hi[0:96, 192 * a + 96:192 * a + 192], cs)
                    dve.wait_ge(offsets_done, 3)
                    dve.tensor_copy(lo[0:96, 256:640], bank[0:96, 0, 0:384]).then_inc(totals_done, 1)
                    dve.wait_ge(offsets_done, 4)
                    g = cx / 4.0
                    for a in range(2):
                        o0 = 160 * a
                        scaled(b["oa"][0:64, o0:o0 + 64], bank[0:64, 1, 64 * a:64 * a + 64], g)
                        for m in range(3):
                            comps(b["ob"][32 * m:32 * m + 32, o0 + 64:o0 + 160], bank[32 * m:32 * m + 32, 2, 32 * a:32 * a + 32], g, m)
                            comps(b["om"][0:64, m, o0 + 64:o0 + 160], bank[0:64, 1, 128 + 64 * a:160 + 64 * a], g, m)
                            scaled(b["om"][64:96, m, o0:o0 + 64], bank[64:96, 1, 64 * a:64 * a + 64], g * r3)
                if L == 2:
                    g, s3 = 1.0 / 32.0, 3.0 ** 0.5
                    scaled(b["ps"][0:64, 0:160], lo[0:64, 0:160], 1.0)
                    scaled(b["pv"][0:96, 0:96], hi[0:96, 0:96], 1.0)
                    comps(b["pv"][0:96, 96:192], hi[0:96, 96:192], 1.0)
                    scaled(b["oa"][0:64, 0:96], lo[0:64, 160:256], g)
                    for m in range(3):
                        comps(b["ob"][32 * m:32 * m + 32, 96:192], lo[32 * m:32 * m + 32, 288:320], g, m)
                        comps(b["om"][0:64, m, 96:192], lo[0:64, 256:288], g * s3, m)
                        scaled(b["om"][64:96, m, 0:96], lo[64:96, 160:256], g)
                        for q, comp in enumerate([k for k in range(3) if k != m]):
                            sign, to = (1.0, (m + 1) % 3) if comp == (m + 2) % 3 else (-1.0, (m + 2) % 3)
                            comps(b["oc"][32 * q:32 * q + 32, m, 96:192], lo[32 * q:32 * q + 32, 320:352], sign * g * s3 * 2.0 ** -0.5, to)
                stage(dve, stage_of(L, 0))

                sq = arena[:, b["agg_off"]:b["agg_off"] + NT * D]
                sq3d = sq.rearrange("p (t d) -> p t d", d=D)
                then(dve.tensor_reduce(ln_sum, x, AX_X, ALU.add))
                then(dve.tensor_scalar(ln_mean, ln_sum, -1.0 / D, None, ALU.mult))
                mean_b = ln_mean.rearrange("p (t o) -> p t o", o=1).to_broadcast([P, NT, D])
                dve.tensor_tensor(sq3d, x, mean_b, ALU.add).then_inc(ln_a, 1)
                dve.wait_ge(ln_b, 2 * L + 1)
                dve.tensor_reduce(ln_sq, sq3d, AX_X, ALU.add).then_inc(ln_a, 1)
                dve.wait_ge(ln_b, 2 * L + 2)
                then(dve.reciprocal(ln_rstd, ln_rstd))
                dve.tensor_tensor(ln_bias, ln_mean, ln_rstd, ALU.mult)
                stage(dve, stage_of(L, 1))

                NB = NT * L

                def evacuate(s, k):
                    dve.wait_ge(hT_ready, k + 2)
                    dve.tensor_copy(b["hTs"][s][0:64, :], bank[0:64, s, 0:P])
                    dve.tensor_copy(b["hTv"][s][0:96, :], bank[0:96, s, P:2 * P]).then_inc(hT_sb, 1)

                def finish(t, s, k, kout, ks):
                    dve.wait_ge(f_ready, k)
                    if kout is not None:
                        dve.wait_ge(table_out[s], kout)
                    u, f = b["u"][s], bank[:, 4 + 2 * s, :]
                    if L == 1:
                        dve.wait_ge(f_tmp, ks)
                        dve.scalar_tensor_tensor(out=u[:, 0:320], in0=f[:, 0:320], scalar=arena_col(nv_off, t), in1=b["utmp"][s],
                                                 op0=ALU.mult, op1=ALU.add).then_inc(u_ready, 1)
                    elif L == 2:
                        dve.tensor_copy(u[:, 0:352], f[:, 0:352]).then_inc(u_ready, 1)
                    else:
                        dve.tensor_scalar(u[:, 0:320], f[:, 0:320], arena_col(nv_off, t), None, ALU.mult).then_inc(u_ready, 1)
                    if L != 2:
                        dve.wait_ge(u_ready, k + 2)
                        dve.tensor_tensor(x_tile(t), x_tile(t), u[:, 160:320], ALU.add)

                per = 32 if L == 2 else 16
                evacuate(0, NB + 1)
                for t in range(2):
                    evacuate(1 - t % 2, NB + t + 2)
                    finish(t, t % 2, NB + t + 1, out_count(L, t % 2) if L else None, t + 1)
                with dve.Fori(0, NT // 2 - 1) as i:
                    for s in range(2):
                        evacuate(1 - s, i * 2 + (NB + s + 4))
                        finish(i * 2 + (s + 2), s, i * 2 + (NB + s + 3), i * per + (out_count(L, s) + per), i * 2 + (s + 3))
                finish(NT - 1, 0, NB + NT, out_count(L, 0) + per * (NT // 2), NT)
                stage(dve, stage_of(L, 2))

                QB, PB = (QUADS + 2) * L, (PAIRS + 1) * L
                rw = c["rows"]

                def products(rp, q, gs, s, k_gath, k_w):
                    dve.wait_ge(gath_in[gs], k_gath)
                    dve.wait_ge(w_ready, k_w)
                    X, G = b["X"][s], b["gath"][gs]
                    W = bank[:, 2 + s, 0:2 * wn].rearrange("p (g w) -> p g w", w=wn)
                    rows, Sx = b["rows"][q][:, 2 * rp:2 * rp + 2, :], b["S"][s]
                    plain = 0 if L == 2 else 4
                    dve.tensor_tensor(Sx[:, :, plain, :], iota.unsqueeze(1).to_broadcast([P, 2, P]),
                                      rows[:, :, rw["dl"]:rw["dl"] + 1].to_broadcast([P, 2, P]), ALU.is_equal).then_inc(onehot_ready, 1)
                    dve.tensor_tensor(X[:, :, 0:320].rearrange("p g (k w) -> p g k w", k=2)[:, :, :, 0:64],
                                      W[:, :, 0:128].rearrange("p g (k w) -> p g k w", k=2),
                                      G[:, :, 0:64].unsqueeze(2).to_broadcast([P, 2, 2, 64]), ALU.mult).then_inc(first_products, 1)
                    e1 = G[:, :, 64:160]
                    wb = lambda o, n: W[:, :, o:o + 32].unsqueeze(2).to_broadcast([P, 2, n, 32])
                    e1m = e1.rearrange("p g (m v) -> p g m v", m=3)
                    dve.tensor_tensor(X[:, :, 64:160].rearrange("p g (m v) -> p g m v", m=3), wb(128, 3), e1m, ALU.mult)
                    Xm = X[:, :, 160:160 + 3 * mw].rearrange("p g (m w) -> p g m w", m=3)
                    ins = dve.tensor_tensor(Xm[:, :, :, 64:96], wb(160, 3), e1m, ALU.mult)
                    if L == 2:
                        for m, (c0, stp) in enumerate(((1, 1), (0, 2), (0, 1))):
                            ins = dve.tensor_tensor(Xm[:, :, m, 96:160].rearrange("p g (a v) -> p g a v", a=2), wb(192, 2),
                                                    e1m[:, :, c0:c0 + stp + 1:stp, :], ALU.mult)
                    ins.then_inc(prod_free, 1)
                    n, k0 = (1, 1) if L == 2 else (2, 0)
                    dve.wait_ge(onehot_ready, k_w)
                    dve.tensor_tensor(Sx[:, :, k0:k0 + n, :], Sx[:, :, plain:plain + 1, :].to_broadcast([P, 2, n, P]),
                                      rows[:, :, rw["sh"]:rw["sh"] + n].unsqueeze(3).to_broadcast([P, 2, n, P]), ALU.mult).then_inc(x_ready, 1)

                def add(s, tile, k_sums, k_prev):
                    dve.wait_ge(sums_ready, k_sums)
                    dve.wait_ge(summed, k_prev)
                    a = agg_tile(L, tile)
                    if L == 2:
                        a = a.rearrange("p (h w) -> p h w", h=2)
                        sm = bank[:, 4 + 2 * s:6 + 2 * s, 0:320]
                    else:
                        sm = bank[:, 4 + 2 * s, 0:c["aw"]]
                    dve.tensor_tensor(a, a, sm, ALU.add).then_inc(summed, 1)

                brow = bucket_rows[1 if L == 2 else 0]
                products(0, 0, 0, 0, 32 * (gath_base(L, 0) + 1), PB + 1)
                with dve.Fori(0, ITERS) as i:
                    for r in range(8):
                        n = r + 1
                        products(n % 2, (n // 2) % 4, n % 4, n % 2,
                                 i * 64 + 32 * (gath_base(L, n % 4) + 1 + n // 4), i * 8 + (PB + n + 1))
                        tile = dve.value_load(brow[0:1, bass.ds(i * 8 + r, 1)], min_val=0, max_val=NT - 1)
                        add(r % 2, tile, i * 8 + (PAIRS * L + r + 1), i * 8 + (PAIRS * L + r + 2))
                stage(dve, stage_of(L, 3))

                if L == 0:
                    counts = b["agg"][:, :, 448]
                    then(dve.tensor_scalar(recip_count, counts, 1.0, None, ALU.max))
                    dve.reciprocal(recip_count, recip_count).then_inc(counts_ready, 1)

                n0 = step.n

                def chunkB(s, k):
                    dve.wait_ge(agg_T, k + 2)
                    dve.tensor_copy(b["aTB"][s][0:96, :, :], bank[0:96, 2 * s + 1, :].rearrange("p (a b) -> p a b", b=P)).then_inc(aggB_sb, 1)

                def result(t, s, k, ks, kk, k_skip):
                    dve.wait_ge(o_ready, k)
                    o, u = bank[:, 4 + s, :], b["u"][s]
                    xt = x_tile(t)
                    if L in (0, 3):
                        sc = b["scal"][s][:, 0:1]
                        dve.tensor_scalar(sc, o[:, 0:1], arena_col(sq_off, t), None, ALU.mult).then_inc(dve_step, 1)
                        dve.wait_ge(dve_step, ks)
                        dve.scalar_tensor_tensor(out=xt, in0=o[:, 1:161], scalar=sc, in1=xt, op0=ALU.mult, op1=ALU.add).then_inc(node_x, 1)
                    if L == 1:
                        dve.wait_ge(o_tmp, kk)
                        dve.scalar_tensor_tensor(out=u[:, 0:160], in0=o[:, 0:160], scalar=arena_col(mask_off, t), in1=b["utmp"][s][:, 0:160],
                                                 op0=ALU.mult, op1=ALU.add).then_inc(dve_step, 1)
                        dve.wait_ge(dve_step, ks)
                        dve.tensor_tensor(xt, xt, u[:, 0:160], ALU.add).then_inc(node_x, 1)
                    if L == 2:
                        dve.wait_ge(skip_in[s], k_skip)
                        dve.tensor_tensor(u[:, 0:192], o[:, 0:192], b["sk"][s], ALU.add).then_inc(o_y, 1)
                        dve.wait_ge(o_gate, kk)
                        gt = b["utmp"][s]
                        dve.tensor_tensor(u[:, 192:256], u[:, 0:64], gt[:, 0:64], ALU.mult)
                        dve.tensor_tensor(u[:, 256:352].rearrange("p (v m) -> p v m", m=3), u[:, 96:192].rearrange("p (v m) -> p v m", m=3),
                                          gt[:, 64:96].unsqueeze(2).to_broadcast([P, 32, 3]), ALU.mult).then_inc(dve_step, 1)
                        dve.wait_ge(dve_step, ks)
                        dve.tensor_tensor(xt, xt, u[:, 192:352], ALU.add).then_inc(node_x, 1)

                chunkB(0, NB + 1)
                with dve.Fori(0, NT // 2) as i:
                    for s in range(2):
                        chunkB(1 - s, i * 2 + (NB + s + 2))
                        result(i * 2 + s, s, i * 2 + (NB + s + 1), i * 2 + (n0 + s + 1), i * 2 + (s + 1), i * 16 + 16)
                result(NT - 1, 0, NB + NT, n0 + NT, NT, 16 * (NT // 2 + 1))
                step.n += NT
                stage(dve, stage_of(L, 4))


def kernel(**inputs):
    import numpy as _np
    import concourse.bacc as _bacc
    from concourse import mybir as _mybir
    from concourse.bass_utils import run_bass_kernel_spmd as _run

    nc = _bacc.Bacc("TRN2", target_bir_lowering=False, num_devices=1)
    arrays, aps = {}, {}
    host = dict(inputs)
    host["consts"] = shape_constants()
    for name, value in host.items():
        a = _np.ascontiguousarray(value)
        arrays[f"in_{name}_dram"] = a
        aps[name] = nc.dram_tensor(f"in_{name}_dram", a.shape, _mybir.dt.from_np(a.dtype), kind="ExternalInput").ap()
    out = nc.dram_tensor("out_0_dram", (N, D), F32, kind="ExternalOutput").ap()
    gnn_kernel(nc, aps, out)
    r = _run(nc, [arrays], core_ids=[0])
    return r.results[0]["out_0_dram"]
```

```python
from contextlib import ExitStack

import concourse.bass as bass
from concourse import mybir

ALU = mybir.AluOpType
ACT = mybir.ActivationFunctionType
F32 = mybir.dt.float32
I32 = mybir.dt.int32
I16 = mybir.dt.int16
AX_X = mybir.AxisListType.X

N, E, D = 6250, 100000, 160
S, V = 64, 32
P = 128
NT = -(-N // P)
NREST = N - (NT - 1) * P
EP = 125
EC = E // EP
PAIRS = -(-((E + NT * 255) // 256) // 8) * 8
QUADS = PAIRS // 2
ITERS = PAIRS // 8
SLOTS = (QUADS + 2) * 512
CC = 25
CHUNKS = EC // CC
HC = 4
MOVING = EC // (2 * 2 * HC)
BIG = 640

ROW_D = dict(w=40, a16=0, a10=16, a8=26, sh=34, dl=38, idx=39)
ROW_S = dict(w=69, a64=0, sh=64, dl=67, idx=68)
LAYERS = [
    dict(aw=385, xw=450, mw=96, kin=16, col=ROW_D["a16"], hid=64, wn=192, rows=ROW_D, nout=161, ncat=320),
    dict(aw=384, xw=450, mw=96, kin=10, col=ROW_D["a10"], hid=100, wn=192, rows=ROW_D, nout=320, ncat=640),
    dict(aw=640, xw=640, mw=160, kin=64, col=ROW_S["a64"], hid=64, wn=224, rows=ROW_S, nout=192, ncat=352),
    dict(aw=384, xw=450, mw=96, kin=8, col=ROW_D["a8"], hid=64, wn=192, rows=ROW_D, nout=161, ncat=320),
]
VM0, COUNT, W1E0 = 96, 384, 386
PAIR_STEP = ROW_D["w"]
PAIR_ROWS = PAIR_STEP + ROW_D["sh"]
NC_IDENT, NC_TRI, NC_IOTA, NC_ONES, NC_BUCKET, NC_STEP = 0, 128, 256, 384, 512, 512 + NT
STEPC = -(-PAIRS // P)
NCONST = NC_STEP + STEPC


def shape_constants():
    import numpy as np

    c = np.zeros((P, NCONST), np.float32)
    c[:, NC_IDENT:NC_IDENT + P] = np.eye(P)
    c[:, NC_TRI:NC_TRI + P] = np.triu(np.ones((P, P)), 1)
    c[:, NC_IOTA:NC_IOTA + P] = np.arange(1, P + 1)
    c[:, NC_ONES:NC_ONES + P] = 1.0
    c[:, NC_BUCKET:NC_BUCKET + NT] = np.arange(NT)
    c[:, NC_STEP:] = np.arange(STEPC)[None, :] * P + np.arange(P)[:, None]
    return c


def gnn_kernel(nc, A, out):
    with ExitStack() as ctx:
        sem = lambda name: ctx.enter_context(nc.semaphore(name))

        rows_d = nc.dram_tensor("rows_by_dst", (SLOTS, ROW_D["w"]), F32).ap()
        rows_s = nc.dram_tensor("rows_by_src", (SLOTS, ROW_S["w"]), F32).ap()
        table = nc.dram_tensor("node_table", (NT * P, D), F32).ap()
        skip_dram = nc.dram_tensor("node_skip", (NT * P, 192), F32).ap()
        bucket_dram = nc.dram_tensor("bucket_of_pair", (2, STEPC * P), I16).ap()

        TOTAL = 51900
        arena = ctx.enter_context(nc.sbuf_tensor("arena", [P, TOTAL], F32))
        top = [0]

        def cut(*shape):
            n = 1
            for s in shape:
                n *= s
            off = top[0]
            top[0] += n
            assert top[0] <= TOTAL, (top[0], TOTAL)
            v = arena[:, off:off + n]
            if len(shape) == 2:
                v = v.rearrange("p (a b) -> p a b", b=shape[1])
            elif len(shape) == 3:
                v = v.rearrange("p (a b c) -> p a b c", b=shape[1], c=shape[2])
            elif len(shape) == 4:
                v = v.rearrange("p (a b c d) -> p a b c d", b=shape[1], c=shape[2], d=shape[3])
            return v

        const = cut(NCONST)
        ident = const[:, NC_IDENT:NC_IDENT + P]
        tri = const[:, NC_TRI:NC_TRI + P]
        iota = const[:, NC_IOTA:NC_IOTA + P]
        ones = const[:, NC_ONES:NC_ONES + P]
        X0 = top[0]
        x = cut(NT, D)
        nv = cut(3, NT)
        recip_count = cut(NT)
        attr_sq = cut(NT)
        attr_mask = cut(2, NT)
        ln_sum, ln_mean, ln_sq, ln_rstd, ln_bias = (cut(NT) for _ in range(5))
        eps = cut(1)
        bucket_rows = [cut(STEPC * P // 2).bitcast(I16) for _ in range(2)]
        layer_base = top[0]

        idx_d, idx_s = cut(EC).bitcast(I32), cut(EC).bitcast(I32)
        slot_d, slot_s = cut(EC), cut(EC)
        addr_d, addr_s = cut(EC).bitcast(I32), cut(EC).bitcast(I32)
        low_d, low_s = cut(EC), cut(EC)
        vec, vec_sq = cut(EC, 3), cut(EC, 3)
        vec_norm = cut(3, EC)
        bucket = cut(EC)
        itmp = [cut(EC).bitcast(I32) for _ in range(3)]
        onehot_b, scan_b, ones_e = cut(EC), cut(EC), cut(EC)
        totals, offs, cnt_f, tend, basef = (cut(NT) for _ in range(5))
        cnt_i = cut(NT).bitcast(I32)
        step_cmp, step_f = cut(NT), cut(STEPC)
        step_i = cut(STEPC).bitcast(I16)[:, 0:STEPC]
        zrow = cut(P * 16)
        st16, st10, st8, st4 = ([cut(CC, w) for _ in range(2)] for w in (16, 10, 8, 4))
        pay_d = [cut(CC, ROW_D["w"]) for _ in range(2)]
        adr = [cut(CC).bitcast(I32) for _ in range(2)]
        sort_top = top[0]

        edge_f = (EC + HC) * 4
        keep = edge_f + (EC + HC) * 2 + 2 * HC * (ROW_S["w"] + 1)
        top[0] = TOTAL - keep
        KEPT = top[0]
        tail_f = cut(EC + HC, 4)
        tail_i = cut(EC + HC, 2).bitcast(I32)
        pay_s = [cut(HC, ROW_S["w"] + 1) for _ in range(2)]
        assert sort_top <= KEPT

        B = []
        for L, c in enumerate(LAYERS):
            top[0] = layer_base
            b = {}
            b["agg_off"] = top[0]
            b["agg"] = cut(NT, c["aw"])
            b["w1"] = {0: lambda: cut(128), 1: lambda: cut(2, 100), 2: lambda: cut(64), 3: lambda: cut(128)}[L]()
            b["w2"] = cut(c["wn"] if L == 1 else 2 * c["wn"])
            if L == 3:
                b["wmid"] = cut(128)
            b["ps"] = cut(256 if L == 1 else 160)
            b["pv"] = cut(384 if L == 1 else 192)
            b["oa"] = cut(c["nout"])
            b["om"] = cut(3, c["nout"])
            if L == 2:
                b["ob"] = cut(c["nout"])
                b["oc"] = cut(3, c["nout"])
            rings = top[0]
            b["rows"] = [cut(4, c["rows"]["w"]) for _ in range(4)]
            b["gath"] = [cut(2, D) for _ in range(4)]
            b["X"] = [cut(2, c["xw"]) for _ in range(2)]
            b["S"] = [cut(2, 4 if L == 2 else 1, P) for _ in range(2)]
            if L != 2:
                b["E0"] = [cut(2, D) for _ in range(4)]
                b["esh"] = [cut(2, 3, V) for _ in range(2)]
                b["dot"] = [cut(2, V) for _ in range(2)]
            b["tT"] = [cut(4 if L == 2 else 2, P) for _ in range(2)]
            b["hT"] = [cut(4 if L == 1 else 2, P) for _ in range(2)]
            if L == 3:
                b["h1T"] = [cut(2, P) for _ in range(2)]
            top[0] = rings
            b["h"] = [cut(D) for _ in range(2)]
            b["hTs"] = [cut(P) for _ in range(2)]
            b["hTv"] = [cut(P) for _ in range(2)]
            b["u"] = [cut(352) for _ in range(2)]
            b["utmp"] = [cut(320) for _ in range(2)]
            b["sk"] = [cut(192) for _ in range(2)]
            b["scal"] = [cut(8) for _ in range(2)]
            top[0] = rings
            b["_pad"] = cut(2 * D + 4 * P + 2 * 352 + 2 * 320 + 2 * 192 + 16)
            b["aggS"] = [cut(c["aw"]) for _ in range(2)]
            if L == 2:
                b["aTA"] = [cut(4, P) for _ in range(2)]
            b["aTB"] = [cut(4, P) for _ in range(2)]
            if L in (0, 1, 3):
                top[0] = max(top[0], rings + 8000)
            b["ws"] = cut(2, 640) if L != 2 else None
            assert L > 1 or top[0] <= KEPT
            B.append(b)
        B[2]["ws"] = arena[:, B[2]["agg_off"] + 20000:B[2]["agg_off"] + 21280].rearrange("p (a b) -> p a b", b=640)

        bank = ctx.enter_context(nc.psum_tensor("bank", [P, 8, 512], F32))

        stage_end = sem("stage_end")
        const_in = sem("const_in")
        idx_in, ones_set, zero_set = sem("idx_in"), sem("ones_set"), sem("zero_set")
        x_in = sem("x_in")
        weights_in = sem("weights_in")
        prefilled = sem("prefilled")
        dve_step, act_step = sem("dve_step"), sem("act_step")
        totals_done, offsets_done = sem("totals_done"), sem("offsets_done")
        step_out, step_in = sem("step_out"), sem("step_in")
        table_done = sem("table_done")
        stage_in = [sem(f"stage_in{i}") for i in range(2)]
        payload_ready = sem("payload_ready")
        vec_in, vec_squared, vec_summed, vec_root = sem("vec_in"), sem("vec_squared"), sem("vec_summed"), sem("vec_root")
        attr64_in = [sem(f"attr64_in{i}") for i in range(2)]
        tail_ready = [sem(f"tail_ready{i}") for i in range(2)]
        sent = [sem(f"sent{i}") for i in range(2)]
        scattered = [sem(f"scattered{i}") for i in range(2)]
        counts_ready = sem("counts_ready")
        pool_steps = sem("pool_steps")
        rows_in = [sem(f"rows_in{i}") for i in range(4)]
        gath_in = [sem(f"gath_in{i}") for i in range(4)]
        prod_free = sem("prod_free")
        turned, turned_sb, hidden1, hidden1_sb, hidden2, hidden_sb = (
            sem(n) for n in ("turned", "turned_sb", "hidden1", "hidden1_sb", "hidden2", "hidden_sb"))
        onehot_ready = sem("onehot_ready")
        e_scaled, dot_step = sem("e_scaled"), sem("dot_step")
        w_ready, first_products, copies_done, x_ready = sem("w_ready"), sem("first_products"), sem("copies_done"), sem("x_ready")
        sums_ready, summed = sem("sums_ready"), sem("summed")
        ln_a, ln_b = sem("ln_a"), sem("ln_b")
        h_ready, hT_ready, hT_sb, f_ready, f_tmp, u_ready, node_x = (
            sem(n) for n in ("h_ready", "hT_ready", "hT_sb", "f_ready", "f_tmp", "u_ready", "node_x"))
        table_out = [sem(f"table_out{i}") for i in range(2)]
        agg_zero = sem("agg_zero")
        agg_st, agg_T, aggA_sb, aggB_sb, o_ready, o_tmp, o_gate, o_y = (
            sem(n) for n in ("agg_st", "agg_T", "aggA_sb", "aggB_sb", "o_ready", "o_tmp", "o_gate", "o_y"))
        skip_in = [sem(f"skip_in{i}") for i in range(2)]
        out_done = sem("out_done")

        block = ctx.enter_context(nc.Block())
        ENGINES = 5

        def stage(e, n):
            e.drain().then_inc(stage_end, 1)
            e.wait_ge(stage_end, ENGINES * n)

        class Count:

            def __init__(self, s):
                self.s, self.n = s, 0

            def up(self, ins):
                ins.then_inc(self.s, 1)
                self.n += 1

        def weight_loads(L):
            b, c = B[L], LAYERS[L]
            lo, hi = b["ws"][:, 0, :], b["ws"][:, 1, :]
            r = []

            def spread(dst, w):
                for m in range(3):
                    r.append((dst[m:96:3, 32 * m:32 * m + 32], w))

            if L in (0, 3):
                p = f"L{L}_gnn_"
                r.append((lo[0:64, 0:64], A[p + "Wl1_0"]))
                r.append((lo[0:64, 64:128], A[p + "Wsc0"]))
                spread(hi[:, 0:96], A[p + "Wl1_1"])
                spread(hi[:, 96:192], A[p + "Wsc1"])
                r.append((lo[0:96, 128:192], A[p + "Wl2_s"]))
                r.append((lo[0:96, 192:193], A[p + "Wa"]))
                r.append((lo[0:96, 193:225], A[p + "Wl2_v"]))
            if L == 1:
                p = "L1_gnn_"
                r.append((lo[0:64, 0:64], A[p + "Ws_l1_a"]))
                r.append((lo[0:64, 64:128], A[p + "Ws_sc_a"]))
                r.append((lo[0:64, 128:192], A[p + "Ws_l1_c"]))
                r.append((lo[0:64, 192:256], A[p + "Ws_sc_c"]))
                spread(hi[:, 0:96], A[p + "Wv_l1_a"])
                spread(hi[:, 96:192], A[p + "Wv_sc_a"])
                spread(hi[:, 192:288], A[p + "Wv_l1_c"])
                spread(hi[:, 288:384], A[p + "Wv_sc_c"])
                for i, n in enumerate(("Ws_l2_a", "Ws_l2_c", "Wv_l2_a", "Wv_l2_c")):
                    r.append((lo[0:96, 256 + 96 * i:352 + 96 * i], A[p + n]))
                r.append((hi[0:96, 384:448], A[p + "Ws_l3"]))
                r.append((hi[0:96, 448:480], A[p + "Wv_l3"]))
            if L == 2:
                p = "L2_gnn_"
                r.append((lo[0:64, 0:64], A[p + "W_nl0"]))
                r.append((lo[0:64, 64:160], A[p + "W_skip0"]))
                spread(hi[:, 0:96], A[p + "W_nl1"])
                spread(hi[:, 96:192], A[p + "W_skip1"])
                r.append((lo[0:96, 160:256], A[p + "W_out_s"]))
                r.append((lo[0:64, 256:288], A[p + "W_out_v"][0:64, :]))
                for m in range(3):
                    r.append((lo[32 * m:32 * m + 32, 288:320], A[p + "W_out_v"][64:96, :]))
                for q in range(2):
                    r.append((lo[32 * q:32 * q + 32, 320:352], A[p + "W_out_v"][96:128, :]))
                r.append((lo[64:96, 352:384], A[p + "W_out_v"][64:96, :]))
            if L == 0:
                for g in range(2):
                    at = PAIR_STEP * g + c["col"]
                    r.append((b["w1"][at:at + 16, 64 * g:64 * g + 64], A["L0_gnn_Wfc1"]))
                    r.append((hi[64 * g:64 * g + 64, 192:384], A["L0_gnn_Wfc2"]))
            if L == 1:
                for g in range(2):
                    at = PAIR_STEP * g + c["col"]
                    r.append((b["w1"][at:at + 10, g, :], A["L1_gnn_W_fc1"]))
                r.append((b["w2"][0:100, :], A["L1_gnn_W_fc2"]))
            if L == 2:
                r.append((b["w1"][0:64, :], A["L2_gnn_W_fc1"]))
                for g in range(2):
                    r.append((b["w2"][64 * g:64 * g + 64, 224 * g:224 * g + 224], A["L2_gnn_W_fc2"]))
            if L == 3:
                for g in range(2):
                    at = PAIR_STEP * g + c["col"]
                    r.append((b["w1"][at:at + 8, 64 * g:64 * g + 64], A["L3_gnn_Wfc1"]))
                    r.append((b["wmid"][64 * g:64 * g + 64, 64 * g:64 * g + 64], A["L3_gnn_Wfc2"]))
                    r.append((hi[64 * g:64 * g + 64, 192:384], A["L3_gnn_Wfc3"]))
            return r

        n_loads = [len(weight_loads(L)) for L in range(4)]
        loads_to = [16 * sum(n_loads[:L + 1]) for L in range(4)]

        def stage_of(L, k):
            return 3 + 5 * L + k

        tile_at = lambda t: bass.ds(X0 + t * D, D)
        x_tile = lambda t: arena[:, tile_at(t)]

        def agg_tile(L, t):
            return arena[:, bass.ds(B[L]["agg_off"] + t * LAYERS[L]["aw"], LAYERS[L]["aw"])]

        def out_count(upto, s):
            tiles = NT - NT // 2 if s == 0 else NT // 2
            return sum(16 * tiles * (2 if L == 2 else 1) for L in range(upto))

        def rows_base(L, q):
            return L * (ITERS + (1 if q < 2 else 0))

        def gath_base(L, s):
            return L * (2 * ITERS + (1 if s == 0 else 0))

        nv_off = X0 + NT * D
        recip_off = nv_off + 3 * NT
        sq_off = recip_off + NT
        mask_off = sq_off + NT
        ln_rstd_off = mask_off + 2 * NT + 3 * NT
        ln_bias_off = ln_rstd_off + NT

        def arena_col(off, t):
            return arena[:, off + t:off + t + 1] if isinstance(t, int) else arena[:, bass.ds(t + off, 1)]

        @block.sync
        def _(sp):
            sp.dma_start(const, A["consts"]).then_inc(const_in, 16)
            sp.dma_start(idx_d[0:EP, :], A["dst"].rearrange("(p c) -> p c", c=EC)).then_inc(idx_in, 16)
            sp.dma_start(idx_s[0:EP, :], A["src"].rearrange("(p c) -> p c", c=EC)).then_inc(idx_in, 16)
            sp.dma_start(vec[0:EP, :, :], A["edge_attr_3"].rearrange("(p c) w -> p c w", c=EC)).then_inc(vec_in, 16)
            sp.wait_ge(zero_set, 3)
            full = (NT - 1) * P
            sp.dma_start(x[:, 0:NT - 1, :], A["x"][0:full, :].rearrange("(t p) d -> p t d", p=P)).then_inc(x_in, 16)
            sp.dma_start(x[0:NREST, NT - 1, :], A["x"][full:N, :]).then_inc(x_in, 16)
            for rows, w in ((rows_d, ROW_D["w"]), (rows_s, ROW_S["w"])):
                per = SLOTS * w // P
                whole = per // 2048
                flat = rows.rearrange("(p r) w -> p (r w)", p=P)
                for k in range(0, whole):
                    sp.dma_start(flat[:, 2048 * k:2048 * k + 2048], zrow).then_inc(prefilled, 16)
                if per % 2048:
                    sp.dma_start(flat[:, 2048 * whole:per], zrow[:, 0:per % 2048]).then_inc(prefilled, 16)
            for i, name in enumerate(("node_vec1", "node_vec1_n2", "node_vec1_n3")):
                with nc.allow_non_contiguous_dma(reason="node scalars, one per partition"):
                    sp.dma_start(nv[:, i, 0:NT - 1], A[name][0:full, :].rearrange("(t p) o -> p (t o)", p=P)).then_inc(x_in, 16)
                    sp.dma_start(nv[0:NREST, i, NT - 1:NT], A[name][full:N, :]).then_inc(x_in, 16)
            sp.wait_ge(x_in, 16 * 8)
            n_fill = sum(-(-(SLOTS * w // P) // 2048) for w in (ROW_D["w"], ROW_S["w"]))
            sp.wait_ge(prefilled, 16 * n_fill)
            stage(sp, 1)

            def chunk(name, k):
                return A[name].rearrange("(p c) w -> p (c w)", c=EC)[:, bass.ds(k * (CC * A[name].shape[1]), CC * A[name].shape[1])]

            def turn_buckets(o):
                sp.wait_ge(table_done, o + 1)
                with nc.allow_non_contiguous_dma(reason="a short table"):
                    sp.dma_start(bucket_dram[o, :].rearrange("(c p) -> p c", p=P), step_i).then_inc(step_out, 16)
                sp.wait_ge(step_out, 16 * (o + 1))
                sp.dma_start(bucket_rows[o][0:1, :], bucket_dram[o:o + 1, :]).then_inc(step_in, 16)
                sp.wait_ge(step_in, 16 * (o + 1))

            def load_chunk(k, s, i):
                sp.wait_ge(payload_ready, i * 2 + (s + 1))
                for name, st in (("edge_attr_16", st16), ("edge_attr_10", st10), ("edge_attr_8", st8), ("edge_attr_4", st4)):
                    sp.dma_start(st[s][0:EP, :, :].rearrange("p c w -> p (c w)"), chunk(name, k)).then_inc(stage_in[s], 16)

            for s in range(2):
                load_chunk(s, s, 0)
            turn_buckets(0)
            with sp.Fori(1, CHUNKS // 2) as i:
                for s in range(2):
                    load_chunk(i * 2 + s, s, i)
            turn_buckets(1)
            stage(sp, 2)

            for L, c in enumerate(LAYERS):
                b = B[L]
                sp.wait_ge(agg_zero, 2 * L + 1)
                with nc.allow_non_contiguous_dma(reason="weights"):
                    for dst, srcw in weight_loads(L):
                        sp.dma_start(dst, srcw).then_inc(weights_in, 16)
                sp.wait_ge(weights_in, loads_to[L])
                stage(sp, stage_of(L, 0))
                stage(sp, stage_of(L, 1))

                def store(t, s, k):
                    sp.wait_ge(u_ready, k + 2)
                    sp.dma_start(table[bass.ds(t * P, P), :], b["u"][s][:, 0:D]).then_inc(table_out[s], 16)
                    if L == 2:
                        sp.dma_start(skip_dram[bass.ds(t * P, P), :], b["u"][s][:, 160:352]).then_inc(table_out[s], 16)

                with sp.Fori(0, NT // 2) as i:
                    for s in range(2):
                        store(i * 2 + s, s, i * 2 + (NT * L + s + 1))
                store(NT - 1, 0, NT * L + NT)
                for s in range(2):
                    sp.wait_ge(table_out[s], out_count(L + 1, s))
                stage(sp, stage_of(L, 2))

                R = rows_s if L == 2 else rows_d
                w = c["rows"]["w"]
                per_quad = R.rearrange("(q p u) w -> p q (u w)", p=P, u=4)

                def load(q, s, k):
                    sp.wait_ge(x_ready, k)
                    sp.wait_ge(copies_done, k)
                    sp.dma_start(b["rows"][s].rearrange("p a b -> p (a b)"), per_quad[:, q, :] if isinstance(q, int) else
                                 per_quad[:, bass.ds(q, 1), :].rearrange("p a b -> p (a b)")).then_inc(rows_in[s], 16)

                def load_attr64(h, i):
                    if not (isinstance(i, int) and L == 0):
                        sp.wait_ge(sent[h], i * (16 * HC) + 16 * HC * MOVING * L)
                    col = i * (2 * HC) + (2 * HC * MOVING * L + HC * h)
                    sp.dma_start(pay_s[h][0:EP, :, 0:64], A["edge_attr_64"].rearrange("(p c) w -> p c w", c=EC)[:, bass.ds(col, HC), :]
                                 ).then_inc(attr64_in[h], 16)

                def load_iteration(i, moving):
                    for s in range(4):
                        load(i * 4 + s, s, i * 8 + ((PAIRS + 1) * L + 2 * s + 2))
                        if moving and s in (0, 2):
                            load_attr64(s // 2, i)

                if L < 2:
                    load_iteration(0, True)
                    with sp.Fori(1, MOVING) as i:
                        load_iteration(i, True)
                    with sp.Fori(MOVING, ITERS) as i:
                        load_iteration(i, False)
                else:
                    with sp.Fori(0, ITERS) as i:
                        load_iteration(i, False)
                for s in range(2):
                    load(QUADS + s, s, (PAIRS + 1) * L + 2 * (QUADS + s) + 2 - s * 0)
                stage(sp, stage_of(L, 3))

                if L == 2:
                    def fetch(t, s, k):
                        if k is not None:
                            sp.wait_ge(o_y, k)
                        sp.dma_start(b["sk"][s], skip_dram[bass.ds(t * P, P), :]).then_inc(skip_in[s], 16)

                    fetch(0, 0, None)
                    fetch(1, 1, None)
                    with sp.Fori(0, NT // 2 - 1) as i:
                        for s in range(2):
                            fetch(i * 2 + (s + 2), s, i * 2 + (s + 1))
                    fetch(NT - 1, 0, NT - 2)
                    sp.wait_ge(o_y, NT)
                stage(sp, stage_of(L, 4))
            sp.dma_start(out[0:full, :].rearrange("(t p) d -> p t d", p=P), x[:, 0:NT - 1, :]).then_inc(out_done, 16)
            sp.dma_start(out[full:N, :], x[0:NREST, NT - 1, :]).then_inc(out_done, 16)
            sp.wait_ge(out_done, 32)

        @block.gpsimd
        def _(pool):
            pool.memset(x[:, NT - 1, :], 0.0).then_inc(zero_set, 1)
            pool.memset(nv, 0.0).then_inc(zero_set, 1)
            pool.memset(zrow, 0.0).then_inc(zero_set, 1)
            pool.wait_ge(vec_squared, 1)
            sq = lambda m: vec_sq[0:EP, :, m:m + 1].rearrange("p c o -> p (c o)")
            pool.tensor_tensor(vec_norm[0:EP, 0, :], sq(0), sq(1), ALU.add).then_inc(vec_summed, 1)
            pool.wait_ge(vec_summed, 1)
            pool.tensor_tensor(vec_norm[0:EP, 0, :], vec_norm[0:EP, 0, :], sq(2), ALU.add).then_inc(vec_summed, 1)
            stage(pool, 1)
            with pool.Fori(0, CHUNKS // 2) as i:
                for s in range(2):
                    pool.wait_ge(payload_ready, i * 2 + (s + 3))
                    pool.sem_inc(pool_steps, 1)
                    for j in range(CC):
                        pool.indirect_dma_start(
                            out=rows_d, out_offset=bass.IndirectOffsetOnAxis(ap=adr[s][0:EP, j:j + 1], axis=0),
                            in_=pay_d[s][0:EP, j, :], in_offset=None).then_inc(scattered[s], 16)
            for s in range(2):
                pool.wait_ge(scattered[s], 16 * CC * (CHUNKS // 2))
            stage(pool, 2)
            for L, c in enumerate(LAYERS):
                b = B[L]
                hi_end = b["agg_off"] + NT * c["aw"]
                first = [b["w1"], b["w2"]] + ([b["wmid"]] if L == 3 else []) + [b["ws"], b["pv"], b["oa"], b["om"]] + ([b["ob"], b["oc"]] if L == 2 else [])
                for k, v in enumerate(first):
                    ins = pool.memset(v, 0.0)
                    if k == len(first) - 1:
                        ins.then_inc(agg_zero, 1)
                stage(pool, stage_of(L, 0))
                stage(pool, stage_of(L, 1))
                pool.memset(b["agg"], 0.0).then_inc(agg_zero, 1)
                stage(pool, stage_of(L, 2))

                def gather(rs, q, s, k_rows, k_free):
                    pool.wait_ge(rows_in[q], k_rows)
                    pool.sem_inc(pool_steps, 1)
                    pool.wait_ge(prod_free, k_free)
                    pool.sem_inc(pool_steps, 1)
                    for g in range(2):
                        u = 2 * (rs % 2) + g
                        col = c["rows"]["idx"]
                        pool.indirect_dma_start(
                            out=b["gath"][s][:, g, :], out_offset=None, in_=table,
                            in_offset=bass.IndirectOffsetOnAxis(ap=b["rows"][q].bitcast(I32)[:, u, col:col + 1], axis=0),
                        ).then_inc(gath_in[s], 16)

                def send(h, j, i):
                    if j == 0:
                        pool.wait_ge(attr64_in[h], i * 16 + 16 * (MOVING * L + 1))
                        pool.sem_inc(pool_steps, 1)
                        pool.wait_ge(tail_ready[h], i + ((MOVING + 1 - h) * L + 1))
                        pool.sem_inc(pool_steps, 1)
                    w = ROW_S["w"]
                    pool.indirect_dma_start(
                        out=rows_s, out_offset=bass.IndirectOffsetOnAxis(ap=pay_s[h].bitcast(I32)[0:EP, j, w:w + 1], axis=0),
                        in_=pay_s[h][0:EP, j, 0:w], in_offset=None).then_inc(sent[h], 16)

                def gather_iteration(i, moving):
                    for r in range(8):
                        gather(r, r // 2, r % 4, i * 16 + 16 * (rows_base(L, r // 2) + 1), i * 8 + ((PAIRS + 1) * L + r + 1))
                        if moving:
                            send(r // HC, r % HC, i)

                moving = MOVING if L < 2 else 0
                if moving:
                    with pool.Fori(0, moving) as i:
                        gather_iteration(i, True)
                with pool.Fori(moving, ITERS) as i:
                    gather_iteration(i, False)
                if moving:
                    for h in range(2):
                        pool.wait_ge(sent[h], 16 * HC * MOVING * (L + 1))
                gather(0, 0, 0, 16 * (rows_base(L, 0) + ITERS + 1), (PAIRS + 1) * L + PAIRS + 1)
                stage(pool, stage_of(L, 3))
                if L == 2:
                    def take(t, s, k):
                        pool.wait_ge(agg_T, k)
                        pool.tensor_copy(b["aggS"][s], agg_tile(L, t)).then_inc(agg_st, 1)

                    with pool.Fori(0, NT // 2) as i:
                        for s in range(2):
                            take(i * 2 + s, s, i * 2 + (NT * L + s + 1))
                    take(NT - 1, 0, NT * L + NT)
                stage(pool, stage_of(L, 4))

        @block.scalar
        def _(act):
            act.wait_ge(const_in, 16)
            act.wait_ge(vec_in, 16)
            act.activation(vec_sq[0:EP, :, :], vec[0:EP, :, :], ACT.Square).then_inc(vec_squared, 1)
            act.wait_ge(vec_summed, 2)
            act.activation(vec_norm[0:EP, 1, :], vec_norm[0:EP, 0, :], ACT.Sqrt).then_inc(vec_root, 1)
            stage(act, 1)

            def fill(i, s):
                k = i * 2 + s
                cols = slice(k * CC, k * CC + CC) if isinstance(k, int) else bass.ds(k * CC, CC)
                act.wait_ge(stage_in[s], i * 64 + 64)
                if not isinstance(i, int):
                    act.wait_ge(scattered[s], i * (16 * CC))
                pay_ = pay_d[s][0:EP, :, :]
                r = ROW_D
                act.activation(adr[s][0:EP, :], addr_d[0:EP, cols], ACT.Copy)
                act.activation(pay_[:, :, r["idx"]:r["idx"] + 1].bitcast(I32), idx_s[0:EP, cols].rearrange("p (c o) -> p c o", o=1), ACT.Copy)
                act.activation(pay_[:, :, r["dl"]:r["dl"] + 1], low_d[0:EP, cols].rearrange("p (c o) -> p c o", o=1), ACT.Copy)
                act.activation(pay_[:, :, r["a16"]:r["a16"] + 16], st16[s][0:EP, :, :], ACT.Copy)
                act.activation(pay_[:, :, r["a10"]:r["a10"] + 10], st10[s][0:EP, :, :], ACT.Copy)
                act.activation(pay_[:, :, r["a8"]:r["a8"] + 8], st8[s][0:EP, :, :], ACT.Copy)
                act.activation(pay_[:, :, r["sh"]:r["sh"] + 4], st4[s][0:EP, :, :], ACT.Copy).then_inc(payload_ready, 1)

            for s in range(2):
                fill(0, s)
            with act.Fori(1, CHUNKS // 2) as i:
                for s in range(2):
                    fill(i, s)
            stage(act, 2)
            for L, c in enumerate(LAYERS):
                b = B[L]
                stage(act, stage_of(L, 0))
                sq = arena[:, b["agg_off"]:b["agg_off"] + NT * D]
                act.wait_ge(ln_a, 2 * L + 1)
                act.activation(sq, sq, ACT.Square).then_inc(ln_b, 1)
                act.wait_ge(ln_a, 2 * L + 2)
                act.activation(ln_rstd, ln_sq, ACT.Sqrt, bias=eps, scale=1.0 / D).then_inc(ln_b, 1)
                stage(act, stage_of(L, 1))

                def normed(t, s, k):
                    act.wait_ge(hT_ready, k)
                    act.activation(b["h"][s], x_tile(t), ACT.Relu, bias=arena_col(ln_bias_off, t),
                                   scale=arena_col(ln_rstd_off, t)).then_inc(h_ready, 1)

                def second(t, s, k):
                    act.wait_ge(f_ready, k)
                    act.activation(b["utmp"][s], bank[:, 4 + 2 * s + 1, 0:320], ACT.Copy, scale=arena_col(nv_off + NT, t)).then_inc(f_tmp, 1)

                NB = NT * L
                normed(0, 0, NB + 1)
                normed(1, 1, NB + 2)
                with act.Fori(0, NT // 2 - 1) as i:
                    for s in range(2):
                        normed(i * 2 + (s + 2), s, i * 2 + (NB + s + 3))
                        if L == 1:
                            second(i * 2 + s, s, i * 2 + (NB + s + 1))
                normed(NT - 1, 0, NB + NT)
                if L == 1:
                    for t in range(NT - 3, NT):
                        second(t, t % 2, NB + t + 1)
                stage(act, stage_of(L, 2))

                def act_turn(par, kt):
                    act.wait_ge(turned, kt)
                    rowsn, cols = (ROW_S["w"], 512) if L == 2 else (PAIR_ROWS, 256)
                    act.activation(b["tT"][par][0:rowsn, :, :], bank[0:rowsn, 0, 0:cols].rearrange("p (a b) -> p a b", b=P),
                                   ACT.Copy).then_inc(turned_sb, 1)

                def act_hidden(par, kh):
                    act.wait_ge(hidden1, kh)
                    if L == 0:
                        act.activation(b["hT"][par], bank[:, 1, 0:256].rearrange("p (a b) -> p a b", b=P), ACT.Silu, scale=0.25).then_inc(hidden_sb, 1)
                    elif L == 1:
                        act.activation(b["hT"][par][0:100, :, :], bank[0:100, 1, :].rearrange("p (a b) -> p a b", b=P), ACT.Silu).then_inc(hidden_sb, 1)
                    elif L == 2:
                        act.activation(b["hT"][par], bank[:, 1, 0:256].rearrange("p (a b) -> p a b", b=P), ACT.Relu).then_inc(hidden_sb, 1)
                    else:
                        act.activation(b["h1T"][par], bank[:, 1, 0:256].rearrange("p (a b) -> p a b", b=P), ACT.Gelu_apprx_tanh,
                                       scale=8.0 ** -0.5).then_inc(hidden1_sb, 1)

                def act_hidden2(par, kh):
                    act.wait_ge(hidden2, kh)
                    act.activation(b["hT"][par], bank[:, 1, 256:512].rearrange("p (a b) -> p a b", b=P), ACT.Gelu_apprx_tanh,
                                   scale=0.125).then_inc(hidden_sb, 1)

                def act_scale(n, i):
                    gs, q = n % 4, (n // 2) % 4
                    act.wait_ge(gath_in[gs], i * 64 + 32 * (gath_base(L, gs) + 1 + n // 4))
                    for g in range(2):
                        sh = c["rows"]["sh"]
                        ins = act.activation(b["E0"][gs][:, g, :], b["gath"][gs][:, g, :], ACT.Copy, scale=b["rows"][q][:, 2 * (n % 2) + g, sh:sh + 1])
                    ins.then_inc(e_scaled, 1)

                def act_last(n, kp):
                    act.wait_ge(first_products, kp)
                    s, q = n % 2, (n // 2) % 4
                    for g in range(2):
                        sh = c["rows"]["sh"] + 3
                        ins = act.activation(b["X"][s][:, g, VM0 + 192:VM0 + 256], b["X"][s][:, g, W1E0:W1E0 + 64], ACT.Copy,
                                             scale=b["rows"][q][:, 2 * (n % 2) + g, sh:sh + 1])
                    ins.then_inc(copies_done, 1)

                def act_pair(q, rp, s, kp):
                    act.wait_ge(onehot_ready, kp)
                    rows, Sx, rw = b["rows"][q], b["S"][s], c["rows"]
                    for k in (2, 3):
                        sh = rw["sh"] + k - 1
                        for g in range(2):
                            act.activation(Sx[:, g, k, :], Sx[:, g, 0, :], ACT.Copy, scale=rows[:, 2 * rp + g, sh:sh + 1])
                    act.wait_ge(first_products, kp)
                    X, mw = b["X"][s], c["mw"]
                    Xm = X[:, :, 160:160 + 3 * mw].rearrange("p g (m w) -> p g m w", m=3)
                    act.activation(Xm[:, :, 1:3, 0:64], Xm[:, :, 0:1, 0:64].to_broadcast([P, 2, 2, 64]), ACT.Copy).then_inc(copies_done, 1)

                QB, PB = (QUADS + 2) * L, (PAIRS + 1) * L
                act_turn(0, QB + 1)
                act_turn(1, QB + 2)
                act_hidden(0, QB + 1)
                if L == 3:
                    act_hidden2(0, 1)
                act_hidden(1, QB + 2)
                if L == 2:
                    act_pair(0, 0, 0, PB + 1)
                else:
                    act_scale(0, 0)
                with act.Fori(0, ITERS) as i:
                    for q in range(4):
                        if L != 2:
                            act_last(2 * q, i * 8 + (PB + 2 * q + 1))
                            act_scale(2 * q + 1, i)
                        act_turn(q % 2, i * 4 + (QB + q + 3))
                        if L == 3:
                            act_hidden2((q + 1) % 2, i * 4 + (q + 2))
                        if L == 2:
                            act_pair(q, 1, 1, i * 8 + (PB + 2 * q + 2))
                        else:
                            act_last(2 * q + 1, i * 8 + (PB + 2 * q + 2))
                            act_scale(2 * q + 2, i)
                        act_hidden(q % 2, i * 4 + (QB + q + 3))
                        if L == 2:
                            act_pair((q + 1) % 4, 0, 0, i * 8 + (PB + 2 * q + 3))
                if L != 2:
                    act_last(0, PB + PAIRS + 1)
                stage(act, stage_of(L, 3))

                def take(t, s, k):
                    act.wait_ge(agg_T, k)
                    act.activation(b["aggS"][s], agg_tile(L, t), ACT.Copy, scale=arena_col(recip_off, t) if L == 0 else 1.0).then_inc(agg_st, 1)

                def after(t, s, k):
                    if L == 1:
                        act.wait_ge(o_ready, k)
                        act.activation(b["utmp"][s][:, 0:160], bank[:, 4 + s, 160:320], ACT.Copy, scale=arena_col(mask_off + NT, t)).then_inc(o_tmp, 1)
                    if L == 2:
                        act.wait_ge(o_y, k - 2 * NT)
                        act.activation(b["utmp"][s][:, 0:96], b["u"][s][:, 0:96], ACT.Sigmoid).then_inc(o_gate, 1)

                if L == 0:
                    act.wait_ge(counts_ready, 1)
                if L == 2:
                    with act.Fori(0, NT // 2) as i:
                        for s in range(2):
                            after(None, s, i * 2 + (NB + s + 1))
                    after(None, 0, NB + NT)
                else:
                    take(0, 0, NB + 1)
                    take(1, 1, NB + 2)
                    with act.Fori(0, NT // 2 - 1) as i:
                        for s in range(2):
                            take(i * 2 + (s + 2), s, i * 2 + (NB + s + 3))
                            after(i * 2 + s, s, i * 2 + (NB + s + 1))
                    for t in range(NT - 3, NT):
                        if t == NT - 3:
                            take(NT - 1, 0, NB + NT)
                        after(t, t % 2, NB + t + 1)
                stage(act, stage_of(L, 4))

        @block.tensor
        def _(pe):
            pe.sem_inc(hT_ready, 2)
            pe.sem_inc(agg_T, 2)
            pe.wait_ge(const_in, 16)
            for o in range(2):
                pe.wait_ge(totals_done, o + 1)
                pe.matmul(bank[0:EP, 0, 0:NT], tri[0:EP, 0:EP], totals[0:EP, :], start=True, stop=True)
                pe.matmul(bank[:, 1, 0:NT], ones[0:EP, :], totals[0:EP, :], start=True, stop=True).then_inc(offsets_done, 1)
                stage(pe, o + 1)
            for L, c in enumerate(LAYERS):
                b = B[L]
                if L == 1:
                    lo, hi = b["ws"][:, 0, :], b["ws"][:, 1, :]
                    pe.wait_ge(weights_in, loads_to[L])
                    for k in range(4):
                        ins = pe.transpose(bank[0:96, 0, 96 * k:96 * k + 96], lo[0:96, 256 + 96 * k:352 + 96 * k], ident[0:96, 0:96])
                    ins.then_inc(offsets_done, 1)
                    pe.wait_ge(totals_done, 3)
                    for k, (cols, wid) in enumerate(((384, 64), (384, 64), (448, 32), (448, 32))):
                        ins = pe.matmul(bank[0:96, 1, 64 * k:64 * k + wid], lo[0:96, 256 + 96 * k:352 + 96 * k], hi[0:96, cols:cols + wid], start=True, stop=True)
                    ins.then_inc(offsets_done, 1)
                stage(pe, stage_of(L, 0))
                stage(pe, stage_of(L, 1))

                def turn_h(s, k):
                    pe.wait_ge(h_ready, k)
                    pe.transpose(bank[0:96, s, P:2 * P], b["h"][s][:, 64:160], ident)
                    pe.transpose(bank[0:64, s, 0:P], b["h"][s][:, 0:64], ident).then_inc(hT_ready, 1)

                def mix(s, k, kfree):
                    pe.wait_ge(hT_sb, k)
                    pe.wait_ge(u_ready, kfree)
                    f0, f1 = 4 + 2 * s, 5 + 2 * s
                    hs, hv = b["hTs"][s][0:64, :], b["hTv"][s][0:96, :]
                    both = lambda bk, half, o, n: bank[:, bk, 0:2 * half].rearrange("p (z w) -> p z w", z=2)[:, :, o:o + n]
                    if L == 2:
                        parts = [(both(f0, 192, 64, 96), hv, b["pv"][0:96, 0:192]),
                                 (bank[:, f0, 0:64], hs, b["ps"][0:64, 0:64]), (bank[:, f0, 160:256], hs, b["ps"][0:64, 64:160])]
                    else:
                        parts = []
                        for a in range(2 if L == 1 else 1):
                            parts.append((both((f0, f1)[a], 160, 64, 96), hv, b["pv"][0:96, 192 * a:192 * a + 192]))
                            parts.append((both((f0, f1)[a], 160, 0, 64), hs, b["ps"][0:64, 128 * a:128 * a + 128]))
                    for o, l, r in parts:
                        ins = pe.matmul(o, l, r, start=True, stop=True)
                    ins.then_inc(f_ready, 1)

                NB = NT * L
                turn_h(0, NB + 1)
                with pe.Fori(0, NT // 2) as i:
                    for s in range(2):
                        turn_h(1 - s, i * 2 + (NB + s + 2))
                        mix(s, i * 2 + (NB + s + 1), i * 2 + (NB + s + 1))
                mix(0, NB + NT, NB + NT)
                stage(pe, stage_of(L, 2))

                kin, wn, xw, mw = c["kin"], c["wn"], c["xw"], c["mw"]
                QB, PB = (QUADS + 2) * L, (PAIRS + 1) * L

                def turn(q, par, k_rows, k_bank):
                    pe.wait_ge(rows_in[q], k_rows)
                    if k_bank is not None:
                        pe.wait_ge(turned_sb, k_bank)
                    rows = b["rows"][q]
                    if L == 2:
                        for u in range(4):
                            ins = pe.transpose(bank[0:ROW_S["w"], 0, P * u:P * u + P], rows[:, u, :], ident)
                    else:
                        flat = rows.rearrange("p a b -> p (a b)")
                        for v in range(2):
                            ins = pe.transpose(bank[0:PAIR_ROWS, 0, P * v:P * v + P],
                                               flat[:, 2 * PAIR_STEP * v:2 * PAIR_STEP * v + PAIR_ROWS], ident)
                    ins.then_inc(turned, 1)

                def first_layer(par, k_turned, k_bank):
                    pe.wait_ge(turned_sb, k_turned)
                    if k_bank is not None:
                        pe.wait_ge(hidden_sb, k_bank)
                    tT = b["tT"][par]
                    if L == 2:
                        for g in range(2):
                            ins = pe.matmul(bank[64 * g:64 * g + 64, 1, 0:256], b["w1"][0:ROW_S["w"], :],
                                            tT[0:ROW_S["w"], g:4:2, :], start=True, stop=True, tile_position=(0, 64 * g))
                    elif L == 1:
                        for u in range(4):
                            ins = pe.matmul(bank[0:100, 1, P * u:P * u + P], b["w1"][0:PAIR_ROWS, u % 2, :],
                                            tT[0:PAIR_ROWS, u // 2, :], start=True, stop=True)
                    else:
                        ins = pe.matmul(bank[:, 1, 0:256], b["w1"][0:PAIR_ROWS, :], tT[0:PAIR_ROWS, :, :], start=True, stop=True)
                    ins.then_inc(hidden1, 1)

                def second_layer(par, k):
                    pe.wait_ge(hidden1_sb, k)
                    for v in range(2):
                        ins = pe.matmul(bank[:, 1, 256 + P * v:256 + P * v + P], b["wmid"], b["h1T"][par][:, v, :], start=True, stop=True)
                    ins.then_inc(hidden2, 1)

                def edge_weights(rp, par, s, k_hidden, k_free):
                    pe.wait_ge(hidden_sb, k_hidden)
                    pe.wait_ge(prod_free, k_free)
                    if L == 1:
                        for g in range(2):
                            ins = pe.matmul(bank[:, 2 + s, wn * g:wn * g + wn], b["hT"][par][0:100, 2 * rp + g, :], b["w2"][0:100, :],
                                            start=True, stop=True)
                    else:
                        ins = pe.matmul(bank[:, 2 + s, 0:2 * wn], b["hT"][par][:, rp, :], b["w2"], start=True, stop=True)
                    ins.then_inc(w_ready, 1)

                def sums(s, k_x, k_free):
                    pe.wait_ge(x_ready, k_x + 8)
                    pe.wait_ge(copies_done, k_x + 8)
                    pe.wait_ge(summed, k_free)
                    X, Sx = b["X"][s], b["S"][s]
                    if L != 2:
                        for g in range(2):
                            ins = pe.matmul(bank[:, 4 + 2 * s, 0:c["aw"]], Sx[:, g, 0, :], X[:, g, 0:c["aw"]], start=g == 0, stop=g == 1)
                        ins.then_inc(sums_ready, 1)
                        return
                    for g in range(2):
                        last = g == 1
                        for k in range(4):
                            first = g == 0 and k in (0, 2)
                            o = bank[:, 4 + 2 * s + k // 2, 160 * (k % 2):160 * (k % 2) + 160]
                            r = X[:, g, 0:160] if k == 0 else X[:, g, 160 + mw * (k - 1):160 + mw * k]
                            ins = pe.matmul(o, Sx[:, g, k, :], r, start=first, stop=last, skip_group_check=True)
                    ins.then_inc(sums_ready, 1)

                turn(0, 0, 16 * (rows_base(L, 0) + 1), QB if L else None)
                turn(1, 1, 16 * (rows_base(L, 1) + 1), QB + 1)
                first_layer(0, QB + 1, QB if L else None)
                if L == 3:
                    second_layer(0, 1)
                first_layer(1, QB + 2, QB + 1)
                edge_weights(0, 0, 0, QB + 1, PB + 3)
                with pe.Fori(0, ITERS) as i:
                    for q in range(4):
                        nq = (q + 2) % 4
                        turn(nq, q % 2, i * 16 + 16 * (rows_base(L, nq) + (1 if q < 2 else 2)), i * 4 + (QB + q + 2))
                        if L == 3:
                            second_layer((q + 1) % 2, i * 4 + (q + 2))
                        edge_weights(1, q % 2, 1, i * 4 + (QB + q + 1), i * 8 + (PB + 2 * q + 4))
                        sums(0, i * 8 + (PB + 2 * q + 1), i * 8 + (PAIRS * L + 2 * q + 1))
                        first_layer(q % 2, i * 4 + (QB + q + 3), i * 4 + (QB + q + 2))
                        edge_weights(0, (q + 1) % 2, 0, i * 4 + (QB + q + 2), i * 8 + (PB + 2 * q + 5))
                        sums(1, i * 8 + (PB + 2 * q + 2), i * 8 + (PAIRS * L + 2 * q + 2))
                stage(pe, stage_of(L, 3))

                def turn_sums(s, k):
                    pe.wait_ge(agg_st, k)
                    a = b["aggS"][s]
                    if L != 2:
                        for v in range(4):
                            ins = pe.transpose(bank[0:96, 2 * s + 1, P * v:P * (v + 1)], a[:, 96 * v:96 * v + 96], ident)
                        ins.then_inc(agg_T, 1)
                        return
                    pe.transpose(bank[0:96, 2 * s + 1, 0:P], a[:, 64:160], ident)
                    pe.transpose(bank[0:64, 2 * s, 0:P], a[:, 0:64], ident)
                    if True:
                        for m in range(3):
                            pe.transpose(bank[0:64, 2 * s, P * (m + 1):P * (m + 2)], a[:, 256 + 160 * m:320 + 160 * m], ident)
                    for m in range(3):
                        ins = pe.transpose(bank[0:96, 2 * s + 1, P * (m + 1):P * (m + 2)], a[:, 160 + mw * m:256 + mw * m], ident)
                    ins.then_inc(agg_T, 1)

                def outputs(s, k, kfree):
                    if L == 2:
                        pe.wait_ge(aggA_sb, k - NT * 2)
                    pe.wait_ge(aggB_sb, k)
                    pe.wait_ge(node_x, kfree)
                    o, Bt = bank[:, 4 + s, :], b["aTB"][s]
                    if L == 2:
                        At = b["aTA"][s]
                        for m in range(3):
                            pe.matmul(o[:, 0:192], Bt[0:96, 1 + m, :], b["om"][0:96, m, :], start=m == 0, stop=False, skip_group_check=True)
                        pe.matmul(o[:, 0:96], At[0:64, 0, :], b["oa"][0:64, 0:96], start=False, stop=True, skip_group_check=True)
                        for m in range(3):
                            pe.matmul(o[:, 96:192], At[0:64, 1 + m, :], b["oc"][0:64, m, 96:192], start=False, stop=False, skip_group_check=True)
                        ins = pe.matmul(o[:, 96:192], Bt[0:96, 0, :], b["ob"][0:96, 96:192], start=False, stop=True, skip_group_check=True)
                    else:
                        if L == 1:
                            scal = lambda a: a[:, 0:320].rearrange("p (z w) -> p z w", z=2)[:, :, 0:64]
                            vect = lambda a: a[:, 0:320].rearrange("p (z w) -> p z w", z=2)[:, :, 64:160]
                        else:
                            scal, vect = (lambda a: a[:, 0:65]), (lambda a: a[:, 65:161])
                        pe.matmul(scal(o), Bt[0:96, 0, :], scal(b["oa"][0:96, :]), start=True, stop=True, skip_group_check=True)
                        for m in range(3):
                            ins = pe.matmul(vect(o), Bt[0:96, 1 + m, :], vect(b["om"][0:96, m, :]), start=False, stop=m == 2, skip_group_check=True)
                    ins.then_inc(o_ready, 1)

                turn_sums(0, NB + 1)
                with pe.Fori(0, NT // 2) as i:
                    for s in range(2):
                        turn_sums(1 - s, i * 2 + (NB + s + 2))
                        outputs(s, i * 2 + (NB + s + 1), i * 2 + (NB + s + 1))
                outputs(0, NB + NT, NB + NT)
                stage(pe, stage_of(L, 4))

        @block.vector
        def _(dve):
            step = Count(dve_step)

            def then(ins):
                step.up(ins)
                dve.wait_ge(dve_step, step.n)

            dve.sem_inc(x_ready, 8)
            dve.sem_inc(copies_done, 8)
            dve.sem_inc(prod_free, 4)
            dve.sem_inc(summed, 2)
            dve.sem_inc(u_ready, 2)
            dve.sem_inc(node_x, 2)
            dve.sem_inc(payload_ready, 2)
            dve.memset(eps, 1e-5)
            dve.memset(ones_e[0:EP, :], 1.0)
            dve.memset(slot_d[0:EP, :], 0.0)
            then(dve.memset(slot_s[0:EP, :], 0.0))
            dve.wait_ge(const_in, 16)
            dve.wait_ge(idx_in, 32)
            bval = lambda k: const[0:EP, bass.ds(NC_BUCKET + k, 1)]
            for o, (idx, slot, addr, low) in enumerate(((idx_d, slot_d, addr_d, low_d), (idx_s, slot_s, addr_s, low_s))):
                dve.tensor_scalar(itmp[0][0:EP, :], idx[0:EP, :], 7, None, ALU.arith_shift_right)
                then(dve.tensor_scalar(itmp[1][0:EP, :], idx[0:EP, :], 127, None, ALU.bitwise_and))
                dve.tensor_copy(bucket[0:EP, :], itmp[0][0:EP, :])
                then(dve.tensor_scalar(low[0:EP, :], itmp[1][0:EP, :], 1.0, None, ALU.add))
                n0 = step.n
                with dve.Fori(0, NT) as k:
                    dve.wait_ge(dve_step, k + n0)
                    dve.tensor_scalar(onehot_b[0:EP, :], bucket[0:EP, :], bval(k), 0.0, ALU.is_equal, ALU.add,
                                      accum_out=totals[0:EP, bass.ds(k, 1)]).then_inc(dve_step, 1)
                step.n += NT
                dve.wait_ge(dve_step, step.n)
                dve.drain().then_inc(totals_done, 1)
                dve.wait_ge(offsets_done, o + 1)
                then(dve.tensor_scalar(cnt_i, bank[:, 1, 0:NT], 255.0, None, ALU.add))
                then(dve.tensor_scalar(cnt_i, cnt_i, 8, None, ALU.arith_shift_right))
                then(dve.tensor_copy(cnt_f, cnt_i))
                then(dve.tensor_tensor_scan(tend, ones[:, 0:NT], cnt_f, 0.0, ALU.mult, ALU.add))
                then(dve.tensor_tensor(basef, tend, cnt_f, ALU.subtract))
                then(dve.tensor_scalar(basef, basef, 256.0, -1.0, ALU.mult, ALU.add))
                then(dve.tensor_tensor(offs[0:EP, :], bank[0:EP, 0, 0:NT], basef[0:EP, :], ALU.add))
                for j in range(STEPC):
                    then(dve.tensor_scalar(step_cmp, tend, const[:, NC_STEP + j:NC_STEP + j + 1], 0.0, ALU.is_le, ALU.add,
                                           accum_out=step_f[:, j:j + 1]))
                if o == 1:
                    dve.wait_ge(step_out, 16)
                then(dve.tensor_scalar(step_i, step_f, float(NT - 1), None, ALU.min))
                dve.drain().then_inc(table_done, 1)
                n0 = step.n
                with dve.Fori(0, NT) as k:
                    dve.wait_ge(dve_step, k * 4 + n0)
                    dve.tensor_scalar(onehot_b[0:EP, :], bucket[0:EP, :], bval(k), None, ALU.is_equal).then_inc(dve_step, 1)
                    dve.wait_ge(dve_step, k * 4 + (n0 + 1))
                    dve.tensor_tensor_scan(scan_b[0:EP, :], ones_e[0:EP, :], onehot_b[0:EP, :], offs[0:EP, bass.ds(k, 1)],
                                           ALU.mult, ALU.add).then_inc(dve_step, 1)
                    dve.wait_ge(dve_step, k * 4 + (n0 + 2))
                    dve.tensor_tensor(scan_b[0:EP, :], scan_b[0:EP, :], onehot_b[0:EP, :], ALU.mult).then_inc(dve_step, 1)
                    dve.wait_ge(dve_step, k * 4 + (n0 + 3))
                    dve.tensor_tensor(slot[0:EP, :], slot[0:EP, :], scan_b[0:EP, :], ALU.add).then_inc(dve_step, 1)
                step.n += 4 * NT
                dve.wait_ge(dve_step, step.n)
                s_i, hi_i, mid_i = (t[0:EP, :] for t in itmp)
                then(dve.tensor_copy(s_i, slot[0:EP, :]))
                dve.tensor_scalar(hi_i, s_i, -512, None, ALU.bitwise_and)
                dve.tensor_scalar(mid_i, s_i, 127, 2, ALU.bitwise_and, ALU.logical_shift_left)
                then(dve.tensor_scalar(addr[0:EP, :], s_i, 7, 3, ALU.arith_shift_right, ALU.bitwise_and))
                then(dve.tensor_tensor(hi_i, hi_i, mid_i, ALU.add))
                then(dve.tensor_tensor(addr[0:EP, :], addr[0:EP, :], hi_i, ALU.add))
                if o == 0:
                    stage(dve, 1)
            dve.memset(tail_f[0:EP, EC:EC + HC, :], 0.0)
            dve.memset(tail_i[0:EP, EC:EC + HC, :], 0)
            dve.tensor_copy(tail_f[0:EP, 0:EC, 3:4], low_s[0:EP, :].rearrange("p (c o) -> p c o", o=1))
            dve.tensor_copy(tail_i[0:EP, 0:EC, 0:1], idx_d[0:EP, :].rearrange("p (c o) -> p c o", o=1))
            dve.tensor_copy(tail_i[0:EP, 0:EC, 1:2], addr_s[0:EP, :].rearrange("p (c o) -> p c o", o=1))
            dve.wait_ge(vec_root, 1)
            then(dve.reciprocal(vec_norm[0:EP, 2, :], vec_norm[0:EP, 1, :]))
            dve.tensor_tensor(tail_f[0:EP, 0:EC, 0:3], vec[0:EP, :, :],
                              vec_norm[0:EP, 2, :].rearrange("p (c o) -> p c o", o=1).to_broadcast([EP, EC, 3]), ALU.mult)
            stage(dve, 2)

            for L, c in enumerate(LAYERS):
                b = B[L]
                mw, xw, wn = c["mw"], c["xw"], c["wn"]
                if L == 0:
                    dve.tensor_tensor(attr_sq, nv[:, 0, :], nv[:, 0, :], ALU.mult)
                    dve.tensor_tensor(attr_mask[:, 0, :], nv[:, 0, :], nv[:, 2, :], ALU.mult)
                    dve.tensor_tensor(attr_mask[:, 1, :], nv[:, 1, :], nv[:, 2, :], ALU.mult)
                dve.wait_ge(weights_in, loads_to[L])
                lo, hi = b["ws"][:, 0, :], b["ws"][:, 1, :]

                def scaled(dst, src, f):
                    dve.tensor_scalar(dst, src, float(f), None, ALU.mult)

                def comps(dst, src, f, m=None):
                    d = dst.rearrange("p (v m) -> p m v", m=3)
                    if m is None:
                        dve.tensor_scalar(d, src.rearrange("p (m v) -> p m v", m=3), float(f), None, ALU.mult)
                    else:
                        dve.tensor_scalar(d[:, m, :], src, float(f), None, ALU.mult)

                r3 = 3.0 ** -0.5
                if L in (0, 3):
                    i0, i1, i9 = 64.0 ** -0.5, 32.0 ** -0.5, 96.0 ** -0.5
                    g9 = i9 * (1.0 if L == 0 else 32.0 ** -0.5)
                    scaled(b["ps"][0:64, 0:128], lo[0:64, 0:128], i0)
                    scaled(b["pv"][0:96, 0:96], hi[0:96, 0:96], i1)
                    comps(b["pv"][0:96, 96:192], hi[0:96, 96:192], i1)
                    for g in range(2):
                        scaled(b["w2"][64 * g:64 * g + 64, 192 * g:192 * g + 192], hi[64 * g:64 * g + 64, 192:384], 0.125)
                    scaled(b["oa"][0:64, 1:65], lo[0:64, 128:192], g9)
                    scaled(b["oa"][0:64, 0:1], lo[0:64, 192:193], g9)
                    scaled(b["oa"][64:96, 1:65], lo[64:96, 128:192], g9 * r3)
                    scaled(b["oa"][64:96, 0:1], lo[64:96, 192:193], g9 * r3)
                    for m in range(3):
                        comps(b["om"][0:96, m, 65:161], lo[0:96, 193:225], g9, m)
                if L == 1:
                    import math
                    cs, cx = math.sin(math.pi / 8), math.cos(math.pi / 8)
                    for a in range(2):
                        scaled(b["ps"][0:64, 128 * a:128 * a + 64], lo[0:64, 128 * a:128 * a + 64], 1.0)
                        scaled(b["ps"][0:64, 128 * a + 64:128 * a + 128], lo[0:64, 128 * a + 64:128 * a + 128], cs)
                        scaled(b["pv"][0:96, 192 * a:192 * a + 96], hi[0:96, 192 * a:192 * a + 96], 1.0)
                        comps(b["pv"][0:96, 192 * a + 96:192 * a + 192], hi[0:96, 192 * a + 96:192 * a + 192], cs)
                    dve.wait_ge(offsets_done, 3)
                    dve.tensor_copy(lo[0:96, 256:640], bank[0:96, 0, 0:384]).then_inc(totals_done, 1)
                    dve.wait_ge(offsets_done, 4)
                    g = cx / 4.0
                    for a in range(2):
                        o0 = 160 * a
                        scaled(b["oa"][0:64, o0:o0 + 64], bank[0:64, 1, 64 * a:64 * a + 64], g)
                        scaled(b["oa"][64:96, o0:o0 + 64], bank[64:96, 1, 64 * a:64 * a + 64], g * r3)
                        for m in range(3):
                            comps(b["om"][0:96, m, o0 + 64:o0 + 160], bank[0:96, 1, 128 + 64 * a:160 + 64 * a], g, m)
                if L == 2:
                    g, s3 = 1.0 / 32.0, 3.0 ** 0.5
                    scaled(b["ps"][0:64, 0:160], lo[0:64, 0:160], 1.0)
                    scaled(b["pv"][0:96, 0:96], hi[0:96, 0:96], 1.0)
                    comps(b["pv"][0:96, 96:192], hi[0:96, 96:192], 1.0)
                    scaled(b["oa"][0:64, 0:96], lo[0:64, 160:256], g)
                    for m in range(3):
                        comps(b["ob"][32 * m:32 * m + 32, 96:192], lo[32 * m:32 * m + 32, 288:320], g, m)
                        comps(b["om"][0:64, m, 96:192], lo[0:64, 256:288], g * s3, m)
                        scaled(b["om"][64:96, m, 0:96], lo[64:96, 160:256], g)
                        for q, comp in enumerate([k for k in range(3) if k != m]):
                            sign, to = (1.0, (m + 1) % 3) if comp == (m + 2) % 3 else (-1.0, (m + 2) % 3)
                            comps(b["oc"][32 * q:32 * q + 32, m, 96:192], lo[32 * q:32 * q + 32, 320:352], sign * g * s3 * 2.0 ** -0.5, to)
                stage(dve, stage_of(L, 0))

                sq = arena[:, b["agg_off"]:b["agg_off"] + NT * D]
                sq3d = sq.rearrange("p (t d) -> p t d", d=D)
                then(dve.tensor_reduce(ln_sum, x, AX_X, ALU.add))
                then(dve.tensor_scalar(ln_mean, ln_sum, -1.0 / D, None, ALU.mult))
                mean_b = ln_mean.rearrange("p (t o) -> p t o", o=1).to_broadcast([P, NT, D])
                dve.tensor_tensor(sq3d, x, mean_b, ALU.add).then_inc(ln_a, 1)
                dve.wait_ge(ln_b, 2 * L + 1)
                dve.tensor_reduce(ln_sq, sq3d, AX_X, ALU.add).then_inc(ln_a, 1)
                dve.wait_ge(ln_b, 2 * L + 2)
                then(dve.reciprocal(ln_rstd, ln_rstd))
                dve.tensor_tensor(ln_bias, ln_mean, ln_rstd, ALU.mult)
                stage(dve, stage_of(L, 1))

                NB = NT * L

                def evacuate(s, k):
                    dve.wait_ge(hT_ready, k + 2)
                    dve.tensor_copy(b["hTs"][s][0:64, :], bank[0:64, s, 0:P])
                    dve.tensor_copy(b["hTv"][s][0:96, :], bank[0:96, s, P:2 * P]).then_inc(hT_sb, 1)

                def finish(t, s, k, kout, ks):
                    dve.wait_ge(f_ready, k)
                    if kout is not None:
                        dve.wait_ge(table_out[s], kout)
                    u, f = b["u"][s], bank[:, 4 + 2 * s, :]
                    if L == 1:
                        dve.wait_ge(f_tmp, ks)
                        dve.scalar_tensor_tensor(out=u[:, 0:320], in0=f[:, 0:320], scalar=arena_col(nv_off, t), in1=b["utmp"][s],
                                                 op0=ALU.mult, op1=ALU.add).then_inc(u_ready, 1)
                    elif L == 2:
                        dve.tensor_copy(u[:, 0:352], f[:, 0:352]).then_inc(u_ready, 1)
                    else:
                        dve.tensor_scalar(u[:, 0:320], f[:, 0:320], arena_col(nv_off, t), None, ALU.mult).then_inc(u_ready, 1)
                    if L != 2:
                        dve.wait_ge(u_ready, k + 2)
                        dve.tensor_tensor(x_tile(t), x_tile(t), u[:, 160:320], ALU.add)

                per = 32 if L == 2 else 16
                evacuate(0, NB + 1)
                for t in range(2):
                    evacuate(1 - t % 2, NB + t + 2)
                    finish(t, t % 2, NB + t + 1, out_count(L, t % 2) if L else None, t + 1)
                with dve.Fori(0, NT // 2 - 1) as i:
                    for s in range(2):
                        evacuate(1 - s, i * 2 + (NB + s + 4))
                        finish(i * 2 + (s + 2), s, i * 2 + (NB + s + 3), i * per + (out_count(L, s) + per), i * 2 + (s + 3))
                finish(NT - 1, 0, NB + NT, out_count(L, 0) + per * (NT // 2), NT)
                stage(dve, stage_of(L, 2))

                QB, PB = (QUADS + 2) * L, (PAIRS + 1) * L
                rw = c["rows"]

                J = (PAIRS + 1) * min(L, 2)

                def products013(rp, q, gs, s, k_gath, k_w):
                    k = k_w - PB + J
                    dve.wait_ge(gath_in[gs], k_gath)
                    X, G, E0, esh, dot = b["X"][s], b["gath"][gs], b["E0"][gs], b["esh"][s], b["dot"][s]
                    W = bank[:, 2 + s, 0:2 * wn].rearrange("p (g w) -> p g w", w=wn)
                    rows, onehot = b["rows"][q][:, 2 * rp:2 * rp + 2, :], b["S"][s][:, :, 0, :]
                    sh = lambda m, n, w: rows[:, :, rw["sh"] + m:rw["sh"] + m + n].unsqueeze(3).to_broadcast([P, 2, n, w])
                    by_m = lambda a: a.rearrange("p g (m v) -> p g m v", m=3)
                    dve.tensor_tensor(esh, by_m(G[:, :, 64:160]), sh(1, 3, V), ALU.mult).then_inc(dot_step, 1)
                    dve.wait_ge(w_ready, k_w)
                    w1e0 = X[:, :, W1E0:W1E0 + 64]
                    dve.tensor_tensor(w1e0, W[:, :, 64:128], G[:, :, 0:64], ALU.mult).then_inc(first_products, 1)
                    dve.tensor_tensor(onehot, iota.unsqueeze(1).to_broadcast([P, 2, P]),
                                      rows[:, :, rw["dl"]:rw["dl"] + 1].to_broadcast([P, 2, P]), ALU.is_equal).then_inc(onehot_ready, 1)
                    dve.wait_ge(dot_step, k * 2 - 1)
                    dve.tensor_reduce(dot, esh.rearrange("p g m v -> p g v m"), AX_X, ALU.add).then_inc(dot_step, 1)
                    dve.wait_ge(e_scaled, k)
                    Xv = by_m(X[:, :, VM0:VM0 + 288])
                    dve.tensor_tensor(X[:, :, 0:64], W[:, :, 0:64], E0[:, :, 0:64], ALU.mult)
                    dve.tensor_tensor(Xv[:, :, :, 64:96], W[:, :, 128:160].unsqueeze(2).to_broadcast([P, 2, 3, V]),
                                      by_m(E0[:, :, 64:160]), ALU.mult)
                    dve.wait_ge(dot_step, k * 2)
                    dve.tensor_tensor(X[:, :, 64:96], W[:, :, 160:192], dot, ALU.mult).then_inc(prod_free, 1)
                    dve.wait_ge(first_products, k_w)
                    dve.tensor_tensor(Xv[:, :, 0:2, 0:64], w1e0.unsqueeze(2).to_broadcast([P, 2, 2, 64]), sh(1, 2, 64), ALU.mult).then_inc(x_ready, 1)

                def products2(rp, q, gs, s, k_gath, k_w):
                    dve.wait_ge(gath_in[gs], k_gath)
                    dve.wait_ge(w_ready, k_w)
                    X, G = b["X"][s], b["gath"][gs]
                    W = bank[:, 2 + s, 0:2 * wn].rearrange("p (g w) -> p g w", w=wn)
                    rows, Sx = b["rows"][q][:, 2 * rp:2 * rp + 2, :], b["S"][s]
                    plain = 0
                    dve.tensor_tensor(Sx[:, :, plain, :], iota.unsqueeze(1).to_broadcast([P, 2, P]),
                                      rows[:, :, rw["dl"]:rw["dl"] + 1].to_broadcast([P, 2, P]), ALU.is_equal).then_inc(onehot_ready, 1)
                    dve.tensor_tensor(X[:, :, 0:320].rearrange("p g (k w) -> p g k w", k=2)[:, :, :, 0:64],
                                      W[:, :, 0:128].rearrange("p g (k w) -> p g k w", k=2),
                                      G[:, :, 0:64].unsqueeze(2).to_broadcast([P, 2, 2, 64]), ALU.mult).then_inc(first_products, 1)
                    e1 = G[:, :, 64:160]
                    wb = lambda o, n: W[:, :, o:o + 32].unsqueeze(2).to_broadcast([P, 2, n, 32])
                    e1m = e1.rearrange("p g (m v) -> p g m v", m=3)
                    dve.tensor_tensor(X[:, :, 64:160].rearrange("p g (m v) -> p g m v", m=3), wb(128, 3), e1m, ALU.mult)
                    Xm = X[:, :, 160:160 + 3 * mw].rearrange("p g (m w) -> p g m w", m=3)
                    ins = dve.tensor_tensor(Xm[:, :, :, 64:96], wb(160, 3), e1m, ALU.mult)
                    for m, (c0, stp) in enumerate(((1, 1), (0, 2), (0, 1))):
                        ins = dve.tensor_tensor(Xm[:, :, m, 96:160].rearrange("p g (a v) -> p g a v", a=2), wb(192, 2),
                                                e1m[:, :, c0:c0 + stp + 1:stp, :], ALU.mult)
                    ins.then_inc(prod_free, 1)
                    n, k0 = 1, 1
                    dve.wait_ge(onehot_ready, k_w)
                    dve.tensor_tensor(Sx[:, :, k0:k0 + n, :], Sx[:, :, plain:plain + 1, :].to_broadcast([P, 2, n, P]),
                                      rows[:, :, rw["sh"]:rw["sh"] + n].unsqueeze(3).to_broadcast([P, 2, n, P]), ALU.mult).then_inc(x_ready, 1)

                def add(s, tile, k_sums, k_prev):
                    dve.wait_ge(sums_ready, k_sums)
                    dve.wait_ge(summed, k_prev)
                    a = agg_tile(L, tile)
                    if L == 2:
                        a = a.rearrange("p (h w) -> p h w", h=2)
                        sm = bank[:, 4 + 2 * s:6 + 2 * s, 0:320]
                    else:
                        sm = bank[:, 4 + 2 * s, 0:c["aw"]]
                    dve.tensor_tensor(a, a, sm, ALU.add).then_inc(summed, 1)

                products = products2 if L == 2 else products013
                brow = bucket_rows[1 if L == 2 else 0]
                def tail(h, i):
                    if not (isinstance(i, int) and L == 0):
                        dve.wait_ge(sent[h], i * (16 * HC) + 16 * HC * MOVING * L)
                    cols = bass.ds(i * (2 * HC) + (2 * HC * MOVING * L + HC * h), HC)
                    dve.tensor_copy(pay_s[h][0:EP, :, 64:68], tail_f[0:EP, cols, :])
                    dve.tensor_copy(pay_s[h].bitcast(I32)[0:EP, :, 68:70], tail_i[0:EP, cols, :]).then_inc(tail_ready[h], 1)

                def iteration(i, moving):
                    for r in range(8):
                        if moving and r % HC == 0:
                            tail(1 - r // HC, i + r // HC)
                        n = r + 1
                        products(n % 2, (n // 2) % 4, n % 4, n % 2,
                                 i * 64 + 32 * (gath_base(L, n % 4) + 1 + n // 4), i * 8 + (PB + n + 1))
                        tile = dve.value_load(brow[0:1, bass.ds(i * 8 + r, 1)], min_val=0, max_val=NT - 1)
                        add(r % 2, tile, i * 8 + (PAIRS * L + r + 1), i * 8 + (PAIRS * L + r + 2))

                if L == 0:
                    for s in range(2):
                        dve.memset(b["X"][s][:, :, COUNT:COUNT + 1], 1.0)
                if L < 2:
                    tail(0, 0)
                products(0, 0, 0, 0, 32 * (gath_base(L, 0) + 1), PB + 1)
                if L < 2:
                    iteration(0, True)
                    with dve.Fori(1, MOVING) as i:
                        iteration(i, True)
                    with dve.Fori(MOVING, ITERS) as i:
                        iteration(i, False)
                else:
                    with dve.Fori(0, ITERS) as i:
                        iteration(i, False)
                stage(dve, stage_of(L, 3))

                if L == 0:
                    counts = b["agg"][:, :, COUNT]
                    then(dve.tensor_scalar(recip_count, counts, 1.0, None, ALU.max))
                    dve.reciprocal(recip_count, recip_count).then_inc(counts_ready, 1)

                n0 = step.n

                def chunkB(s, k):
                    dve.wait_ge(agg_T, k + 2)
                    if L == 2:
                        dve.tensor_copy(b["aTA"][s][0:64, :, :], bank[0:64, 2 * s, :].rearrange("p (a b) -> p a b", b=P)).then_inc(aggA_sb, 1)
                    dve.tensor_copy(b["aTB"][s][0:96, :, :], bank[0:96, 2 * s + 1, :].rearrange("p (a b) -> p a b", b=P)).then_inc(aggB_sb, 1)

                def result(t, s, k, ks, kk, k_skip):
                    dve.wait_ge(o_ready, k)
                    o, u = bank[:, 4 + s, :], b["u"][s]
                    xt = x_tile(t)
                    if L in (0, 3):
                        sc = b["scal"][s][:, 0:1]
                        dve.tensor_scalar(sc, o[:, 0:1], arena_col(sq_off, t), None, ALU.mult).then_inc(dve_step, 1)
                        dve.wait_ge(dve_step, ks)
                        dve.scalar_tensor_tensor(out=xt, in0=o[:, 1:161], scalar=sc, in1=xt, op0=ALU.mult, op1=ALU.add).then_inc(node_x, 1)
                    if L == 1:
                        dve.wait_ge(o_tmp, kk)
                        dve.scalar_tensor_tensor(out=u[:, 0:160], in0=o[:, 0:160], scalar=arena_col(mask_off, t), in1=b["utmp"][s][:, 0:160],
                                                 op0=ALU.mult, op1=ALU.add).then_inc(dve_step, 1)
                        dve.wait_ge(dve_step, ks)
                        dve.tensor_tensor(xt, xt, u[:, 0:160], ALU.add).then_inc(node_x, 1)
                    if L == 2:
                        dve.wait_ge(skip_in[s], k_skip)
                        dve.tensor_tensor(u[:, 0:192], o[:, 0:192], b["sk"][s], ALU.add).then_inc(o_y, 1)
                        dve.wait_ge(o_gate, kk)
                        gt = b["utmp"][s]
                        dve.tensor_tensor(u[:, 192:256], u[:, 0:64], gt[:, 0:64], ALU.mult)
                        dve.tensor_tensor(u[:, 256:352].rearrange("p (v m) -> p v m", m=3), u[:, 96:192].rearrange("p (v m) -> p v m", m=3),
                                          gt[:, 64:96].unsqueeze(2).to_broadcast([P, 32, 3]), ALU.mult).then_inc(dve_step, 1)
                        dve.wait_ge(dve_step, ks)
                        dve.tensor_tensor(xt, xt, u[:, 192:352], ALU.add).then_inc(node_x, 1)

                chunkB(0, NB + 1)
                with dve.Fori(0, NT // 2) as i:
                    for s in range(2):
                        chunkB(1 - s, i * 2 + (NB + s + 2))
                        result(i * 2 + s, s, i * 2 + (NB + s + 1), i * 2 + (n0 + s + 1), i * 2 + (s + 1), i * 16 + 16)
                result(NT - 1, 0, NB + NT, n0 + NT, NT, 16 * (NT // 2 + 1))
                step.n += NT
                stage(dve, stage_of(L, 4))


def kernel(**inputs):
    import numpy as _np
    import concourse.bacc as _bacc
    from concourse import mybir as _mybir
    from concourse.bass_utils import run_bass_kernel_spmd as _run

    nc = _bacc.Bacc("TRN2", target_bir_lowering=False, num_devices=1)
    arrays, aps = {}, {}
    host = dict(inputs)
    host["consts"] = shape_constants()
    for name, value in host.items():
        a = _np.ascontiguousarray(value)
        arrays[f"in_{name}_dram"] = a
        aps[name] = nc.dram_tensor(f"in_{name}_dram", a.shape, _mybir.dt.from_np(a.dtype), kind="ExternalInput").ap()
    out = nc.dram_tensor("out_0_dram", (N, D), F32, kind="ExternalOutput").ap()
    gnn_kernel(nc, aps, out)
    r = _run(nc, [arrays], core_ids=[0])
    return r.results[0]["out_0_dram"]
```

```python
from contextlib import ExitStack

import concourse.bass as bass
from concourse import mybir

ALU = mybir.AluOpType
ACT = mybir.ActivationFunctionType
F32 = mybir.dt.float32
I32 = mybir.dt.int32
I16 = mybir.dt.int16
AX_X = mybir.AxisListType.X

N, E, D = 6250, 100000, 160
S, V = 64, 32
P = 128
NT = -(-N // P)
NREST = N - (NT - 1) * P
EP = 125
EC = E // EP
PAIRS = -(-((E + NT * 255) // 256) // 8) * 8
QUADS = PAIRS // 2
ITERS = PAIRS // 8
SLOTS = (QUADS + 2) * 512
CC = 25
CHUNKS = EC // CC
HC = 4
MOVING = EC // (2 * 2 * HC)

ROW_D = dict(w=40, a16=0, a10=16, a8=26, sh=34, dl=38, idx=39)
ROW_S = dict(w=71, a64=0, sh=64, dl=69, idx=70)
LAYERS = [
    dict(aw=385, xw=450, col=ROW_D["a16"], by_act=1, wn=192, rows=ROW_D, nout=161),
    dict(aw=384, xw=450, col=ROW_D["a10"], by_act=1, wn=192, rows=ROW_D, nout=320),
    dict(aw=480, xw=544, col=ROW_S["a64"], by_act=3, wn=224, rows=ROW_S, nout=192),
    dict(aw=384, xw=450, col=ROW_D["a8"], by_act=2, wn=192, rows=ROW_D, nout=161),
]
VM0, COUNT, CROSS = 96, 384, 384
PAIR_STEP = ROW_D["w"]
PAIR_ROWS = PAIR_STEP + ROW_D["sh"]
NC_IDENT, NC_TRI, NC_IOTA, NC_ONES, NC_BUCKET, NC_STEP = 0, 128, 256, 384, 512, 512 + NT
STEPC = -(-PAIRS // P)
NCONST = NC_STEP + STEPC


def shape_constants():
    import numpy as np

    c = np.zeros((P, NCONST), np.float32)
    c[:, NC_IDENT:NC_IDENT + P] = np.eye(P)
    c[:, NC_TRI:NC_TRI + P] = np.triu(np.ones((P, P)), 1)
    c[:, NC_IOTA:NC_IOTA + P] = np.arange(1, P + 1)
    c[:, NC_ONES:NC_ONES + P] = 1.0
    c[:, NC_BUCKET:NC_BUCKET + NT] = np.arange(NT)
    c[:, NC_STEP:] = np.arange(STEPC)[None, :] * P + np.arange(P)[:, None]
    return c


def gnn_kernel(nc, A, out):
    with ExitStack() as ctx:
        sem = lambda name: ctx.enter_context(nc.semaphore(name))

        rows_d = nc.dram_tensor("rows_by_dst", (SLOTS, ROW_D["w"]), F32).ap()
        rows_s = nc.dram_tensor("rows_by_src", (SLOTS, ROW_S["w"]), F32).ap()
        table = nc.dram_tensor("node_table", (NT * P, D), F32).ap()
        skip_dram = nc.dram_tensor("node_skip", (NT * P, 192), F32).ap()
        bucket_dram = nc.dram_tensor("bucket_of_pair", (2, STEPC * P), I16).ap()

        TOTAL = 51900
        arena = ctx.enter_context(nc.sbuf_tensor("arena", [P, TOTAL], F32))
        top = [0]

        def cut(*shape):
            n = 1
            for s in shape:
                n *= s
            off = top[0]
            top[0] += n
            assert top[0] <= TOTAL, (top[0], TOTAL)
            v = arena[:, off:off + n]
            if len(shape) == 2:
                v = v.rearrange("p (a b) -> p a b", b=shape[1])
            elif len(shape) == 3:
                v = v.rearrange("p (a b c) -> p a b c", b=shape[1], c=shape[2])
            elif len(shape) == 4:
                v = v.rearrange("p (a b c d) -> p a b c d", b=shape[1], c=shape[2], d=shape[3])
            return v

        const = cut(NCONST)
        ident = const[:, NC_IDENT:NC_IDENT + P]
        tri = const[:, NC_TRI:NC_TRI + P]
        iota = const[:, NC_IOTA:NC_IOTA + P]
        ones = const[:, NC_ONES:NC_ONES + P]
        X0 = top[0]
        x = cut(NT, D)
        nv = cut(3, NT)
        recip_count = cut(NT)
        attr_sq = cut(NT)
        attr_mask = cut(2, NT)
        ln_sum, ln_mean, ln_sq, ln_rstd, ln_bias = (cut(NT) for _ in range(5))
        eps = cut(1)
        bucket_rows = [cut(STEPC * P // 2).bitcast(I16) for _ in range(2)]
        layer_base = top[0]

        idx_d, idx_s = cut(EC).bitcast(I32), cut(EC).bitcast(I32)
        slot_d, slot_s = cut(EC), cut(EC)
        addr_d, addr_s = cut(EC).bitcast(I32), cut(EC).bitcast(I32)
        low_d, low_s = cut(EC), cut(EC)
        vec, vec_sq = cut(EC, 3), cut(EC, 3)
        vec_norm = cut(3, EC)
        bucket = cut(EC)
        itmp = [cut(EC).bitcast(I32) for _ in range(3)]
        onehot_b, scan_b, ones_e = cut(EC), cut(EC), cut(EC)
        totals, offs, cnt_f, tend, basef = (cut(NT) for _ in range(5))
        cnt_i = cut(NT).bitcast(I32)
        step_cmp, step_f = cut(NT), cut(STEPC)
        step_i = cut(STEPC).bitcast(I16)[:, 0:STEPC]
        zrow = cut(P * 16)
        st16, st10, st8, st4 = ([cut(CC, w) for _ in range(2)] for w in (16, 10, 8, 4))
        pay_d = [cut(CC, ROW_D["w"]) for _ in range(2)]
        adr = [cut(CC).bitcast(I32) for _ in range(2)]
        of_bucket, distance, slots_in = ([cut(EC) for _ in range(2)] for _ in range(3))
        sort_top = top[0]

        edge_f = (EC + HC) * 6
        keep = edge_f + (EC + HC) * 2 + 2 * HC * (ROW_S["w"] + 1)
        top[0] = TOTAL - keep
        KEPT = top[0]
        tail_f = cut(EC + HC, 6)
        tail_i = cut(EC + HC, 2).bitcast(I32)
        pay_s = [cut(HC, ROW_S["w"] + 1) for _ in range(2)]
        assert sort_top + (NT + 1) // 2 * D <= KEPT

        B = []
        for L, c in enumerate(LAYERS):
            top[0] = layer_base
            b = {}
            b["agg_off"] = top[0]
            b["agg"] = cut(NT, c["aw"])
            b["w1"] = {0: lambda: cut(128), 1: lambda: cut(2, 100), 2: lambda: cut(64), 3: lambda: cut(128)}[L]()
            b["w2"] = cut(c["wn"] if L == 1 else 2 * c["wn"])
            if L == 3:
                b["wmid"] = cut(128)
            b["ps"] = cut(256 if L == 1 else 160)
            b["pv"] = cut(384 if L == 1 else 192)
            b["oa"] = cut(c["nout"])
            b["om"] = cut(3, c["nout"])
            if L == 2:
                b["oc"] = cut(c["nout"])
            rings = top[0]
            b["rows"] = [cut(4, c["rows"]["w"]) for _ in range(4)]
            b["gath"] = [cut(2, D) for _ in range(4)]
            b["X"] = [cut(2, c["xw"]) for _ in range(2)]
            b["S"] = [cut(2, P) for _ in range(2)]
            b["esh"] = [cut(2, 3, V) for _ in range(2)]
            b["dot"] = [cut(2, V) for _ in range(2)]
            if L == 2:
                b["cA"], b["cB"] = ([cut(2, 3, V) for _ in range(4)] for _ in range(2))
                b["cC"] = [cut(2, 3, V) for _ in range(2)]
            else:
                b["E0"] = [cut(2, D) for _ in range(4)]
            b["tT"] = [cut(4 if L == 2 else 2, P) for _ in range(2)]
            b["hT"] = [cut(4 if L == 1 else 2, P) for _ in range(2)]
            if L == 3:
                b["h1T"] = [cut(2, P) for _ in range(2)]
            top[0] = rings
            b["h"] = [cut(D) for _ in range(2)]
            b["hTs"] = [cut(P) for _ in range(2)]
            b["hTv"] = [cut(P) for _ in range(2)]
            b["u"] = [cut(352) for _ in range(2)]
            b["utmp"] = [cut(320) for _ in range(2)]
            b["sk"] = [cut(192) for _ in range(2)]
            b["scal"] = [cut(8) for _ in range(2)]
            top[0] = rings
            b["_pad"] = cut(2 * D + 4 * P + 2 * 352 + 2 * 320 + 2 * 192 + 16)
            b["aggS"] = [cut(c["aw"]) for _ in range(2)]
            if L == 2:
                b["aTA"] = [cut(P) for _ in range(2)]
            b["aTB"] = [cut(4, P) for _ in range(2)]
            if L in (0, 1, 3):
                top[0] = max(top[0], rings + 8000)
            b["ws"] = cut(2, 640) if L != 2 else None
            assert L > 1 or top[0] <= KEPT
            B.append(b)
        B[2]["ws"] = arena[:, B[2]["agg_off"] + 20000:B[2]["agg_off"] + 21280].rearrange("p (a b) -> p a b", b=640)

        bank = ctx.enter_context(nc.psum_tensor("bank", [P, 8, 512], F32))

        stage_end = sem("stage_end")
        const_in = sem("const_in")
        idx_in, ones_set, zero_set = sem("idx_in"), sem("ones_set"), sem("zero_set")
        x_in = sem("x_in")
        weights_in = sem("weights_in")
        prefilled = sem("prefilled")
        dve_step, act_step = sem("dve_step"), sem("act_step")
        totals_done, offsets_done = sem("totals_done"), sem("offsets_done")
        bucket_onehot, bucket_distance, slots_masked, slots_added = (
            sem(n) for n in ("bucket_onehot", "bucket_distance", "slots_masked", "slots_added"))
        step_out, step_in = sem("step_out"), sem("step_in")
        table_done = sem("table_done")
        stage_in = [sem(f"stage_in{i}") for i in range(2)]
        payload_ready = sem("payload_ready")
        vec_in, vec_squared, vec_summed, vec_root = sem("vec_in"), sem("vec_squared"), sem("vec_summed"), sem("vec_root")
        attr64_in = [sem(f"attr64_in{i}") for i in range(2)]
        tail_ready = [sem(f"tail_ready{i}") for i in range(2)]
        sent = [sem(f"sent{i}") for i in range(2)]
        scattered = [sem(f"scattered{i}") for i in range(2)]
        counts_ready = sem("counts_ready")
        pool_steps = sem("pool_steps")
        rows_in = [sem(f"rows_in{i}") for i in range(4)]
        gath_in = [sem(f"gath_in{i}") for i in range(4)]
        prod_free = sem("prod_free")
        turned, turned_sb, hidden1, hidden1_sb, hidden2, hidden_sb = (
            sem(n) for n in ("turned", "turned_sb", "hidden1", "hidden1_sb", "hidden2", "hidden_sb"))
        e_scaled, dot_step = sem("e_scaled"), sem("dot_step")
        w_ready, first_products, copies_done, x_ready = sem("w_ready"), sem("first_products"), sem("copies_done"), sem("x_ready")
        sums_ready, summed = sem("sums_ready"), sem("summed")
        ln_a, ln_b = sem("ln_a"), sem("ln_b")
        h_ready, hT_ready, hT_sb, f_ready, f_tmp, u_ready, node_x = (
            sem(n) for n in ("h_ready", "hT_ready", "hT_sb", "f_ready", "f_tmp", "u_ready", "node_x"))
        table_out = [sem(f"table_out{i}") for i in range(2)]
        agg_zero = sem("agg_zero")
        agg_st, agg_T, aggA_sb, aggB_sb, o_ready, o_tmp, o_gate, o_y = (
            sem(n) for n in ("agg_st", "agg_T", "aggA_sb", "aggB_sb", "o_ready", "o_tmp", "o_gate", "o_y"))
        skip_in = [sem(f"skip_in{i}") for i in range(2)]
        out_done = sem("out_done")

        block = ctx.enter_context(nc.Block())
        ENGINES = 5

        def stage(e, n):
            e.drain().then_inc(stage_end, 1)
            e.wait_ge(stage_end, ENGINES * n)

        class Count:

            def __init__(self, s):
                self.s, self.n = s, 0

            def up(self, ins):
                ins.then_inc(self.s, 1)
                self.n += 1

        def weight_loads(L):
            b, c = B[L], LAYERS[L]
            lo, hi = b["ws"][:, 0, :], b["ws"][:, 1, :]
            r = []

            def spread(dst, w):
                for m in range(3):
                    r.append((dst[m:96:3, 32 * m:32 * m + 32], w))

            if L in (0, 3):
                p = f"L{L}_gnn_"
                r.append((lo[0:64, 0:64], A[p + "Wl1_0"]))
                r.append((lo[0:64, 64:128], A[p + "Wsc0"]))
                spread(hi[:, 0:96], A[p + "Wl1_1"])
                spread(hi[:, 96:192], A[p + "Wsc1"])
                r.append((lo[0:96, 128:192], A[p + "Wl2_s"]))
                r.append((lo[0:96, 192:193], A[p + "Wa"]))
                r.append((lo[0:96, 193:225], A[p + "Wl2_v"]))
            if L == 1:
                p = "L1_gnn_"
                r.append((lo[0:64, 0:64], A[p + "Ws_l1_a"]))
                r.append((lo[0:64, 64:128], A[p + "Ws_sc_a"]))
                r.append((lo[0:64, 128:192], A[p + "Ws_l1_c"]))
                r.append((lo[0:64, 192:256], A[p + "Ws_sc_c"]))
                spread(hi[:, 0:96], A[p + "Wv_l1_a"])
                spread(hi[:, 96:192], A[p + "Wv_sc_a"])
                spread(hi[:, 192:288], A[p + "Wv_l1_c"])
                spread(hi[:, 288:384], A[p + "Wv_sc_c"])
                for i, n in enumerate(("Ws_l2_a", "Ws_l2_c", "Wv_l2_a", "Wv_l2_c")):
                    r.append((lo[0:96, 256 + 96 * i:352 + 96 * i], A[p + n]))
                r.append((hi[0:96, 384:448], A[p + "Ws_l3"]))
                r.append((hi[0:96, 448:480], A[p + "Wv_l3"]))
            if L == 2:
                p = "L2_gnn_"
                r.append((lo[0:64, 0:64], A[p + "W_nl0"]))
                r.append((lo[0:64, 64:160], A[p + "W_skip0"]))
                spread(hi[:, 0:96], A[p + "W_nl1"])
                spread(hi[:, 96:192], A[p + "W_skip1"])
                r.append((lo[0:96, 160:256], A[p + "W_out_s"]))
                r.append((lo[0:96, 256:288], A[p + "W_out_v"][0:96, :]))
                for m in range(3):
                    r.append((lo[32 * m:32 * m + 32, 320:352], A[p + "W_out_v"][96:128, :]))
            if L == 0:
                for g in range(2):
                    at = PAIR_STEP * g + c["col"]
                    r.append((b["w1"][at:at + 16, 64 * g:64 * g + 64], A["L0_gnn_Wfc1"]))
                    r.append((hi[64 * g:64 * g + 64, 192:384], A["L0_gnn_Wfc2"]))
            if L == 1:
                for g in range(2):
                    at = PAIR_STEP * g + c["col"]
                    r.append((b["w1"][at:at + 10, g, :], A["L1_gnn_W_fc1"]))
                r.append((b["w2"][0:100, :], A["L1_gnn_W_fc2"]))
            if L == 2:
                r.append((b["w1"][0:64, :], A["L2_gnn_W_fc1"]))
                for g in range(2):
                    r.append((b["w2"][64 * g:64 * g + 64, 224 * g:224 * g + 224], A["L2_gnn_W_fc2"]))
            if L == 3:
                for g in range(2):
                    at = PAIR_STEP * g + c["col"]
                    r.append((b["w1"][at:at + 8, 64 * g:64 * g + 64], A["L3_gnn_Wfc1"]))
                    r.append((b["wmid"][64 * g:64 * g + 64, 64 * g:64 * g + 64], A["L3_gnn_Wfc2"]))
                    r.append((hi[64 * g:64 * g + 64, 192:384], A["L3_gnn_Wfc3"]))
            return r

        n_loads = [len(weight_loads(L)) for L in range(4)]
        loads_to = [16 * sum(n_loads[:L + 1]) for L in range(4)]

        def stage_of(L, k):
            return 2 + 4 * L + k

        tile_at = lambda t: bass.ds(X0 + t * D, D)
        x_tile = lambda t: arena[:, tile_at(t)]

        def agg_tile(L, t):
            return arena[:, bass.ds(B[L]["agg_off"] + t * LAYERS[L]["aw"], LAYERS[L]["aw"])]

        def out_count(upto, s):
            tiles = NT - NT // 2 if s == 0 else NT // 2
            return sum(16 * tiles * (2 if L == 2 else 1) for L in range(upto))

        def rows_base(L, q):
            return L * (ITERS + (1 if q < 2 else 0))

        def gath_base(L, s):
            return L * (2 * ITERS + (1 if s == 0 else 0))

        nv_off = X0 + NT * D
        recip_off = nv_off + 3 * NT
        sq_off = recip_off + NT
        mask_off = sq_off + NT
        ln_rstd_off = mask_off + 2 * NT + 3 * NT
        ln_bias_off = ln_rstd_off + NT

        def arena_col(off, t):
            return arena[:, off + t:off + t + 1] if isinstance(t, int) else arena[:, bass.ds(t + off, 1)]

        @block.sync
        def _(sp):
            sp.dma_start(const, A["consts"]).then_inc(const_in, 16)
            sp.dma_start(idx_d[0:EP, :], A["dst"].rearrange("(p c) -> p c", c=EC)).then_inc(idx_in, 16)
            sp.dma_start(idx_s[0:EP, :], A["src"].rearrange("(p c) -> p c", c=EC)).then_inc(idx_in, 16)
            sp.dma_start(vec[0:EP, :, :], A["edge_attr_3"].rearrange("(p c) w -> p c w", c=EC)).then_inc(vec_in, 16)
            sp.wait_ge(zero_set, 3)
            full = (NT - 1) * P
            sp.dma_start(x[:, 0:NT - 1, :], A["x"][0:full, :].rearrange("(t p) d -> p t d", p=P)).then_inc(x_in, 16)
            sp.dma_start(x[0:NREST, NT - 1, :], A["x"][full:N, :]).then_inc(x_in, 16)
            for rows, w in ((rows_d, ROW_D["w"]), (rows_s, ROW_S["w"])):
                per = SLOTS * w // P
                whole = per // 2048
                flat = rows.rearrange("(p r) w -> p (r w)", p=P)
                for k in range(0, whole):
                    sp.dma_start(flat[:, 2048 * k:2048 * k + 2048], zrow).then_inc(prefilled, 16)
                if per % 2048:
                    sp.dma_start(flat[:, 2048 * whole:per], zrow[:, 0:per % 2048]).then_inc(prefilled, 16)
            for i, name in enumerate(("node_vec1", "node_vec1_n2", "node_vec1_n3")):
                with nc.allow_non_contiguous_dma(reason="node scalars, one per partition"):
                    sp.dma_start(nv[:, i, 0:NT - 1], A[name][0:full, :].rearrange("(t p) o -> p (t o)", p=P)).then_inc(x_in, 16)
                    sp.dma_start(nv[0:NREST, i, NT - 1:NT], A[name][full:N, :]).then_inc(x_in, 16)
            sp.wait_ge(x_in, 16 * 8)
            n_fill = sum(-(-(SLOTS * w // P) // 2048) for w in (ROW_D["w"], ROW_S["w"]))
            sp.wait_ge(prefilled, 16 * n_fill)
            stage(sp, 1)

            def chunk(name, k):
                return A[name].rearrange("(p c) w -> p (c w)", c=EC)[:, bass.ds(k * (CC * A[name].shape[1]), CC * A[name].shape[1])]

            def turn_buckets(o):
                sp.wait_ge(table_done, o + 1)
                with nc.allow_non_contiguous_dma(reason="a short table"):
                    sp.dma_start(bucket_dram[o, :].rearrange("(c p) -> p c", p=P), step_i).then_inc(step_out, 16)
                sp.wait_ge(step_out, 16 * (o + 1))
                sp.dma_start(bucket_rows[o][0:1, :], bucket_dram[o:o + 1, :]).then_inc(step_in, 16)
                sp.wait_ge(step_in, 16 * (o + 1))

            def load_chunk(k, s, i):
                sp.wait_ge(payload_ready, i * 2 + (s + 1))
                for name, st in (("edge_attr_16", st16), ("edge_attr_10", st10), ("edge_attr_8", st8), ("edge_attr_4", st4)):
                    sp.dma_start(st[s][0:EP, :, :].rearrange("p c w -> p (c w)"), chunk(name, k)).then_inc(stage_in[s], 16)

            for s in range(2):
                load_chunk(s, s, 0)
            turn_buckets(0)
            with sp.Fori(1, CHUNKS // 2) as i:
                for s in range(2):
                    load_chunk(i * 2 + s, s, i)
            turn_buckets(1)
            stage(sp, 2)

            for L, c in enumerate(LAYERS):
                b = B[L]
                sp.wait_ge(agg_zero, 2 * L + 1)
                with nc.allow_non_contiguous_dma(reason="weights"):
                    for dst, srcw in weight_loads(L):
                        sp.dma_start(dst, srcw).then_inc(weights_in, 16)
                sp.wait_ge(weights_in, loads_to[L])
                stage(sp, stage_of(L, 1))

                def store(t, s, k):
                    sp.wait_ge(u_ready, k + 2)
                    sp.dma_start(table[bass.ds(t * P, P), :], b["u"][s][:, 0:D]).then_inc(table_out[s], 16)
                    if L == 2:
                        sp.dma_start(skip_dram[bass.ds(t * P, P), :], b["u"][s][:, 160:352]).then_inc(table_out[s], 16)

                with sp.Fori(0, NT // 2) as i:
                    for s in range(2):
                        store(i * 2 + s, s, i * 2 + (NT * L + s + 1))
                store(NT - 1, 0, NT * L + NT)
                for s in range(2):
                    sp.wait_ge(table_out[s], out_count(L + 1, s))
                stage(sp, stage_of(L, 2))

                R = rows_s if L == 2 else rows_d
                w = c["rows"]["w"]
                per_quad = R.rearrange("(q p u) w -> p q (u w)", p=P, u=4)

                def load(q, s, k):
                    sp.wait_ge(x_ready, k)
                    sp.wait_ge(copies_done, k)
                    sp.dma_start(b["rows"][s].rearrange("p a b -> p (a b)"), per_quad[:, q, :] if isinstance(q, int) else
                                 per_quad[:, bass.ds(q, 1), :].rearrange("p a b -> p (a b)")).then_inc(rows_in[s], 16)

                def load_attr64(h, i):
                    if not (isinstance(i, int) and L == 0):
                        sp.wait_ge(sent[h], i * (16 * HC) + 16 * HC * MOVING * L)
                    col = i * (2 * HC) + (2 * HC * MOVING * L + HC * h)
                    sp.dma_start(pay_s[h][0:EP, :, 0:64], A["edge_attr_64"].rearrange("(p c) w -> p c w", c=EC)[:, bass.ds(col, HC), :]
                                 ).then_inc(attr64_in[h], 16)

                def load_iteration(i, moving):
                    for s in range(4):
                        load(i * 4 + s, s, i * 8 + ((PAIRS + 1) * L + 2 * s + 2))
                        if moving and s in (0, 2):
                            load_attr64(s // 2, i)

                if L < 2:
                    load_iteration(0, True)
                    with sp.Fori(1, MOVING) as i:
                        load_iteration(i, True)
                    with sp.Fori(MOVING, ITERS) as i:
                        load_iteration(i, False)
                else:
                    with sp.Fori(0, ITERS) as i:
                        load_iteration(i, False)
                for s in range(2):
                    load(QUADS + s, s, (PAIRS + 1) * L + 2 * (QUADS + s) + 2)
                stage(sp, stage_of(L, 3))

                if L == 2:
                    def fetch(t, s, k):
                        if k is not None:
                            sp.wait_ge(o_y, k)
                        sp.dma_start(b["sk"][s], skip_dram[bass.ds(t * P, P), :]).then_inc(skip_in[s], 16)

                    fetch(0, 0, None)
                    fetch(1, 1, None)
                    with sp.Fori(0, NT // 2 - 1) as i:
                        for s in range(2):
                            fetch(i * 2 + (s + 2), s, i * 2 + (s + 1))
                    fetch(NT - 1, 0, NT - 2)
                    sp.wait_ge(o_y, NT)
                stage(sp, stage_of(L, 4))
            sp.dma_start(out[0:full, :].rearrange("(t p) d -> p t d", p=P), x[:, 0:NT - 1, :]).then_inc(out_done, 16)
            sp.dma_start(out[full:N, :], x[0:NREST, NT - 1, :]).then_inc(out_done, 16)
            sp.wait_ge(out_done, 32)

        @block.gpsimd
        def _(pool):
            pool.memset(x[:, NT - 1, :], 0.0).then_inc(zero_set, 1)
            pool.memset(nv, 0.0).then_inc(zero_set, 1)
            pool.memset(zrow, 0.0).then_inc(zero_set, 1)
            pool.wait_ge(vec_squared, 1)
            sq = lambda m: vec_sq[0:EP, :, m:m + 1].rearrange("p c o -> p (c o)")
            pool.tensor_tensor(vec_norm[0:EP, 0, :], sq(0), sq(1), ALU.add).then_inc(vec_summed, 1)
            pool.wait_ge(vec_summed, 1)
            pool.tensor_tensor(vec_norm[0:EP, 0, :], vec_norm[0:EP, 0, :], sq(2), ALU.add).then_inc(vec_summed, 1)

            def collect(k, s):
                pool.wait_ge(slots_masked, k + 3)
                pool.wait_ge(slots_added, k + 2)
                pool.tensor_tensor(slot_d[0:EP, :], slot_d[0:EP, :], slots_in[s][0:EP, :], ALU.add).then_inc(slots_added, 1)

            with pool.Fori(0, NT // 2) as i:
                for s in range(2):
                    collect(i * 2 + s, s)
            collect(NT - 1, 0)
            stage(pool, 1)
            with pool.Fori(0, CHUNKS // 2) as i:
                for s in range(2):
                    pool.wait_ge(payload_ready, i * 2 + (s + 3))
                    pool.sem_inc(pool_steps, 1)
                    for j in range(CC):
                        pool.indirect_dma_start(
                            out=rows_d, out_offset=bass.IndirectOffsetOnAxis(ap=adr[s][0:EP, j:j + 1], axis=0),
                            in_=pay_d[s][0:EP, j, :], in_offset=None).then_inc(scattered[s], 16)
            for s in range(2):
                pool.wait_ge(scattered[s], 16 * CC * (CHUNKS // 2))
            stage(pool, 2)
            for L, c in enumerate(LAYERS):
                b = B[L]
                first = [b["w1"], b["w2"]] + ([b["wmid"]] if L == 3 else []) + [b["ws"], b["pv"], b["oa"], b["om"]] + ([b["oc"]] if L == 2 else [])
                for k, v in enumerate(first):
                    ins = pool.memset(v, 0.0)
                    if k == len(first) - 1:
                        ins.then_inc(agg_zero, 1)
                stage(pool, stage_of(L, 1))
                pool.memset(b["agg"], 0.0).then_inc(agg_zero, 1)
                stage(pool, stage_of(L, 2))

                def gather(rs, q, s, k_rows, k_free):
                    pool.wait_ge(rows_in[q], k_rows)
                    pool.sem_inc(pool_steps, 1)
                    pool.wait_ge(prod_free, k_free)
                    pool.sem_inc(pool_steps, 1)
                    for g in range(2):
                        u = 2 * (rs % 2) + g
                        col = c["rows"]["idx"]
                        pool.indirect_dma_start(
                            out=b["gath"][s][:, g, :], out_offset=None, in_=table,
                            in_offset=bass.IndirectOffsetOnAxis(ap=b["rows"][q].bitcast(I32)[:, u, col:col + 1], axis=0),
                        ).then_inc(gath_in[s], 16)

                def send(h, j, i):
                    if j == 0:
                        pool.wait_ge(attr64_in[h], i * 16 + 16 * (MOVING * L + 1))
                        pool.sem_inc(pool_steps, 1)
                        pool.wait_ge(tail_ready[h], i + ((MOVING + 1 - h) * L + 1))
                        pool.sem_inc(pool_steps, 1)
                    w = ROW_S["w"]
                    pool.indirect_dma_start(
                        out=rows_s, out_offset=bass.IndirectOffsetOnAxis(ap=pay_s[h].bitcast(I32)[0:EP, j, w:w + 1], axis=0),
                        in_=pay_s[h][0:EP, j, 0:w], in_offset=None).then_inc(sent[h], 16)

                def gather_iteration(i, moving):
                    for r in range(8):
                        gather(r, r // 2, r % 4, i * 16 + 16 * (rows_base(L, r // 2) + 1), i * 8 + ((PAIRS + 1) * L + r + 1))
                        if moving:
                            send(r // HC, r % HC, i)

                moving = MOVING if L < 2 else 0
                if moving:
                    with pool.Fori(0, moving) as i:
                        gather_iteration(i, True)
                with pool.Fori(moving, ITERS) as i:
                    gather_iteration(i, False)
                if moving:
                    for h in range(2):
                        pool.wait_ge(sent[h], 16 * HC * MOVING * (L + 1))
                gather(0, 0, 0, 16 * (rows_base(L, 0) + ITERS + 1), (PAIRS + 1) * L + PAIRS + 1)
                stage(pool, stage_of(L, 3))
                if L == 2:
                    def take(t, s, k):
                        pool.wait_ge(agg_T, k)
                        pool.tensor_copy(b["aggS"][s], agg_tile(L, t)).then_inc(agg_st, 1)

                    with pool.Fori(0, NT // 2) as i:
                        for s in range(2):
                            take(i * 2 + s, s, i * 2 + (NT * L + s + 1))
                    take(NT - 1, 0, NT * L + NT)
                stage(pool, stage_of(L, 4))

        @block.scalar
        def _(act):
            act.wait_ge(const_in, 16)
            act.wait_ge(vec_in, 16)
            act.activation(vec_sq[0:EP, :, :], vec[0:EP, :, :], ACT.Square).then_inc(vec_squared, 1)
            act.wait_ge(vec_summed, 2)
            act.activation(vec_norm[0:EP, 1, :], vec_norm[0:EP, 0, :], ACT.Sqrt).then_inc(vec_root, 1)

            def find(k, s):
                act.activation(distance[s][0:EP, :], bucket[0:EP, :], ACT.Abs, bias=const[0:EP, bass.ds(NC_BUCKET + k, 1)], scale=-1.0).then_inc(bucket_distance, 1)
                act.wait_ge(bucket_distance, k + 1)
                act.wait_ge(slots_masked, k + 1)
                act.activation(of_bucket[s][0:EP, :], distance[s][0:EP, :], ACT.Relu, bias=ones[0:EP, 0:1], scale=-1.0).then_inc(bucket_onehot, 1)

            act.wait_ge(totals_done, 1)
            with act.Fori(0, NT // 2) as i:
                for s in range(2):
                    find(i * 2 + s, s)
            find(NT - 1, 0)
            stage(act, 1)

            def fill(i, s):
                k = i * 2 + s
                cols = slice(k * CC, k * CC + CC) if isinstance(k, int) else bass.ds(k * CC, CC)
                act.wait_ge(stage_in[s], i * 64 + 64)
                if not isinstance(i, int):
                    act.wait_ge(scattered[s], i * (16 * CC))
                pay_ = pay_d[s][0:EP, :, :]
                r = ROW_D
                act.activation(adr[s][0:EP, :], addr_d[0:EP, cols], ACT.Copy)
                act.activation(pay_[:, :, r["idx"]:r["idx"] + 1].bitcast(I32), idx_s[0:EP, cols].rearrange("p (c o) -> p c o", o=1), ACT.Copy)
                act.activation(pay_[:, :, r["dl"]:r["dl"] + 1], low_d[0:EP, cols].rearrange("p (c o) -> p c o", o=1), ACT.Copy)
                act.activation(pay_[:, :, r["a16"]:r["a16"] + 16], st16[s][0:EP, :, :], ACT.Copy)
                act.activation(pay_[:, :, r["a10"]:r["a10"] + 10], st10[s][0:EP, :, :], ACT.Copy)
                act.activation(pay_[:, :, r["a8"]:r["a8"] + 8], st8[s][0:EP, :, :], ACT.Copy)
                act.activation(pay_[:, :, r["sh"]:r["sh"] + 4], st4[s][0:EP, :, :], ACT.Copy).then_inc(payload_ready, 1)

            for s in range(2):
                fill(0, s)
            with act.Fori(1, CHUNKS // 2) as i:
                for s in range(2):
                    fill(i, s)
            stage(act, 2)
            for L, c in enumerate(LAYERS):
                b = B[L]
                sq = arena[:, b["agg_off"]:b["agg_off"] + NT * D]
                if L:
                    act.wait_ge(ln_a, 2 * L - 1)
                    act.activation(sq, sq, ACT.Square).then_inc(ln_b, 1)
                    act.wait_ge(ln_a, 2 * L)
                act.activation(ln_rstd, ln_sq, ACT.Sqrt, bias=eps, scale=1.0 / D).then_inc(ln_b, 1)
                stage(act, stage_of(L, 1))

                def normed(t, s, k):
                    act.wait_ge(hT_ready, k)
                    act.activation(b["h"][s], x_tile(t), ACT.Relu, bias=arena_col(ln_bias_off, t),
                                   scale=arena_col(ln_rstd_off, t)).then_inc(h_ready, 1)

                def second(t, s, k):
                    act.wait_ge(f_ready, k)
                    act.activation(b["utmp"][s], bank[:, 4 + 2 * s + 1, 0:320], ACT.Copy, scale=arena_col(nv_off + NT, t)).then_inc(f_tmp, 1)

                NB = NT * L
                normed(0, 0, NB + 1)
                normed(1, 1, NB + 2)
                with act.Fori(0, NT // 2 - 1) as i:
                    for s in range(2):
                        normed(i * 2 + (s + 2), s, i * 2 + (NB + s + 3))
                        if L == 1:
                            second(i * 2 + s, s, i * 2 + (NB + s + 1))
                normed(NT - 1, 0, NB + NT)
                if L == 1:
                    for t in range(NT - 3, NT):
                        second(t, t % 2, NB + t + 1)
                stage(act, stage_of(L, 2))

                def act_turn(par, kt):
                    act.wait_ge(turned, kt)
                    rowsn, cols = (ROW_S["w"], 512) if L == 2 else (PAIR_ROWS, 256)
                    act.activation(b["tT"][par][0:rowsn, :, :], bank[0:rowsn, 0, 0:cols].rearrange("p (a b) -> p a b", b=P),
                                   ACT.Copy).then_inc(turned_sb, 1)

                def act_hidden(par, kh):
                    act.wait_ge(hidden1, kh)
                    if L == 0:
                        act.activation(b["hT"][par], bank[:, 1, 0:256].rearrange("p (a b) -> p a b", b=P), ACT.Silu, scale=0.25).then_inc(hidden_sb, 1)
                    elif L == 1:
                        act.activation(b["hT"][par][0:100, :, :], bank[0:100, 1, :].rearrange("p (a b) -> p a b", b=P), ACT.Silu).then_inc(hidden_sb, 1)
                    elif L == 2:
                        act.activation(b["hT"][par], bank[:, 1, 0:256].rearrange("p (a b) -> p a b", b=P), ACT.Relu).then_inc(hidden_sb, 1)
                    else:
                        act.activation(b["h1T"][par], bank[:, 1, 0:256].rearrange("p (a b) -> p a b", b=P), ACT.Gelu_apprx_tanh,
                                       scale=8.0 ** -0.5).then_inc(hidden1_sb, 1)

                def act_hidden2(par, kh):
                    act.wait_ge(hidden2, kh)
                    act.activation(b["hT"][par], bank[:, 1, 256:512].rearrange("p (a b) -> p a b", b=P), ACT.Gelu_apprx_tanh,
                                   scale=0.125).then_inc(hidden_sb, 1)

                def act_scale(n, i):
                    gs, q = n % 4, (n // 2) % 4
                    act.wait_ge(gath_in[gs], i * 64 + 32 * (gath_base(L, gs) + 1 + n // 4))
                    sh = c["rows"]["sh"]
                    for g in range(2):
                        G = b["gath"][gs][:, g, :]
                        col = lambda m: b["rows"][q][:, 2 * (n % 2) + g, sh + m:sh + m + 1]
                        if L == 2:
                            act.activation(b["cA"][gs][:, g, 2, :], G[:, 64:96], ACT.Copy, scale=col(1))
                            ins = act.activation(b["cB"][gs][:, g, 0, :], G[:, 128:160], ACT.Copy, scale=col(1))
                        else:
                            ins = act.activation(b["E0"][gs][:, g, :], G, ACT.Copy, scale=col(0))
                    ins.then_inc(e_scaled, 1)

                by_act = c["by_act"]

                def act_last(n, kp):
                    act.wait_ge(first_products, kp)
                    s, q = n % 2, (n // 2) % 4
                    for g in range(2):
                        for m in range(3 - by_act, 3):
                            sh = c["rows"]["sh"] + m + (0 if L == 2 else 1)
                            v = VM0 + 96 * m
                            ins = act.activation(b["X"][s][:, g, v:v + 64], b["X"][s][:, g, c["xw"] - 64:c["xw"]], ACT.Copy,
                                                 scale=b["rows"][q][:, 2 * (n % 2) + g, sh:sh + 1])
                    ins.then_inc(copies_done, 1)

                QB, PB = (QUADS + 2) * L, (PAIRS + 1) * L
                act_turn(0, QB + 1)
                act_turn(1, QB + 2)
                act_hidden(0, QB + 1)
                if L == 3:
                    act_hidden2(0, 1)
                act_hidden(1, QB + 2)
                act_scale(0, 0)
                with act.Fori(0, ITERS) as i:
                    for q in range(4):
                        act_last(2 * q, i * 8 + (PB + 2 * q + 1))
                        act_scale(2 * q + 1, i)
                        act_turn(q % 2, i * 4 + (QB + q + 3))
                        if L == 3:
                            act_hidden2((q + 1) % 2, i * 4 + (q + 2))
                        act_last(2 * q + 1, i * 8 + (PB + 2 * q + 2))
                        act_scale(2 * q + 2, i)
                        act_hidden(q % 2, i * 4 + (QB + q + 3))
                act_last(0, PB + PAIRS + 1)
                stage(act, stage_of(L, 3))

                def take(t, s, k):
                    act.wait_ge(agg_T, k)
                    act.activation(b["aggS"][s], agg_tile(L, t), ACT.Copy, scale=arena_col(recip_off, t) if L == 0 else 1.0).then_inc(agg_st, 1)

                def after(t, s, k):
                    if L == 1:
                        act.wait_ge(o_ready, k)
                        act.activation(b["utmp"][s][:, 0:160], bank[:, 4 + s, 160:320], ACT.Copy, scale=arena_col(mask_off + NT, t)).then_inc(o_tmp, 1)
                    if L == 2:
                        act.wait_ge(o_y, k - 2 * NT)
                        act.activation(b["utmp"][s][:, 0:96], b["u"][s][:, 0:96], ACT.Sigmoid).then_inc(o_gate, 1)

                if L == 0:
                    act.wait_ge(counts_ready, 1)
                if L == 2:
                    with act.Fori(0, NT // 2) as i:
                        for s in range(2):
                            after(None, s, i * 2 + (NB + s + 1))
                    after(None, 0, NB + NT)
                else:
                    take(0, 0, NB + 1)
                    take(1, 1, NB + 2)
                    with act.Fori(0, NT // 2 - 1) as i:
                        for s in range(2):
                            take(i * 2 + (s + 2), s, i * 2 + (NB + s + 3))
                            after(i * 2 + s, s, i * 2 + (NB + s + 1))
                    for t in range(NT - 3, NT):
                        if t == NT - 3:
                            take(NT - 1, 0, NB + NT)
                        after(t, t % 2, NB + t + 1)
                stage(act, stage_of(L, 4))

        @block.tensor
        def _(pe):
            pe.sem_inc(hT_ready, 2)
            pe.sem_inc(agg_T, 2)
            pe.wait_ge(const_in, 16)
            for o in range(2):
                pe.wait_ge(totals_done, o + 1)
                pe.matmul(bank[0:EP, 0, 0:NT], tri[0:EP, 0:EP], totals[0:EP, :], start=True, stop=True)
                pe.matmul(bank[:, 1, 0:NT], ones[0:EP, :], totals[0:EP, :], start=True, stop=True).then_inc(offsets_done, 1)
                stage(pe, o + 1)
            for L, c in enumerate(LAYERS):
                b = B[L]
                if L == 1:
                    lo, hi = b["ws"][:, 0, :], b["ws"][:, 1, :]
                    pe.wait_ge(weights_in, loads_to[L])
                    for k in range(4):
                        ins = pe.transpose(bank[0:96, 0, 96 * k:96 * k + 96], lo[0:96, 256 + 96 * k:352 + 96 * k], ident[0:96, 0:96])
                    ins.then_inc(offsets_done, 1)
                    pe.wait_ge(totals_done, 3)
                    for k, (cols, wid) in enumerate(((384, 64), (384, 64), (448, 32), (448, 32))):
                        ins = pe.matmul(bank[0:96, 1, 64 * k:64 * k + wid], lo[0:96, 256 + 96 * k:352 + 96 * k], hi[0:96, cols:cols + wid], start=True, stop=True)
                    ins.then_inc(offsets_done, 1)
                stage(pe, stage_of(L, 1))

                def turn_h(s, k):
                    pe.wait_ge(h_ready, k)
                    pe.transpose(bank[0:96, s, P:2 * P], b["h"][s][:, 64:160], ident)
                    pe.transpose(bank[0:64, s, 0:P], b["h"][s][:, 0:64], ident).then_inc(hT_ready, 1)

                def mix(s, k, kfree):
                    pe.wait_ge(hT_sb, k)
                    pe.wait_ge(u_ready, kfree)
                    f0, f1 = 4 + 2 * s, 5 + 2 * s
                    hs, hv = b["hTs"][s][0:64, :], b["hTv"][s][0:96, :]
                    both = lambda bk, half, o, n: bank[:, bk, 0:2 * half].rearrange("p (z w) -> p z w", z=2)[:, :, o:o + n]
                    if L == 2:
                        parts = [(both(f0, 192, 64, 96), hv, b["pv"][0:96, 0:192]),
                                 (bank[:, f0, 0:64], hs, b["ps"][0:64, 0:64]), (bank[:, f0, 160:256], hs, b["ps"][0:64, 64:160])]
                    else:
                        parts = []
                        for a in range(2 if L == 1 else 1):
                            parts.append((both((f0, f1)[a], 160, 64, 96), hv, b["pv"][0:96, 192 * a:192 * a + 192]))
                            parts.append((both((f0, f1)[a], 160, 0, 64), hs, b["ps"][0:64, 128 * a:128 * a + 128]))
                    for o, l, r in parts:
                        ins = pe.matmul(o, l, r, start=True, stop=True)
                    ins.then_inc(f_ready, 1)

                NB = NT * L
                turn_h(0, NB + 1)
                with pe.Fori(0, NT // 2) as i:
                    for s in range(2):
                        turn_h(1 - s, i * 2 + (NB + s + 2))
                        mix(s, i * 2 + (NB + s + 1), i * 2 + (NB + s + 1))
                mix(0, NB + NT, NB + NT)
                stage(pe, stage_of(L, 2))

                wn = c["wn"]
                QB, PB = (QUADS + 2) * L, (PAIRS + 1) * L

                def turn(q, par, k_rows, k_bank):
                    pe.wait_ge(rows_in[q], k_rows)
                    if k_bank is not None:
                        pe.wait_ge(turned_sb, k_bank)
                    rows = b["rows"][q]
                    if L == 2:
                        for u in range(4):
                            ins = pe.transpose(bank[0:ROW_S["w"], 0, P * u:P * u + P], rows[:, u, :], ident)
                    else:
                        flat = rows.rearrange("p a b -> p (a b)")
                        for v in range(2):
                            ins = pe.transpose(bank[0:PAIR_ROWS, 0, P * v:P * v + P],
                                               flat[:, 2 * PAIR_STEP * v:2 * PAIR_STEP * v + PAIR_ROWS], ident)
                    ins.then_inc(turned, 1)

                def first_layer(par, k_turned, k_bank):
                    pe.wait_ge(turned_sb, k_turned)
                    if k_bank is not None:
                        pe.wait_ge(hidden_sb, k_bank)
                    tT = b["tT"][par]
                    if L == 2:
                        for g in range(2):
                            ins = pe.matmul(bank[64 * g:64 * g + 64, 1, 0:256], b["w1"][0:ROW_S["w"], :],
                                            tT[0:ROW_S["w"], g:4:2, :], start=True, stop=True, tile_position=(0, 64 * g))
                    elif L == 1:
                        for u in range(4):
                            ins = pe.matmul(bank[0:100, 1, P * u:P * u + P], b["w1"][0:PAIR_ROWS, u % 2, :],
                                            tT[0:PAIR_ROWS, u // 2, :], start=True, stop=True)
                    else:
                        ins = pe.matmul(bank[:, 1, 0:256], b["w1"][0:PAIR_ROWS, :], tT[0:PAIR_ROWS, :, :], start=True, stop=True)
                    ins.then_inc(hidden1, 1)

                def second_layer(par, k):
                    pe.wait_ge(hidden1_sb, k)
                    for v in range(2):
                        ins = pe.matmul(bank[:, 1, 256 + P * v:256 + P * v + P], b["wmid"], b["h1T"][par][:, v, :], start=True, stop=True)
                    ins.then_inc(hidden2, 1)

                def edge_weights(rp, par, s, k_hidden, k_free):
                    pe.wait_ge(hidden_sb, k_hidden)
                    pe.wait_ge(prod_free, k_free)
                    if L == 1:
                        for g in range(2):
                            ins = pe.matmul(bank[:, 2 + s, wn * g:wn * g + wn], b["hT"][par][0:100, 2 * rp + g, :], b["w2"][0:100, :],
                                            start=True, stop=True)
                    else:
                        ins = pe.matmul(bank[:, 2 + s, 0:2 * wn], b["hT"][par][:, rp, :], b["w2"], start=True, stop=True)
                    ins.then_inc(w_ready, 1)

                def sums(s, k_x, k_free):
                    pe.wait_ge(x_ready, k_x + 8)
                    pe.wait_ge(copies_done, k_x + 8)
                    pe.wait_ge(summed, k_free)
                    X, Sx = b["X"][s], b["S"][s]
                    for g in range(2):
                        ins = pe.matmul(bank[:, 4 + 2 * s, 0:c["aw"]], Sx[:, g, :], X[:, g, 0:c["aw"]], start=g == 0, stop=g == 1)
                    ins.then_inc(sums_ready, 1)

                turn(0, 0, 16 * (rows_base(L, 0) + 1), QB if L else None)
                turn(1, 1, 16 * (rows_base(L, 1) + 1), QB + 1)
                first_layer(0, QB + 1, QB if L else None)
                if L == 3:
                    second_layer(0, 1)
                first_layer(1, QB + 2, QB + 1)
                edge_weights(0, 0, 0, QB + 1, PB + 3)
                with pe.Fori(0, ITERS) as i:
                    for q in range(4):
                        nq = (q + 2) % 4
                        turn(nq, q % 2, i * 16 + 16 * (rows_base(L, nq) + (1 if q < 2 else 2)), i * 4 + (QB + q + 2))
                        if L == 3:
                            second_layer((q + 1) % 2, i * 4 + (q + 2))
                        edge_weights(1, q % 2, 1, i * 4 + (QB + q + 1), i * 8 + (PB + 2 * q + 4))
                        sums(0, i * 8 + (PB + 2 * q + 1), i * 8 + (PAIRS * L + 2 * q + 1))
                        first_layer(q % 2, i * 4 + (QB + q + 3), i * 4 + (QB + q + 2))
                        edge_weights(0, (q + 1) % 2, 0, i * 4 + (QB + q + 2), i * 8 + (PB + 2 * q + 5))
                        sums(1, i * 8 + (PB + 2 * q + 2), i * 8 + (PAIRS * L + 2 * q + 2))
                stage(pe, stage_of(L, 3))

                def turn_sums(s, k):
                    pe.wait_ge(agg_st, k)
                    a = b["aggS"][s]
                    if L == 2:
                        pe.transpose(bank[0:96, 2 * s, 0:P], a[:, CROSS:CROSS + 96], ident)
                    for v in range(4):
                        ins = pe.transpose(bank[0:96, 2 * s + 1, P * v:P * (v + 1)], a[:, 96 * v:96 * v + 96], ident)
                    ins.then_inc(agg_T, 1)

                def outputs(s, k, kfree):
                    if L == 2:
                        pe.wait_ge(aggA_sb, k - NT * 2)
                    pe.wait_ge(aggB_sb, k)
                    pe.wait_ge(node_x, kfree)
                    o, Bt = bank[:, 4 + s, :], b["aTB"][s]
                    if L == 1:
                        scal = lambda a: a[:, 0:320].rearrange("p (z w) -> p z w", z=2)[:, :, 0:64]
                        vect = lambda a: a[:, 0:320].rearrange("p (z w) -> p z w", z=2)[:, :, 64:160]
                    elif L == 2:
                        scal, vect = (lambda a: a[:, 0:96]), (lambda a: a[:, 96:192])
                    else:
                        scal, vect = (lambda a: a[:, 0:65]), (lambda a: a[:, 65:161])
                    pe.matmul(scal(o), Bt[0:96, 0, :], scal(b["oa"][0:96, :]), start=True, stop=True, skip_group_check=True)
                    if L == 2:
                        pe.matmul(vect(o), b["aTA"][s][0:96, :], vect(b["oc"][0:96, :]), start=False, stop=False, skip_group_check=True)
                    for m in range(3):
                        ins = pe.matmul(vect(o), Bt[0:96, 1 + m, :], vect(b["om"][0:96, m, :]), start=False, stop=m == 2, skip_group_check=True)
                    ins.then_inc(o_ready, 1)

                turn_sums(0, NB + 1)
                with pe.Fori(0, NT // 2) as i:
                    for s in range(2):
                        turn_sums(1 - s, i * 2 + (NB + s + 2))
                        outputs(s, i * 2 + (NB + s + 1), i * 2 + (NB + s + 1))
                outputs(0, NB + NT, NB + NT)
                stage(pe, stage_of(L, 4))

        @block.vector
        def _(dve):
            step = Count(dve_step)

            def then(ins):
                step.up(ins)
                dve.wait_ge(dve_step, step.n)

            dve.sem_inc(x_ready, 8)
            dve.sem_inc(copies_done, 8)
            dve.sem_inc(prod_free, 4)
            dve.sem_inc(summed, 2)
            dve.sem_inc(u_ready, 2)
            dve.sem_inc(node_x, 2)
            dve.sem_inc(payload_ready, 2)
            dve.sem_inc(slots_masked, 2)
            dve.sem_inc(slots_added, 2)
            dve.memset(eps, 1e-5)
            dve.memset(ones_e[0:EP, :], 1.0)
            dve.memset(slot_d[0:EP, :], 0.0)
            then(dve.memset(slot_s[0:EP, :], 0.0))
            dve.wait_ge(const_in, 16)
            dve.wait_ge(idx_in, 32)
            bval = lambda k: const[0:EP, bass.ds(NC_BUCKET + k, 1)]
            for o, (idx, slot, addr, low) in enumerate(((idx_d, slot_d, addr_d, low_d), (idx_s, slot_s, addr_s, low_s))):
                dve.tensor_scalar(itmp[0][0:EP, :], idx[0:EP, :], 7, None, ALU.arith_shift_right)
                then(dve.tensor_scalar(itmp[1][0:EP, :], idx[0:EP, :], 127, None, ALU.bitwise_and))
                dve.tensor_copy(bucket[0:EP, :], itmp[0][0:EP, :])
                then(dve.tensor_scalar(low[0:EP, :], itmp[1][0:EP, :], 1.0, None, ALU.add))
                n0 = step.n
                def count(k, buf):
                    dve.tensor_scalar(buf[0:EP, :], bucket[0:EP, :], bval(k), 0.0, ALU.is_equal, ALU.add,
                                      accum_out=totals[0:EP, bass.ds(k, 1)]).then_inc(dve_step, 1)

                count(0, onehot_b)
                with dve.Fori(0, NT // 2) as i:
                    for s, buf in enumerate((scan_b, onehot_b)):
                        dve.wait_ge(dve_step, i * 2 + (n0 + s))
                        count(i * 2 + (s + 1), buf)
                step.n += NT
                dve.wait_ge(dve_step, step.n)
                dve.drain().then_inc(totals_done, 1)
                dve.wait_ge(offsets_done, o + 1)
                then(dve.tensor_scalar(cnt_i, bank[:, 1, 0:NT], 255.0, None, ALU.add))
                then(dve.tensor_scalar(cnt_i, cnt_i, 8, None, ALU.arith_shift_right))
                then(dve.tensor_copy(cnt_f, cnt_i))
                then(dve.tensor_tensor_scan(tend, ones[:, 0:NT], cnt_f, 0.0, ALU.mult, ALU.add))
                then(dve.tensor_tensor(basef, tend, cnt_f, ALU.subtract))
                then(dve.tensor_scalar(basef, basef, 256.0, -1.0, ALU.mult, ALU.add))
                then(dve.tensor_tensor(offs[0:EP, :], bank[0:EP, 0, 0:NT], basef[0:EP, :], ALU.add))
                for j in range(STEPC):
                    then(dve.tensor_scalar(step_cmp, tend, const[:, NC_STEP + j:NC_STEP + j + 1], 0.0, ALU.is_le, ALU.add,
                                           accum_out=step_f[:, j:j + 1]))
                if o == 1:
                    dve.wait_ge(step_out, 16)
                then(dve.tensor_scalar(step_i, step_f, float(NT - 1), None, ALU.min))
                dve.drain().then_inc(table_done, 1)
                if o == 0:
                    def number(k, s):
                        dve.wait_ge(bucket_onehot, k + 1)
                        dve.wait_ge(slots_added, k + 1)
                        dve.tensor_tensor_scan(slots_in[s][0:EP, :], ones_e[0:EP, :], of_bucket[s][0:EP, :], offs[0:EP, bass.ds(k, 1)],
                                               ALU.mult, ALU.add).then_inc(dve_step, 1)
                        dve.wait_ge(dve_step, k + (n0 + 1))
                        dve.tensor_tensor(slots_in[s][0:EP, :], slots_in[s][0:EP, :], of_bucket[s][0:EP, :], ALU.mult).then_inc(slots_masked, 1)

                    n0 = step.n
                    with dve.Fori(0, NT // 2) as i:
                        for s in range(2):
                            number(i * 2 + s, s)
                    number(NT - 1, 0)
                    step.n += NT
                    dve.wait_ge(slots_added, NT + 2)
                else:
                    n0 = step.n
                    with dve.Fori(0, NT) as k:
                        dve.wait_ge(dve_step, k * 4 + n0)
                        dve.tensor_scalar(onehot_b[0:EP, :], bucket[0:EP, :], bval(k), None, ALU.is_equal).then_inc(dve_step, 1)
                        dve.wait_ge(dve_step, k * 4 + (n0 + 1))
                        dve.tensor_tensor_scan(scan_b[0:EP, :], ones_e[0:EP, :], onehot_b[0:EP, :], offs[0:EP, bass.ds(k, 1)],
                                               ALU.mult, ALU.add).then_inc(dve_step, 1)
                        dve.wait_ge(dve_step, k * 4 + (n0 + 2))
                        dve.tensor_tensor(scan_b[0:EP, :], scan_b[0:EP, :], onehot_b[0:EP, :], ALU.mult).then_inc(dve_step, 1)
                        dve.wait_ge(dve_step, k * 4 + (n0 + 3))
                        dve.tensor_tensor(slot[0:EP, :], slot[0:EP, :], scan_b[0:EP, :], ALU.add).then_inc(dve_step, 1)
                    step.n += 4 * NT
                    dve.wait_ge(dve_step, step.n)
                s_i, hi_i, mid_i = (t[0:EP, :] for t in itmp)
                then(dve.tensor_copy(s_i, slot[0:EP, :]))
                dve.tensor_scalar(hi_i, s_i, -512, None, ALU.bitwise_and)
                dve.tensor_scalar(mid_i, s_i, 127, 2, ALU.bitwise_and, ALU.logical_shift_left)
                then(dve.tensor_scalar(addr[0:EP, :], s_i, 7, 3, ALU.arith_shift_right, ALU.bitwise_and))
                then(dve.tensor_tensor(hi_i, hi_i, mid_i, ALU.add))
                then(dve.tensor_tensor(addr[0:EP, :], addr[0:EP, :], hi_i, ALU.add))
                if o == 0:
                    stage(dve, 1)
            dve.memset(tail_f[0:EP, EC:EC + HC, :], 0.0)
            dve.memset(tail_i[0:EP, EC:EC + HC, :], 0)
            dve.tensor_copy(tail_f[0:EP, 0:EC, 5:6], low_s[0:EP, :].rearrange("p (c o) -> p c o", o=1))
            dve.tensor_copy(tail_i[0:EP, 0:EC, 0:1], idx_d[0:EP, :].rearrange("p (c o) -> p c o", o=1))
            dve.tensor_copy(tail_i[0:EP, 0:EC, 1:2], addr_s[0:EP, :].rearrange("p (c o) -> p c o", o=1))
            dve.wait_ge(vec_root, 1)
            then(dve.reciprocal(vec_norm[0:EP, 2, :], vec_norm[0:EP, 1, :]))
            for at, n in ((0, 3), (3, 2)):
                dve.tensor_tensor(tail_f[0:EP, 0:EC, at:at + n], vec[0:EP, :, 0:n],
                                  vec_norm[0:EP, 2, :].rearrange("p (c o) -> p c o", o=1).to_broadcast([EP, EC, n]), ALU.mult)

            def means():
                then(dve.tensor_reduce(ln_sum, x, AX_X, ALU.add))
                then(dve.tensor_scalar(ln_mean, ln_sum, -1.0 / D, None, ALU.mult))

            def mean_of(t0, t1):
                return ln_mean[:, t0:t1].rearrange("p (t o) -> p t o", o=1).to_broadcast([P, t1 - t0, D])

            means()
            half = (NT + 1) // 2
            for t0, t1 in ((0, half), (half, NT)):
                part = arena[:, sort_top:sort_top + (t1 - t0) * D].rearrange("p (t d) -> p t d", d=D)
                then(dve.tensor_tensor(part, x[:, t0:t1, :], mean_of(t0, t1), ALU.add))
                then(dve.tensor_tensor(part, part, part, ALU.mult))
                then(dve.tensor_reduce(ln_sq[:, t0:t1], part, AX_X, ALU.add))
            stage(dve, 2)

            for L, c in enumerate(LAYERS):
                b = B[L]
                xw, wn = c["xw"], c["wn"]
                if L == 0:
                    dve.tensor_tensor(attr_sq, nv[:, 0, :], nv[:, 0, :], ALU.mult)
                    dve.tensor_tensor(attr_mask[:, 0, :], nv[:, 0, :], nv[:, 2, :], ALU.mult)
                    dve.tensor_tensor(attr_mask[:, 1, :], nv[:, 1, :], nv[:, 2, :], ALU.mult)
                if L:
                    sq3d = arena[:, b["agg_off"]:b["agg_off"] + NT * D].rearrange("p (t d) -> p t d", d=D)
                    means()
                    dve.tensor_tensor(sq3d, x, mean_of(0, NT), ALU.add).then_inc(ln_a, 1)
                dve.wait_ge(weights_in, loads_to[L])
                lo, hi = b["ws"][:, 0, :], b["ws"][:, 1, :]

                def scaled(dst, src, f):
                    dve.tensor_scalar(dst, src, float(f), None, ALU.mult)

                def comps(dst, src, f, m=None):
                    d = dst.rearrange("p (v m) -> p m v", m=3)
                    if m is None:
                        dve.tensor_scalar(d, src.rearrange("p (m v) -> p m v", m=3), float(f), None, ALU.mult)
                    else:
                        dve.tensor_scalar(d[:, m, :], src, float(f), None, ALU.mult)

                r3 = 3.0 ** -0.5
                if L in (0, 3):
                    i0, i1, i9 = 64.0 ** -0.5, 32.0 ** -0.5, 96.0 ** -0.5
                    g9 = i9 * (1.0 if L == 0 else 32.0 ** -0.5)
                    scaled(b["ps"][0:64, 0:128], lo[0:64, 0:128], i0)
                    scaled(b["pv"][0:96, 0:96], hi[0:96, 0:96], i1)
                    comps(b["pv"][0:96, 96:192], hi[0:96, 96:192], i1)
                    for g in range(2):
                        scaled(b["w2"][64 * g:64 * g + 64, 192 * g:192 * g + 192], hi[64 * g:64 * g + 64, 192:384], 0.125)
                    scaled(b["oa"][0:64, 1:65], lo[0:64, 128:192], g9)
                    scaled(b["oa"][0:64, 0:1], lo[0:64, 192:193], g9)
                    scaled(b["oa"][64:96, 1:65], lo[64:96, 128:192], g9 * r3)
                    scaled(b["oa"][64:96, 0:1], lo[64:96, 192:193], g9 * r3)
                    for m in range(3):
                        comps(b["om"][0:96, m, 65:161], lo[0:96, 193:225], g9, m)
                if L == 1:
                    import math
                    cs, cx = math.sin(math.pi / 8), math.cos(math.pi / 8)
                    for a in range(2):
                        scaled(b["ps"][0:64, 128 * a:128 * a + 64], lo[0:64, 128 * a:128 * a + 64], 1.0)
                        scaled(b["ps"][0:64, 128 * a + 64:128 * a + 128], lo[0:64, 128 * a + 64:128 * a + 128], cs)
                        scaled(b["pv"][0:96, 192 * a:192 * a + 96], hi[0:96, 192 * a:192 * a + 96], 1.0)
                        comps(b["pv"][0:96, 192 * a + 96:192 * a + 192], hi[0:96, 192 * a + 96:192 * a + 192], cs)
                    dve.wait_ge(offsets_done, 3)
                    dve.tensor_copy(lo[0:96, 256:640], bank[0:96, 0, 0:384]).then_inc(totals_done, 1)
                    dve.wait_ge(offsets_done, 4)
                    g = cx / 4.0
                    for a in range(2):
                        o0 = 160 * a
                        scaled(b["oa"][0:64, o0:o0 + 64], bank[0:64, 1, 64 * a:64 * a + 64], g)
                        scaled(b["oa"][64:96, o0:o0 + 64], bank[64:96, 1, 64 * a:64 * a + 64], g * r3)
                        for m in range(3):
                            comps(b["om"][0:96, m, o0 + 64:o0 + 160], bank[0:96, 1, 128 + 64 * a:160 + 64 * a], g, m)
                if L == 2:
                    g, s3 = 1.0 / 32.0, 3.0 ** 0.5
                    scaled(b["ps"][0:64, 0:160], lo[0:64, 0:160], 1.0)
                    scaled(b["pv"][0:96, 0:96], hi[0:96, 0:96], 1.0)
                    comps(b["pv"][0:96, 96:192], hi[0:96, 96:192], 1.0)
                    scaled(b["oa"][0:96, 0:96], lo[0:96, 160:256], g)
                    for m in range(3):
                        comps(b["om"][0:64, m, 96:192], lo[0:64, 256:288], g * s3, m)
                        comps(b["om"][64:96, m, 96:192], lo[64:96, 256:288], g, m)
                        comps(b["oc"][32 * m:32 * m + 32, 96:192], lo[32 * m:32 * m + 32, 320:352], g * s3 * 2.0 ** -0.5, m)

                if L:
                    dve.wait_ge(ln_b, 2 * L)
                    dve.tensor_reduce(ln_sq, sq3d, AX_X, ALU.add).then_inc(ln_a, 1)
                dve.wait_ge(ln_b, 2 * L + 1)
                then(dve.reciprocal(ln_rstd, ln_rstd))
                dve.tensor_tensor(ln_bias, ln_mean, ln_rstd, ALU.mult)
                stage(dve, stage_of(L, 1))

                NB = NT * L

                def evacuate(s, k):
                    dve.wait_ge(hT_ready, k + 2)
                    dve.tensor_copy(b["hTs"][s][0:64, :], bank[0:64, s, 0:P])
                    dve.tensor_copy(b["hTv"][s][0:96, :], bank[0:96, s, P:2 * P]).then_inc(hT_sb, 1)

                def finish(t, s, k, kout, ks):
                    dve.wait_ge(f_ready, k)
                    if kout is not None:
                        dve.wait_ge(table_out[s], kout)
                    u, f = b["u"][s], bank[:, 4 + 2 * s, :]
                    if L == 1:
                        dve.wait_ge(f_tmp, ks)
                        dve.scalar_tensor_tensor(out=u[:, 0:320], in0=f[:, 0:320], scalar=arena_col(nv_off, t), in1=b["utmp"][s],
                                                 op0=ALU.mult, op1=ALU.add).then_inc(u_ready, 1)
                    elif L == 2:
                        dve.tensor_copy(u[:, 0:352], f[:, 0:352]).then_inc(u_ready, 1)
                    else:
                        dve.tensor_scalar(u[:, 0:320], f[:, 0:320], arena_col(nv_off, t), None, ALU.mult).then_inc(u_ready, 1)
                    if L != 2:
                        dve.wait_ge(u_ready, k + 2)
                        dve.tensor_tensor(x_tile(t), x_tile(t), u[:, 160:320], ALU.add)

                per = 32 if L == 2 else 16
                evacuate(0, NB + 1)
                for t in range(2):
                    evacuate(1 - t % 2, NB + t + 2)
                    finish(t, t % 2, NB + t + 1, out_count(L, t % 2) if L else None, t + 1)
                with dve.Fori(0, NT // 2 - 1) as i:
                    for s in range(2):
                        evacuate(1 - s, i * 2 + (NB + s + 4))
                        finish(i * 2 + (s + 2), s, i * 2 + (NB + s + 3), i * per + (out_count(L, s) + per), i * 2 + (s + 3))
                finish(NT - 1, 0, NB + NT, out_count(L, 0) + per * (NT // 2), NT)
                stage(dve, stage_of(L, 2))

                QB, PB = (QUADS + 2) * L, (PAIRS + 1) * L
                rw = c["rows"]

                def products(rp, q, gs, s, k_gath, k):
                    dve.wait_ge(gath_in[gs], k_gath)
                    X, G, esh, dot = b["X"][s], b["gath"][gs], b["esh"][s], b["dot"][s]
                    E0 = G if L == 2 else b["E0"][gs]
                    W = bank[:, 2 + s, 0:2 * wn].rearrange("p (g w) -> p g w", w=wn)
                    rows, onehot = b["rows"][q][:, 2 * rp:2 * rp + 2, :], b["S"][s]
                    sh1 = rw["sh"] + (0 if L == 2 else 1)
                    sh = lambda m, n, w: rows[:, :, sh1 + m:sh1 + m + n].unsqueeze(3).to_broadcast([P, 2, n, w])
                    by_m = lambda a: a.rearrange("p g (m v) -> p g m v", m=3)
                    w_m = lambda o: W[:, :, o:o + V].unsqueeze(2).to_broadcast([P, 2, 3, V])
                    e1 = by_m(G[:, :, 64:160])
                    ins = dve.tensor_tensor(esh, e1, sh(0, 3, V), ALU.mult)
                    if L == 2:
                        cA, cB = b["cA"][gs], b["cB"][gs]
                        dve.tensor_tensor(cA[:, :, 0:2, :], e1[:, :, 1:3, :], sh(2, 2, V), ALU.mult)
                        ins = dve.tensor_tensor(cB[:, :, 1:3, :], e1[:, :, 0:2, :], sh(2, 2, V), ALU.mult)
                    ins.then_inc(dot_step, 1)
                    dve.wait_ge(w_ready, k)
                    w1e0 = X[:, :, xw - 64:xw]
                    dve.tensor_tensor(w1e0, W[:, :, 64:128], G[:, :, 0:64], ALU.mult).then_inc(first_products, 1)
                    dve.wait_ge(dot_step, k * 2 - 1)
                    ins = dve.tensor_reduce(dot, esh.rearrange("p g m v -> p g v m"), AX_X, ALU.add)
                    dve.wait_ge(e_scaled, k)
                    if L == 2:
                        ins = dve.tensor_tensor(b["cC"][s], cA, cB, ALU.subtract)
                    ins.then_inc(dot_step, 1)
                    Xv = by_m(X[:, :, VM0:VM0 + 288])
                    dve.tensor_tensor(X[:, :, 0:64], W[:, :, 0:64], E0[:, :, 0:64], ALU.mult)
                    dve.tensor_tensor(Xv[:, :, :, 64:96], w_m(128), by_m(E0[:, :, 64:160]), ALU.mult)
                    dve.wait_ge(dot_step, k * 2)
                    ins = dve.tensor_tensor(X[:, :, 64:96], W[:, :, 160:192], dot, ALU.mult)
                    if L == 2:
                        ins = dve.tensor_tensor(by_m(X[:, :, CROSS:CROSS + 96]), w_m(192), b["cC"][s], ALU.mult)
                    ins.then_inc(prod_free, 1)
                    ins = dve.tensor_tensor(onehot, iota.unsqueeze(1).to_broadcast([P, 2, P]),
                                            rows[:, :, rw["dl"]:rw["dl"] + 1].to_broadcast([P, 2, P]), ALU.is_equal)
                    if c["by_act"] < 3:
                        n = 3 - c["by_act"]
                        dve.wait_ge(first_products, k)
                        ins = dve.tensor_tensor(Xv[:, :, 0:n, 0:64], w1e0.unsqueeze(2).to_broadcast([P, 2, n, 64]), sh(0, n, 64), ALU.mult)
                    ins.then_inc(x_ready, 1)

                def add(s, tile, k_sums, k_prev):
                    dve.wait_ge(sums_ready, k_sums)
                    dve.wait_ge(summed, k_prev)
                    a = agg_tile(L, tile)
                    sm = bank[:, 4 + 2 * s, 0:c["aw"]]
                    dve.tensor_tensor(a, a, sm, ALU.add).then_inc(summed, 1)

                brow = bucket_rows[1 if L == 2 else 0]
                def tail(h, i):
                    if not (isinstance(i, int) and L == 0):
                        dve.wait_ge(sent[h], i * (16 * HC) + 16 * HC * MOVING * L)
                    cols = bass.ds(i * (2 * HC) + (2 * HC * MOVING * L + HC * h), HC)
                    dve.tensor_copy(pay_s[h][0:EP, :, 64:70], tail_f[0:EP, cols, :])
                    dve.tensor_copy(pay_s[h].bitcast(I32)[0:EP, :, 70:72], tail_i[0:EP, cols, :]).then_inc(tail_ready[h], 1)

                def iteration(i, moving):
                    for r in range(8):
                        if moving and r % HC == 0:
                            tail(1 - r // HC, i + r // HC)
                        n = r + 1
                        products(n % 2, (n // 2) % 4, n % 4, n % 2,
                                 i * 64 + 32 * (gath_base(L, n % 4) + 1 + n // 4), i * 8 + (PB + n + 1))
                        tile = dve.value_load(brow[0:1, bass.ds(i * 8 + r, 1)], min_val=0, max_val=NT - 1)
                        add(r % 2, tile, i * 8 + (PAIRS * L + r + 1), i * 8 + (PAIRS * L + r + 2))

                if L == 0:
                    for s in range(2):
                        dve.memset(b["X"][s][:, :, COUNT:COUNT + 1], 1.0)
                if L < 2:
                    tail(0, 0)
                products(0, 0, 0, 0, 32 * (gath_base(L, 0) + 1), PB + 1)
                if L < 2:
                    iteration(0, True)
                    with dve.Fori(1, MOVING) as i:
                        iteration(i, True)
                    with dve.Fori(MOVING, ITERS) as i:
                        iteration(i, False)
                else:
                    with dve.Fori(0, ITERS) as i:
                        iteration(i, False)
                stage(dve, stage_of(L, 3))

                if L == 0:
                    counts = b["agg"][:, :, COUNT]
                    then(dve.tensor_scalar(recip_count, counts, 1.0, None, ALU.max))
                    dve.reciprocal(recip_count, recip_count).then_inc(counts_ready, 1)

                n0 = step.n

                def chunkB(s, k):
                    dve.wait_ge(agg_T, k + 2)
                    if L == 2:
                        dve.tensor_copy(b["aTA"][s][0:96, :], bank[0:96, 2 * s, 0:P]).then_inc(aggA_sb, 1)
                    dve.tensor_copy(b["aTB"][s][0:96, :, :], bank[0:96, 2 * s + 1, :].rearrange("p (a b) -> p a b", b=P)).then_inc(aggB_sb, 1)

                def result(t, s, k, ks, kk, k_skip):
                    dve.wait_ge(o_ready, k)
                    o, u = bank[:, 4 + s, :], b["u"][s]
                    xt = x_tile(t)
                    if L in (0, 3):
                        sc = b["scal"][s][:, 0:1]
                        dve.tensor_scalar(sc, o[:, 0:1], arena_col(sq_off, t), None, ALU.mult).then_inc(dve_step, 1)
                        dve.wait_ge(dve_step, ks)
                        dve.scalar_tensor_tensor(out=xt, in0=o[:, 1:161], scalar=sc, in1=xt, op0=ALU.mult, op1=ALU.add).then_inc(node_x, 1)
                    if L == 1:
                        dve.wait_ge(o_tmp, kk)
                        dve.scalar_tensor_tensor(out=u[:, 0:160], in0=o[:, 0:160], scalar=arena_col(mask_off, t), in1=b["utmp"][s][:, 0:160],
                                                 op0=ALU.mult, op1=ALU.add).then_inc(dve_step, 1)
                        dve.wait_ge(dve_step, ks)
                        dve.tensor_tensor(xt, xt, u[:, 0:160], ALU.add).then_inc(node_x, 1)
                    if L == 2:
                        dve.wait_ge(skip_in[s], k_skip)
                        dve.tensor_tensor(u[:, 0:192], o[:, 0:192], b["sk"][s], ALU.add).then_inc(o_y, 1)
                        dve.wait_ge(o_gate, kk)
                        gt = b["utmp"][s]
                        dve.tensor_tensor(u[:, 192:256], u[:, 0:64], gt[:, 0:64], ALU.mult)
                        dve.tensor_tensor(u[:, 256:352].rearrange("p (v m) -> p v m", m=3), u[:, 96:192].rearrange("p (v m) -> p v m", m=3),
                                          gt[:, 64:96].unsqueeze(2).to_broadcast([P, 32, 3]), ALU.mult).then_inc(dve_step, 1)
                        dve.wait_ge(dve_step, ks)
                        dve.tensor_tensor(xt, xt, u[:, 192:352], ALU.add).then_inc(node_x, 1)

                chunkB(0, NB + 1)
                with dve.Fori(0, NT // 2) as i:
                    for s in range(2):
                        chunkB(1 - s, i * 2 + (NB + s + 2))
                        result(i * 2 + s, s, i * 2 + (NB + s + 1), i * 2 + (n0 + s + 1), i * 2 + (s + 1), i * 16 + 16)
                result(NT - 1, 0, NB + NT, n0 + NT, NT, 16 * (NT // 2 + 1))
                step.n += NT
                stage(dve, stage_of(L, 4))


def kernel(**inputs):
    import numpy as _np
    import concourse.bacc as _bacc
    from concourse import mybir as _mybir
    from concourse.bass_utils import run_bass_kernel_spmd as _run

    nc = _bacc.Bacc("TRN2", target_bir_lowering=False, num_devices=1)
    arrays, aps = {}, {}
    host = dict(inputs)
    host["consts"] = shape_constants()
    for name, value in host.items():
        a = _np.ascontiguousarray(value)
        arrays[f"in_{name}_dram"] = a
        aps[name] = nc.dram_tensor(f"in_{name}_dram", a.shape, _mybir.dt.from_np(a.dtype), kind="ExternalInput").ap()
    out = nc.dram_tensor("out_0_dram", (N, D), F32, kind="ExternalOutput").ap()
    gnn_kernel(nc, aps, out)
    r = _run(nc, [arrays], core_ids=[0])
    return r.results[0]["out_0_dram"]
```
